# Optimizing a Trainium2 kernel written in Bass

```python
import numpy as np
import jax
import jax.numpy as jnp

def _softmax(x, axis=-1):
    return jax.nn.softmax(x, axis=axis)

def _gelu(x):
    return jax.nn.gelu(x, approximate=True)

def _silu(x):
    return jax.nn.silu(x)

def _sigmoid(x):
    return jax.nn.sigmoid(x)

def _layernorm(x, axis=-1, eps=1e-05):
    m = jnp.mean(x, axis=axis, keepdims=True)
    v = jnp.var(x, axis=axis, keepdims=True)
    return (x - m) / jnp.sqrt(v + eps)

def _scatter_add(tgt, idx, src, axis=0):
    return tgt.at[idx].add(src)

def _segment_sum(src, seg, n):
    return jax.ops.segment_sum(src, seg, n)
kernel_name = 'mk_hybrid_d1_jaxref_r8_0636eb'

def setup_inputs(seed: int=0):
    np.random.seed(seed)
    _w = jnp.asarray

    def _L0_attn_a_setup():
        import jax, jax.numpy as jnp
        import numpy as np
        from jax.scipy.linalg import solve_triangular
        H = 4
        CHUNK = 64
        NORM_EPS = 1e-05

        def _l2norm(x):
            return x / jnp.clip(jnp.linalg.norm(x, axis=-1, keepdims=True), 1e-12)

        def _deltanet_forward(hidden_states, conv_w, Wq, Wk, Wv, Wb, Wg, norm_w, Wo):
            B, L, D = hidden_states.shape
            Kc = conv_w.shape[1]
            dqh = Wq.shape[1] // H
            dvh = Wv.shape[1] // H
            xp = jnp.pad(hidden_states, ((0, 0), (Kc - 1, 0), (0, 0)))
            h = sum((conv_w[:, i] * xp[:, i:i + L, :] for i in range(Kc)))
            h = jax.nn.silu(h)
            q = (h @ Wq).reshape(B, L, H, dqh).transpose(0, 2, 1, 3)
            k = (h @ Wk).reshape(B, L, H, dqh).transpose(0, 2, 1, 3)
            v = (h @ Wv).reshape(B, L, H, dvh).transpose(0, 2, 1, 3)
            q = _l2norm(q)
            k = _l2norm(k)
            beta = jax.nn.sigmoid(h @ Wb).transpose(0, 2, 1)
            qm = q.reshape(B * H, L, dqh)
            km = k.reshape(B * H, L, dqh)
            vm = v.reshape(B * H, L, dvh)
            bm = beta.reshape(B * H, L)
            Nc = L // CHUNK
            eye = jnp.eye(CHUNK, dtype=q.dtype)

            def per_head(qh, kh, vh, bh):
                qs = qh.reshape(Nc, CHUNK, dqh)
                ks_ = kh.reshape(Nc, CHUNK, dqh)
                vs = vh.reshape(Nc, CHUNK, dvh)
                bs = bh.reshape(Nc, CHUNK)

                def step(S, xs):
                    qc, kc, vc, bc = xs
                    kb = kc * bc[:, None]
                    A = jnp.tril(kb @ kc.T, -1)
                    U = solve_triangular(eye + A, vc * bc[:, None] - kb @ S, lower=True)
                    o = qc @ S + jnp.tril(qc @ kc.T) @ U
                    return (S + kc.T @ U, o)
                S0 = jnp.zeros((dqh, dvh), qh.dtype)
                _, o = jax.lax.scan(step, S0, (qs, ks_, vs, bs))
                return o.reshape(L, dvh)
            o = jax.vmap(per_head)(qm, km, vm, bm)
            o = o.reshape(B, H, L, dvh).transpose(0, 2, 1, 3)
            g = (h @ Wg).reshape(B, L, H, dvh)
            rms = o * jax.lax.rsqrt(jnp.mean(o * o, axis=-1, keepdims=True) + NORM_EPS)
            out = rms * norm_w * (g * jax.nn.sigmoid(g))
            return out.reshape(B, L, H * dvh) @ Wo
        key = jax.random.key(seed)
        ks = jax.random.split(key, 9)
        B, L, D = (4, 512, 128)
        dk, dv = (64, 128)
        s = 0.02
        return {'hidden_states': jax.random.normal(ks[0], (B, L, D), jnp.float32), 'conv_w': jax.random.normal(ks[1], (D, 4), jnp.float32) * 0.2, 'Wq': jax.random.normal(ks[2], (D, dk), jnp.float32) * s, 'Wk': jax.random.normal(ks[3], (D, dk), jnp.float32) * s, 'Wv': jax.random.normal(ks[4], (D, dv), jnp.float32) * s, 'Wb': jax.random.normal(ks[5], (D, H), jnp.float32) * s, 'Wg': jax.random.normal(ks[6], (D, dv), jnp.float32) * s, 'norm_w': jnp.ones((dv // H,), jnp.float32), 'Wo': jax.random.normal(ks[7], (dv, D), jnp.float32) * s}
    _L0_attn_a_in = _L0_attn_a_setup()

    def _L0_attn_b_setup():
        import jax, jax.numpy as jnp
        import numpy as np
        B, L, H, U = (4, 512, 128, 128)
        key = jax.random.key(seed)
        k0, k1, k2, k3 = jax.random.split(key, 4)
        inputs = jax.random.normal(k0, (B, L, H), dtype=jnp.float32)
        W_rkv = jax.random.normal(k1, (H, 3 * U), dtype=jnp.float32) / np.sqrt(H)
        b_rkv = jnp.zeros((3 * U,), dtype=jnp.float32)
        W_o = jax.random.normal(k2, (U, H), dtype=jnp.float32) / np.sqrt(U)
        b_o = jnp.zeros((H,), dtype=jnp.float32)
        r_min, r_max = (0.9, 0.999)
        u = jax.random.uniform(k3, (U,), dtype=jnp.float32)
        nu_log = jnp.log(-0.5 * jnp.log(u * (r_max ** 2 - r_min ** 2) + r_min ** 2))
        gamma_log = jnp.zeros((U,), dtype=jnp.float32)
        return {'inputs': inputs, 'W_rkv': W_rkv, 'b_rkv': b_rkv, 'W_o': W_o, 'b_o': b_o, 'nu_log': nu_log, 'gamma_log': gamma_log}
    _L0_attn_b_in = _L0_attn_b_setup()

    def _L0_ffn_setup():
        import math
        import jax, jax.numpy as jnp
        import numpy as np
        TOP_K = 2
        _GELU_C = math.sqrt(2.0 / math.pi)

        def gelu_new(x):
            return 0.5 * x * (1.0 + jnp.tanh(_GELU_C * (x + 0.044715 * x * x * x)))
        key = jax.random.key(seed)
        ks = jax.random.split(key, 6)
        B, T, C, E, H = (2, 256, 128, 8, 512)
        s_in = 1.0 / math.sqrt(C)
        s_hid = 1.0 / math.sqrt(H)
        return {'x': jax.random.normal(ks[0], (B, T, C), dtype=jnp.float32), 'router_w': jax.random.normal(ks[1], (E, C), dtype=jnp.float32) * s_in, 'w_fc': jax.random.normal(ks[2], (E, C, H), dtype=jnp.float32) * s_in, 'b_fc': jax.random.normal(ks[3], (E, H), dtype=jnp.float32) * 0.02, 'w_proj': jax.random.normal(ks[4], (E, H, C), dtype=jnp.float32) * s_hid, 'b_proj': jax.random.normal(ks[5], (E, C), dtype=jnp.float32) * 0.02}
    _L0_ffn_in = _L0_ffn_setup()
    _d = {'L0_attn_a_hidden_states': _L0_attn_a_in['hidden_states'], 'L0_attn_a_conv_w': _L0_attn_a_in['conv_w'], 'L0_attn_a_Wq': _L0_attn_a_in['Wq'], 'L0_attn_a_Wk': _L0_attn_a_in['Wk'], 'L0_attn_a_Wv': _L0_attn_a_in['Wv'], 'L0_attn_a_Wb': _L0_attn_a_in['Wb'], 'L0_attn_a_Wg': _L0_attn_a_in['Wg'], 'L0_attn_a_norm_w': _L0_attn_a_in['norm_w'], 'L0_attn_a_Wo': _L0_attn_a_in['Wo'], 'L0_attn_b_W_rkv': _L0_attn_b_in['W_rkv'], 'L0_attn_b_b_rkv': _L0_attn_b_in['b_rkv'], 'L0_attn_b_W_o': _L0_attn_b_in['W_o'], 'L0_attn_b_b_o': _L0_attn_b_in['b_o'], 'L0_attn_b_nu_log': _L0_attn_b_in['nu_log'], 'L0_attn_b_gamma_log': _L0_attn_b_in['gamma_log'], 'L0_ffn_router_w': _L0_ffn_in['router_w'], 'L0_ffn_w_fc': _L0_ffn_in['w_fc'], 'L0_ffn_b_fc': _L0_ffn_in['b_fc'], 'L0_ffn_w_proj': _L0_ffn_in['w_proj'], 'L0_ffn_b_proj': _L0_ffn_in['b_proj']}
    _x0 = _d['L0_attn_a_hidden_states']
    _d['L0_attn_a_hidden_states'] = jax.random.normal(jax.random.fold_in(jax.random.key(seed), 1), (8, 1024, 128), dtype=_x0.dtype)
    del _x0
    return _d

def reference(L0_attn_a_hidden_states, L0_attn_a_conv_w, L0_attn_a_Wq, L0_attn_a_Wk, L0_attn_a_Wv, L0_attn_a_Wb, L0_attn_a_Wg, L0_attn_a_norm_w, L0_attn_a_Wo, L0_attn_b_W_rkv, L0_attn_b_b_rkv, L0_attn_b_W_o, L0_attn_b_b_o, L0_attn_b_nu_log, L0_attn_b_gamma_log, L0_ffn_router_w, L0_ffn_w_fc, L0_ffn_b_fc, L0_ffn_w_proj, L0_ffn_b_proj):

    def _L0_attn_a_ref(hidden_states, conv_w, Wq, Wk, Wv, Wb, Wg, norm_w, Wo):
        import jax, jax.numpy as jnp
        import numpy as np
        from jax.scipy.linalg import solve_triangular
        H = 4
        CHUNK = 64
        NORM_EPS = 1e-05

        def _l2norm(x):
            return x / jnp.clip(jnp.linalg.norm(x, axis=-1, keepdims=True), 1e-12)

        def _deltanet_forward(hidden_states, conv_w, Wq, Wk, Wv, Wb, Wg, norm_w, Wo):
            B, L, D = hidden_states.shape
            Kc = conv_w.shape[1]
            dqh = Wq.shape[1] // H
            dvh = Wv.shape[1] // H
            xp = jnp.pad(hidden_states, ((0, 0), (Kc - 1, 0), (0, 0)))
            h = sum((conv_w[:, i] * xp[:, i:i + L, :] for i in range(Kc)))
            h = jax.nn.silu(h)
            q = (h @ Wq).reshape(B, L, H, dqh).transpose(0, 2, 1, 3)
            k = (h @ Wk).reshape(B, L, H, dqh).transpose(0, 2, 1, 3)
            v = (h @ Wv).reshape(B, L, H, dvh).transpose(0, 2, 1, 3)
            q = _l2norm(q)
            k = _l2norm(k)
            beta = jax.nn.sigmoid(h @ Wb).transpose(0, 2, 1)
            qm = q.reshape(B * H, L, dqh)
            km = k.reshape(B * H, L, dqh)
            vm = v.reshape(B * H, L, dvh)
            bm = beta.reshape(B * H, L)
            Nc = L // CHUNK
            eye = jnp.eye(CHUNK, dtype=q.dtype)

            def per_head(qh, kh, vh, bh):
                qs = qh.reshape(Nc, CHUNK, dqh)
                ks_ = kh.reshape(Nc, CHUNK, dqh)
                vs = vh.reshape(Nc, CHUNK, dvh)
                bs = bh.reshape(Nc, CHUNK)

                def step(S, xs):
                    qc, kc, vc, bc = xs
                    kb = kc * bc[:, None]
                    A = jnp.tril(kb @ kc.T, -1)
                    U = solve_triangular(eye + A, vc * bc[:, None] - kb @ S, lower=True)
                    o = qc @ S + jnp.tril(qc @ kc.T) @ U
                    return (S + kc.T @ U, o)
                S0 = jnp.zeros((dqh, dvh), qh.dtype)
                _, o = jax.lax.scan(step, S0, (qs, ks_, vs, bs))
                return o.reshape(L, dvh)
            o = jax.vmap(per_head)(qm, km, vm, bm)
            o = o.reshape(B, H, L, dvh).transpose(0, 2, 1, 3)
            g = (h @ Wg).reshape(B, L, H, dvh)
            rms = o * jax.lax.rsqrt(jnp.mean(o * o, axis=-1, keepdims=True) + NORM_EPS)
            out = rms * norm_w * (g * jax.nn.sigmoid(g))
            return out.reshape(B, L, H * dvh) @ Wo
        return _deltanet_forward(hidden_states, conv_w, Wq, Wk, Wv, Wb, Wg, norm_w, Wo)

    def _L0_attn_b_ref(inputs, W_rkv, b_rkv, W_o, b_o, nu_log, gamma_log):
        import jax, jax.numpy as jnp
        import numpy as np
        B, L, H, U = (4, 512, 128, 128)
        rkv = jnp.einsum('blh,hu->blu', inputs, W_rkv) + b_rkv
        r, k, v = jnp.split(rkv, 3, axis=-1)
        r = jax.nn.sigmoid(r)
        k = jnp.exp(k)
        kv = k * v
        u = jnp.concatenate([kv, k], axis=-1)
        nu = jnp.exp(jnp.concatenate([nu_log, nu_log]))
        gamma = jnp.exp(nu_log + gamma_log) - 1.0
        lam = jnp.exp(-nu)
        a = jnp.broadcast_to(lam, u.shape)

        def combine(c1, c2):
            a1, x1 = c1
            a2, x2 = c2
            return (a1 * a2, x1 * a2 + x2)
        _, y = jax.lax.associative_scan(combine, (a, u), axis=1)
        u1, u2 = jnp.split(y, 2, axis=-1)
        x = (u1 + gamma * kv) / (u2 + gamma * k + 1e-06) * r
        return jnp.einsum('blu,uh->blh', x, W_o) + b_o

    def _L0_ffn_ref(x, router_w, w_fc, b_fc, w_proj, b_proj):
        import math
        import jax, jax.numpy as jnp
        import numpy as np
        TOP_K = 2
        _GELU_C = math.sqrt(2.0 / math.pi)

        def gelu_new(x):
            return 0.5 * x * (1.0 + jnp.tanh(_GELU_C * (x + 0.044715 * x * x * x)))
        B, T, C = x.shape
        E = router_w.shape[0]
        N = B * T
        xf = x.reshape(N, C)
        logits = xf @ router_w.T
        probs = jax.nn.softmax(logits, axis=-1)
        topk_probs, topk_idx = jax.lax.top_k(probs, TOP_K)
        topk_probs = topk_probs / jnp.sum(topk_probs, axis=-1, keepdims=True)
        combine = jnp.zeros((N, E), dtype=x.dtype).at[jnp.arange(N)[:, None], topk_idx].add(topk_probs)
        h = gelu_new(jnp.einsum('nc,ech->neh', xf, w_fc) + b_fc)
        out = jnp.einsum('neh,ehc->nec', h, w_proj) + b_proj
        y = jnp.einsum('nec,ne->nc', out, combine)
        return y.reshape(B, T, C)
    x = L0_attn_a_hidden_states
    x = x + _L0_attn_a_ref(_layernorm(x, axis=-1), L0_attn_a_conv_w, L0_attn_a_Wq, L0_attn_a_Wk, L0_attn_a_Wv, L0_attn_a_Wb, L0_attn_a_Wg, L0_attn_a_norm_w, L0_attn_a_Wo)
    x = x + _L0_ffn_ref(_layernorm(x, axis=-1), L0_ffn_router_w, L0_ffn_w_fc, L0_ffn_b_fc, L0_ffn_w_proj, L0_ffn_b_proj)
    x = x + _L0_attn_b_ref(_layernorm(x, axis=-1), L0_attn_b_W_rkv, L0_attn_b_b_rkv, L0_attn_b_W_o, L0_attn_b_b_o, L0_attn_b_nu_log, L0_attn_b_gamma_log)
    x = x + _L0_ffn_ref(_layernorm(x, axis=-1), L0_ffn_router_w, L0_ffn_w_fc, L0_ffn_b_fc, L0_ffn_w_proj, L0_ffn_b_proj)
    return x

_drawn_inputs = setup_inputs


def setup_inputs(seed=0):
    import zlib

    import numpy as np

    out = dict(_drawn_inputs(seed))
    spreads = {'L0_attn_a_norm_w': (1.0, 0.6),
     'L0_attn_b_b_rkv': (0.0, 0.1),
     'L0_attn_b_b_o': (0.0, 0.1),
     'L0_attn_b_gamma_log': (0.0, 2.0)}
    factors = {'L0_attn_a_Wb': 27.591}
    for name, (base, spread) in spreads.items():
        noise = np.random.default_rng([zlib.crc32(name.encode()), seed]).standard_normal(out[name].shape)
        drawn = base * np.exp(spread * noise) if base else spread * noise
        out[name] = jnp.asarray(drawn.astype(out[name].dtype))
    for name, factor in factors.items():
        out[name] = (out[name] * factor).astype(out[name].dtype)
    return out
```

```python
from contextlib import ExitStack

import concourse.bass as bass
from concourse import mybir

F32 = mybir.dt.float32
U32 = mybir.dt.uint32
ALU = mybir.AluOpType
ACT = mybir.ActivationFunctionType
AXX = mybir.AxisListType.X

P = 128
D = 128
HEADS = 4
DK = 16
DKP = 32
DV = 32
RH = DV + DK
C = 32
Q = P // C
SUB = 16
LN_EPS = 1e-5
RMS_EPS = 1e-5
NORM_MIN_SQ = 1e-24
E_CONST = 2.718281828459045


def bc(ap, axis, n):
    v = ap.unsqueeze(axis)
    shape = list(v.shape)
    shape[axis] = n
    return v.to_broadcast(shape)


class Chain:

    def __init__(self, eng, sem):
        self.eng, self.sem, self.base, self.k = eng, sem, 0, 0

    def mark(self, ins):
        ins.then_inc(self.sem, 1)
        self.k += 1

    def link(self, ins):
        self.mark(ins)
        self.wait()

    def wait(self):
        self.eng.wait_ge(self.sem, self.base + self.k)

    def enter(self, i, per):
        self.done, self.per, self.k = self.base + self.k, per, 0
        self.base = i * per + self.done

    def leave(self, n):
        assert self.k == self.per, f"{self.k} links in the body, {self.per} stated"
        self.base, self.k = self.done + n * self.per, 0


def hybrid_kernel(nc, ap, out, phases=4):
    B, L, _ = ap["hidden"].shape
    NB = B * L // P
    BPB = L // P
    E, _, HID = ap["w_fc"].shape
    HC = HID // P
    GB = 4
    GT = GB * P
    NG = NB // GB
    GPB = BPB // GB
    assert GPB == 2
    NPROJ = 2 * HEADS * DK + 2 * HEADS * DV + HEADS
    KQ, V0, G0, B0 = 2 * HEADS * DK, 2 * HEADS * DK, 2 * HEADS * DK + HEADS * DV, NPROJ - HEADS

    ctx = ExitStack()
    with ctx:
        def sb(name, shape, dt=F32):
            return ctx.enter_context(nc.sbuf_tensor(name, [P] + shape, dt))

        def sem(name):
            return ctx.enter_context(nc.semaphore(name))

        ps = ctx.enter_context(nc.psum_tensor("ps", [P, 8, 512], F32))

        x = sb("x", [NB, D])
        ident = sb("ident", [P])
        bd32 = sb("bd32", [P])
        m_causal = sb("m_causal", [P])
        m_off = sb("m_off", [P])
        neg_half = sb("neg_half", [NB])
        e_col = sb("e_col", [1])
        iota8 = sb("iota8", [E])
        ones_row = sb("ones_row", [P])
        conv_w = sb("conv_w", [4])
        w_all = sb("w_all", [NPROJ])
        wo = sb("wo", [D])
        normw = sb("normw", [DV])
        w_rkv = sb("w_rkv", [3 * D])
        b_rkv = sb("b_rkv", [3])
        w_o = sb("w_o", [D])
        bo_row = sb("bo_row", [D])
        nu_col = sb("nu_col", [1])
        ga_col = sb("ga_col", [1])
        lam = sb("lam", [4])
        router = sb("router", [P])
        routerT = sb("routerT", [E])
        bfc_rows = sb("bfc_rows", [P])
        bfcT = sb("bfcT", [E * HC])
        w_fc = sb("w_fc", [E, HID])
        w_pr = sb("w_pr", [E * HC, D])
        b_pr = sb("b_pr", [D])
        half_br = sb("half_br", [1])
        stats = sb("stats", [BPB, 6])
        mv = sb("mv", [BPB, 2])
        unused = sb("unused", [1])
        rstd = sb("rstd", [BPB])
        y = sb("y", [BPB, D])
        yT = sb("yT", [3 + L])
        cv = sb("cv", [2, GT])
        hT = sb("hT", [L])
        kqv = sb("kqv", [BPB, G0])
        gs = sb("gs", [BPB, HEADS * DV])
        th = sb("th", [BPB, HEADS])
        beta = sb("beta", [BPB, HEADS])
        nbeta = sb("nbeta", [BPB, HEADS])
        sq = sb("sq", [BPB, P])
        ss = sb("ss", [BPB, 2 * HEADS])
        rn = sb("rn", [BPB, 2 * HEADS])
        kn = sb("kn", [BPB, HEADS, DKP])
        qn = sb("qn", [BPB, HEADS, DKP])
        R = sb("R", [BPB, HEADS, RH])
        kT = sb("kT", [BPB, P])
        qT = sb("qT", [BPB, P])
        g_off = sb("g_off", [BPB, HEADS, P])
        pT = sb("pT", [BPB, HEADS, P])
        n_c = sb("n_c", [BPB * HEADS, C])
        n_p = sb("n_p", [C, C])
        t_p = sb("t_p", [C, C])
        prod = sb("prod", [2, SUB, SUB])
        t_c = n_c
        t_bd = sb("t_bd", [BPB, HEADS, P])
        yv = sb("yv", [2, HEADS, RH])
        zv = sb("zv", [2, HEADS, RH])
        ub = sb("ub", [BPB, HEADS * DV])
        wp = sb("wp", [BPB, HEADS, DKP])
        wT = kqv[:, 0:BPB // 2, :].rearrange("p a (z c) -> p (a z) c", z=2)
        u = y
        NS = 8
        S = sb("S", [NS, HEADS * DV])
        o = cv[:, :, :].rearrange("p a (n c) -> p (a n) c", c=P)
        ro = sb("ro", [BPB * HEADS])
        oT = hT
        yTg = yT[:, 0:GT]
        lg = sb("lg", [GB, E])
        top = sb("top", [GB, 8])
        idx = sb("idx", [GB, 8], U32)
        idxf = sb("idxf", [GB, 8])
        dlt = sb("dlt", [GB])
        tnh = sb("tnh", [GB])
        w12 = sb("w12", [2, GB])
        oh = sb("oh", [2, GB, E])
        comb = sb("comb", [GB, E])
        combT = hT[:, 0:GT]
        hid = t_bd[:, :, :, :].rearrange("p (k c) h t -> p k c (h t)", k=2)

        def diagonal_blocks(t, i, what):
            start, dims = {
                "lm -> ml": (0, [[1, i], [C, i]]),
                "row": (i, [[C, i]]),
                "row out": (C * i, [[1, i]]),
            }[what]
            return bass.AP(tensor=t[:, :, :].tensor, offset=start,
                           ap=[list(t[:, :, :].ap[0]), [SUB * C + SUB, 2]] + dims)

        def flat(t):
            return t.rearrange("p a h c -> p (a h c)")

        l_k, l_kv, l_u2 = flat(g_off[:, 0:2]), flat(g_off[:, 2:4]), flat(g_off[:, 4:6])
        l_u1, l_r = flat(pT[:, 0:2]), flat(pT[:, 2:4])

        SEMS = {}

        def s(name):
            if name not in SEMS:
                SEMS[name] = sem(name)
            return SEMS[name]

        block = ctx.enter_context(nc.Block())

        out_v = out.rearrange("b (n p) c -> p (b n) c", p=P)
        x_v = ap["hidden"].rearrange("b (n p) c -> b p n c", p=P)

        GRAM_BANK = (4, 0)
        N_W = 17

        @block.sync
        def _(sp):
            sp.dma_start(x[:, 0:BPB, :], x_v[0]).then_inc(s("x_in"), 16)
            kw = HEADS * DK
            vw = HEADS * DV
            loads = [
                (conv_w[:, :], ap["conv_w"]),
                (w_all[:, 0:kw], ap["Wk"]), (w_all[:, kw:2 * kw], ap["Wq"]),
                (w_all[:, V0:V0 + vw], ap["Wv"]), (w_all[:, G0:G0 + vw], ap["Wg"]),
                (w_all[:, B0:NPROJ], ap["Wb"]), (wo[:, :], ap["Wo"]),
                (normw[:, :], ap["norm_w"].partition_broadcast(P)),
                (w_rkv[:, :], ap["W_rkv"]), (b_rkv[:, :], ap["b_rkv"].rearrange("(t p) -> p t", p=P)),
                (w_o[:, :], ap["W_o"]), (bo_row[0:1, :], ap["b_o"].rearrange("(a n) -> a n", a=1)),
                (nu_col[:, :], ap["nu_log"].rearrange("(p a) -> p a", a=1)),
                (ga_col[:, :], ap["gamma_log"].rearrange("(p a) -> p a", a=1)),
                (router[0:E, :], ap["router_w"]),
                (bfc_rows[0:E * HC, :], ap["b_fc"].rearrange("e (c p) -> (e c) p", p=P)),
                (b_pr[0:E, :], ap["b_proj"]),
            ]
            assert len(loads) == N_W
            with nc.allow_non_contiguous_dma(reason="a few hundred 4-byte elements, once"):
                for dst, src in loads:
                    sp.dma_start(dst, src).then_inc(s("w_in"), 16)
            sp.wait_ge(s("x_in"), 16)
            for b in range(1, B):
                sp.dma_start(x[:, b * BPB:(b + 1) * BPB, :], x_v[b]).then_inc(s("x_in"), 16)
                sp.wait_ge(s("x_in"), 16 * (b + 1))
            if phases >= 4:
                with sp.Fori(0, NG) as g:
                    sp.wait_ge(s("moe1_done"), g + 1)
                    sp.dma_start(out_v[:, bass.ds(g * GB, GB), :], x[:, bass.ds(g * GB, GB), :]).then_inc(s("stored"), 16)
            else:
                sp.wait_ge(s("phase_done"), phases)
                sp.wait_ge(s("experts_in"), 32)
                with sp.Fori(0, NG) as g:
                    sp.dma_start(out_v[:, bass.ds(g * GB, GB), :], x[:, bass.ds(g * GB, GB), :]).then_inc(s("stored"), 16)
            sp.wait_ge(s("stored"), 16 * NG)

        @block.gpsimd
        def _(pool):
            ch = Chain(pool, s("pool_chain"))
            pool.memset(ident[:, :], 0.0)
            pool.memset(neg_half[:, :], -0.5)
            pool.memset(e_col[:, :], E_CONST)
            pool.memset(ones_row[:, :], 1.0)
            pool.memset(yT[:, 0:3], 0.0)
            pool.memset(kn[:, :, :, :], 0.0)
            pool.memset(qn[:, :, :, :], 0.0)
            pool.memset(wp[:, :, :, :], 0.0)
            pool.memset(t_p[:, :, :], 0.0)
            ch.link(pool.memset(bd32[:, :], 1.0))
            pool.affine_select(out=ident[:, :], in_=ident[:, :], compare_op=ALU.not_equal, fill=1.0,
                               base=0, pattern=[[-1, P]], channel_multiplier=1)
            t_diag = t_p[:, :, :]
            pool.affine_select(out=t_diag, in_=t_diag, compare_op=ALU.not_equal, fill=1.0,
                               base=0, pattern=[[1, C], [-1, C]], channel_multiplier=0)
            pool.iota(iota8[:, :], pattern=[[1, E]], base=0, channel_multiplier=0,
                      allow_small_or_imprecise_dtypes=True)
            quad = bd32[:, :].rearrange("p (q i) -> p q i", i=C)
            ch.link(pool.affine_select(out=quad, in_=quad, compare_op=ALU.is_ge, fill=0.0,
                                       base=0, pattern=[[-C, Q], [0, C]], channel_multiplier=1))
            ch.link(pool.affine_select(out=quad, in_=quad, compare_op=ALU.is_ge, fill=0.0,
                                       base=C - 1, pattern=[[C, Q], [0, C]], channel_multiplier=-1))
            pool.affine_select(out=m_causal[:, :], in_=bd32[:, :], compare_op=ALU.is_ge, fill=0.0,
                               base=0, pattern=[[1, P]], channel_multiplier=-1)
            off = m_off[:, :].rearrange("p (q i) -> p q i", i=C)
            ch.link(pool.affine_select(out=off, in_=quad, compare_op=ALU.is_ge, fill=0.0,
                                       base=SUB - 1, pattern=[[C, Q], [0, C]], channel_multiplier=-1))
            pool.memset(off[:, :, 0:SUB], 0.0).then_inc(s("consts"), 1)

            pool.wait_ge(s("w_in"), 16 * N_W)
            pool.tensor_tensor(lam[:, 2:3], e_col[:, :], nu_col[:, :], ALU.pow)
            ch.link(pool.tensor_tensor(lam[:, 1:2], nu_col[:, :], ga_col[:, :], ALU.add))
            ch.link(pool.tensor_scalar(lam[:, 2:3], lam[:, 2:3], -1.0, None, ALU.mult))
            ch.link(pool.tensor_tensor(lam[:, 1:2], e_col[:, :], lam[:, 1:2], ALU.pow))
            pool.tensor_scalar(lam[:, 1:2], lam[:, 1:2], -1.0, None, ALU.add)
            pool.tensor_tensor(lam[:, 0:1], e_col[:, :], lam[:, 2:3], ALU.pow)
            pool.tensor_scalar(half_br[:, :], b_rkv[:, 0:1], 0.5, None, ALU.mult).then_inc(s("lam_ready"), 1)

            with pool.Fori(0, B) as b:
                pool.wait_ge(s("d_var"), b + 1)
                pool.tensor_tensor(rstd[:, :], rstd[:, :], neg_half[:, 0:BPB], ALU.pow).then_inc(s("d_rstd"), 1)
                pool.wait_ge(s("d_ss"), b + 1)
                pool.tensor_tensor(rn[:, :, :], ss[:, :, :],
                                   neg_half[:, 0:2 * HEADS * BPB].rearrange("p (n h) -> p n h", n=BPB),
                                   ALU.pow).then_inc(s("d_rn"), 1)
                pool.wait_ge(s("d_inv"), b + 1)
                for n in range(BPB):
                    pool.tensor_tensor(t_bd[:, n].rearrange("p h (q i) -> p h q i", i=C),
                                       bc(t_c[:, n * HEADS:(n + 1) * HEADS, :], 2, Q),
                                       bc(bd32[:, :].rearrange("p (q i) -> p q i", i=C), 1, HEADS),
                                       ALU.mult).then_inc(s("d_tbd"), 1)
                pool.wait_ge(s("d_oss"), b + 1)
                pool.tensor_tensor(ro[:, :], ro[:, :], neg_half[:, 0:BPB * HEADS], ALU.pow).then_inc(s("d_ro"), 1)

            def moe_pool(m):
                with pool.Fori(0, NG) as g:
                    pool.wait_ge(s(f"moe{m}_var"), g + 1)
                    pool.tensor_tensor(rstd[:, 0:GB], rstd[:, 0:GB], neg_half[:, 0:GB], ALU.pow)\
                        .then_inc(s(f"moe{m}_rstd"), 1)

            if phases >= 2:
                moe_pool(0)
            if phases >= 3:
                with pool.Fori(0, B) as b:
                    pool.wait_ge(s("l_var"), b + 1)
                    pool.tensor_tensor(rstd[:, :], rstd[:, :], neg_half[:, 0:BPB], ALU.pow).then_inc(s("l_rstd"), 1)
            if phases >= 4:
                moe_pool(1)

        @block.vector
        def _(ve):
            ch = Chain(ve, s("ve_chain"))

            def carry_wait():
                ve.memset(unused[:, :], 0.0)

            def variances(n0, nb, var_sem):
                for j in range(nb):
                    ins = ve.bn_stats(stats[:, j, :], x[:, bass.ds(n0 + j, 1), :].rearrange("p a c -> p (a c)"))
                ch.link(ins)
                carry_wait()
                for j in range(nb):
                    ins = ve.bn_aggr(mv[:, j, :], stats[:, j, :])
                ch.link(ins)
                ve.tensor_scalar(rstd[:, 0:nb], mv[:, 0:nb, 1], LN_EPS, None, ALU.add).then_inc(s(var_sem), 1)

            def normalise(n0, nb, rstd_sem, rstd_at, y_sem):
                ve.wait_ge(s(rstd_sem), rstd_at)
                for j in range(nb):
                    ve.tensor_scalar(y[:, j, :], x[:, bass.ds(n0 + j, 1), :].rearrange("p a c -> p (a c)"),
                                     mv[:, j, 0:1], rstd[:, j:j + 1], ALU.subtract, ALU.mult).then_inc(s(y_sem), 1)

            ve.wait_ge(s("consts"), 1)
            ve.wait_ge(s("w_in"), 16 * N_W)

            LINKS = 2 + 2 * 3 + 3 + 2 + (SUB - 1) * 2 + 5
            with ve.Fori(0, B) as b:
                ch.enter(b, LINKS)
                ve.wait_ge(s("x_in"), 16 * b + 16)
                n0 = b * BPB
                variances(n0, BPB, "d_var")
                normalise(n0, BPB, "d_rstd", b + 1, "d_y")
                for half in range(GPB):
                    ve.wait_ge(s("d_yT"), b * GPB + half + 1)
                    c0 = half * GT
                    for t in range(4):
                        src = yT[:, c0 + t:c0 + t + GT]
                        if t == 0:
                            ch.link(ve.tensor_scalar(cv[:, half, :], src, conv_w[:, 0:1], None, ALU.mult))
                        else:
                            ins = ve.scalar_tensor_tensor(cv[:, half, :], src, conv_w[:, t:t + 1], cv[:, half, :],
                                                          ALU.mult, ALU.add)
                            if t < 3:
                                ch.link(ins)
                            else:
                                ins.then_inc(s("d_conv"), 1)
                ve.wait_ge(s("d_kqv"), (b + 1) * BPB)
                ch.link(ve.tensor_tensor(sq[:, :, :], kqv[:, :, 0:KQ], kqv[:, :, 0:KQ], ALU.mult))
                ch.link(ve.tensor_reduce(ss[:, :, :], sq[:, :, :].rearrange("p n (h d) -> p n h d", d=DK),
                                         AXX, ALU.add))
                ve.tensor_scalar(ss[:, :, :], ss[:, :, :], NORM_MIN_SQ, None, ALU.max).then_inc(s("d_ss"), 1)
                ve.tensor_scalar(beta[:, :, :], th[:, :, :], 0.5, 0.5, ALU.mult, ALU.add)
                ch.link(ve.tensor_scalar(nbeta[:, :, :], th[:, :, :], -0.5, -0.5, ALU.mult, ALU.add))
                ve.wait_ge(s("d_rn"), b + 1)
                for dst, c0, h0 in ((kn, 0, 0), (qn, HEADS * DK, HEADS)):
                    ins = ve.tensor_tensor(dst[:, :, :, 0:DK],
                                           kqv[:, :, c0:c0 + HEADS * DK].rearrange("p n (h d) -> p n h d", d=DK),
                                           bc(rn[:, :, h0:h0 + HEADS], 3, DK), ALU.mult)
                    ins.then_inc(s("d_kn"), 1)
                ve.tensor_tensor(R[:, :, :, 0:DV],
                                 kqv[:, :, V0:V0 + HEADS * DV].rearrange("p n (h d) -> p n h d", d=DV),
                                 bc(beta[:, :, :], 3, DV), ALU.mult)
                ve.wait_ge(s("d_kn"), 2 * b + 2)
                ve.tensor_tensor(R[:, :, :, DV:RH], kn[:, :, :, 0:DK], bc(beta[:, :, :], 3, DK),
                                 ALU.mult).then_inc(s("d_R"), 1)
                for n in range(BPB):
                    bk = GRAM_BANK[n % 2]
                    ve.wait_ge(s("d_gram"), b * BPB + n + 1)
                    for q in range(Q):
                        r = slice(C * q, C * q + C)
                        ve.tensor_copy(n_c[r, n * HEADS:(n + 1) * HEADS, :], ps[r, bk:bk + HEADS, C * q:C * q + C])
                    ve.tensor_tensor(g_off[:, n], ps[:, bk:bk + HEADS, 0:P], bc(m_off[:, :], 1, HEADS), ALU.mult)
                    ve.tensor_tensor(pT[:, n], ps[:, bk:bk + HEADS, P:2 * P], bc(m_causal[:, :], 1, HEADS),
                                     ALU.mult).then_inc(s("d_gsb"), 1)
                ve.wait_ge(s("d_gsb"), b * BPB + BPB)
                ch.link(ve.tensor_tensor(n_c[:, :, :], n_c[:, :, :],
                                         bc(nbeta[:, :, :].rearrange("p n h -> p (n h)"), 2, C), ALU.mult))
                ch.link(ve.transpose(n_p[:, :, :], n_c[:, :, :].rearrange("p m j -> p j m")))
                for i in range(1, SUB):
                    ch.link(ve.tensor_tensor(prod[:, :, 0:i, 0:i], diagonal_blocks(t_p, i, "lm -> ml"),
                                             bc(diagonal_blocks(n_p, i, "row"), 2, i), ALU.mult))
                    ch.link(ve.tensor_reduce(diagonal_blocks(t_p, i, "row out"), prod[:, :, 0:i, 0:i], AXX, ALU.add))
                ve.transpose(t_c[:, :, :].rearrange("p m i -> p i m"), t_p[:, :, :]).then_inc(s("d_inv"), 1)
                for n in range(BPB + 1):
                    if n < BPB:
                        ve.wait_ge(s("d_z"), b * BPB + n + 1)
                        if n >= 2:
                            ve.wait_ge(s("d_w"), b * BPB + n - 1)
                        ve.tensor_tensor(zv[:, n % 2], ps[:, 2, 192:384].rearrange("p (h d) -> p h d", h=HEADS),
                                         bc(beta[:, n, :], 2, RH), ALU.mult).then_inc(s("d_zv"), 1)
                    if n >= 1:
                        m = n - 1
                        ve.wait_ge(s("d_w"), b * BPB + m + 1)
                        w_ps = ps[:, 3, 0:192].rearrange("p (h d) -> p h d", h=HEADS)
                        ve.tensor_tensor(ub[:, m].rearrange("p (h d) -> p h d", h=HEADS), yv[:, m % 2, :, 0:DV],
                                         w_ps[:, :, 0:DV], ALU.subtract)
                        ve.tensor_tensor(wp[:, m, :, 0:DK], yv[:, m % 2, :, DV:RH], w_ps[:, :, DV:RH],
                                         ALU.subtract).then_inc(s("d_uw"), 1)
                ve.memset(S[:, 0, :], 0.0).then_inc(s("d_S"), 1)
                ve.wait_ge(s("d_uw"), b * BPB + BPB)
                for c in range(BPB * Q):
                    n, q = divmod(c, Q)
                    r = slice(C * q, C * q + C)
                    ve.wait_ge(s("d_ws"), b * BPB * Q + c + 1)
                    ve.tensor_tensor(u[r, n, :], ub[r, n, :], ps[r, 5, 0:P], ALU.subtract).then_inc(s("d_u"), 1)
                    if c + 1 < BPB * Q:
                        ve.wait_ge(s("d_ku"), b * (BPB * Q - 1) + c + 1)
                        if c + 1 >= NS:
                            ve.wait_ge(s("d_o"), b * BPB + (c + 1 - NS) // Q + 1)
                        ve.tensor_tensor(S[:, (c + 1) % NS, :], ps[:, 4, 0:P], bd32[:, :], ALU.mult).then_inc(s("d_S"), 1)
                ve.wait_ge(s("d_osb"), b * BPB + BPB)
                o4 = o[:, :, :].rearrange("p n (h d) -> p (n h) d", d=DV)
                gs4 = gs[:, :, :].rearrange("p n (h d) -> p (n h) d", d=DV)
                ch.link(ve.tensor_tensor(sq[:, :, :], o[:, :, :], o[:, :, :], ALU.mult))
                ch.link(ve.tensor_reduce(ro[:, :], sq[:, :, :].rearrange("p n (h d) -> p (n h) d", d=DV), AXX, ALU.add))
                ve.tensor_scalar(ro[:, :], ro[:, :], 1.0 / DV, RMS_EPS, ALU.mult, ALU.add).then_inc(s("d_oss"), 1)
                ch.link(ve.tensor_tensor(gs4, gs4, bc(normw[:, :], 1, BPB * HEADS), ALU.mult))
                ch.link(ve.tensor_tensor(gs[:, :, :], gs[:, :, :], o[:, :, :], ALU.mult))
                ve.wait_ge(s("d_ro"), b + 1)
                ch.link(ve.tensor_tensor(o4, gs4, bc(ro[:, :], 2, DV), ALU.mult))
                ve.sem_inc(s("d_og"), 1)
                for half in range(GPB):
                    ve.wait_ge(s("d_out"), b * GPB + half + 1)
                    xg = x[:, bass.ds(n0 + half * GB, GB), :]
                    ve.tensor_tensor(xg, xg, ps[:, 6 + half, :].rearrange("p (n c) -> p n c", n=GB), ALU.add)\
                        .then_inc(s("d_x"), 1)
                ch.leave(B)
            ve.wait_ge(s("d_x"), GPB * B)
            ve.sem_inc(s("phase_done"), 1)

            def moe_vector(m):
                def ln(g):
                    variances(g * GB, GB, f"moe{m}_var")
                    normalise(g * GB, GB, f"moe{m}_rstd", g + 1, f"moe{m}_y")

                def route(g):
                    ve.wait_ge(s(f"moe{m}_lg"), g + 1)
                    ch.link(ve.tensor_copy(lg[:, :, :], ps[:, 1, 0:GB * E].rearrange("p (n e) -> p n e", n=GB)))
                    carry_wait()
                    for j in range(GB):
                        ins = ve.max(top[:, j, :], lg[:, j, :])
                    ch.link(ins)
                    carry_wait()
                    for j in range(GB):
                        ins = ve.max_index(idx[:, j, :], top[:, j, :], lg[:, j, :])
                    ch.link(ve.tensor_tensor(dlt[:, :], top[:, :, 1], top[:, :, 0], ALU.subtract))
                    ve.sem_inc(s(f"moe{m}_dlt"), 1)
                    ch.link(ve.tensor_copy(idxf[:, :, 0:2], idx[:, :, 0:2]))
                    for k in range(2):
                        ins = ve.tensor_tensor(oh[:, k], bc(iota8[:, :], 1, GB), bc(idxf[:, :, k], 2, E), ALU.is_equal)
                    ch.link(ins)
                    ve.wait_ge(s(f"moe{m}_tanh"), g + 1)
                    ve.tensor_scalar(w12[:, 0, :], tnh[:, :], -0.5, 0.5, ALU.mult, ALU.add)
                    ch.link(ve.tensor_scalar(w12[:, 1, :], tnh[:, :], 0.5, 0.5, ALU.mult, ALU.add))
                    for k in range(2):
                        ins = ve.tensor_tensor(oh[:, k], oh[:, k], bc(w12[:, k, :], 2, E), ALU.mult)
                    ch.link(ins)
                    ve.tensor_tensor(comb[:, :, :], oh[:, 0], oh[:, 1], ALU.add).then_inc(s(f"moe{m}_comb"), 1)

                LINKS_ROUTE, LINKS_LN = 7, 2

                def group(g, ahead):
                    route(g)
                    xg = x[:, bass.ds(g * GB, GB), :]
                    ve.wait_ge(s(f"moe{m}_bias"), g + 1)
                    ve.tensor_tensor(xg, xg, ps[:, 0, :].rearrange("p (n c) -> p n c", n=GB), ALU.add)\
                        .then_inc(s(f"moe{m}_acc"), 1)
                    for e in range(E):
                        ve.wait_ge(s(f"moe{m}_pr"), g * E + e + 3)
                        ve.wait_ge(s(f"moe{m}_acc"), g * (E + 1) + e + 3)
                        for j in range(GB):
                            xb = x[:, bass.ds(g * GB + j, 1), :].rearrange("p a c -> p (a c)")
                            ins = ve.scalar_tensor_tensor(xb, ps[:, 6 + e % 2, j * D:(j + 1) * D],
                                                          comb[:, j, e:e + 1], xb, ALU.mult, ALU.add)
                        ins.then_inc(s(f"moe{m}_acc"), 1)
                        if e == 3 and ahead:
                            ln(g + 1)
                    ve.wait_ge(s(f"moe{m}_acc"), (g + 1) * (E + 1) + 2)
                    ve.sem_inc(s(f"moe{m}_done"), 1)

                ve.sem_inc(s(f"moe{m}_acc"), 2)
                ln(0)
                with ve.Fori(0, NG - 1) as g:
                    ch.enter(g, LINKS_ROUTE + LINKS_LN)
                    group(g, True)
                    ch.leave(NG - 1)
                group(NG - 1, False)
                ve.sem_inc(s("phase_done"), 1)

            if phases >= 2:
                moe_vector(0)

            if phases >= 3:
                kk, kv, u1, u2, rr = l_k, l_kv, l_u1, l_u2, l_r
                with ve.Fori(0, B) as b:
                    ch.enter(b, 2 + 7)
                    variances(b * BPB, BPB, "l_var")
                    normalise(b * BPB, BPB, "l_rstd", b + 1, "l_y")
                    for half in range(GPB):
                        ve.wait_ge(s("l_k"), b * GPB + half + 1)
                        hs = slice(half * GT, half * GT + GT)
                        ins = ve.scalar_tensor_tensor(kv[:, hs], ps[:, 4 + 3 * half, :], b_rkv[:, 2:3], kk[:, hs],
                                                      ALU.add, ALU.mult)
                    ch.link(ins)
                    decay = lam[:, 0:1].to_broadcast([P, L])
                    ve.tensor_tensor_scan(u1, decay, kv, 0.0, ALU.mult, ALU.add)
                    ch.link(ve.tensor_tensor_scan(u2, decay, kk, 0.0, ALU.mult, ALU.add))
                    ve.scalar_tensor_tensor(u1, kv, lam[:, 1:2], u1, ALU.mult, ALU.add)
                    ch.link(ve.scalar_tensor_tensor(u2, kk, lam[:, 1:2], u2, ALU.mult, ALU.add))
                    ch.link(ve.tensor_scalar(u2, u2, 1e-6, None, ALU.add))
                    ch.link(ve.reciprocal(u2, u2))
                    ch.link(ve.tensor_tensor(u1, u1, u2, ALU.mult))
                    ch.link(ve.tensor_scalar(rr, rr, 0.5, 0.5, ALU.mult, ALU.add))
                    ve.tensor_tensor(u1, u1, rr, ALU.mult).then_inc(s("l_xT"), 1)
                    for half in range(GPB):
                        ve.wait_ge(s("l_out"), b * GPB + half + 1)
                        xg = x[:, bass.ds(b * BPB + half * GB, GB), :]
                        ve.tensor_tensor(xg, xg, ps[:, half, :].rearrange("p (n c) -> p n c", n=GB), ALU.add)\
                            .then_inc(s("l_x"), 1)
                    ch.leave(B)
                ve.wait_ge(s("l_x"), GPB * B)
                ve.sem_inc(s("phase_done"), 1)
            if phases >= 4:
                moe_vector(1)

        @block.scalar
        def _(act):
            act.dma_start(w_fc[:, :, :], ap["w_fc"].rearrange("e c h -> c e h")).then_inc(s("experts_in"), 16)
            act.dma_start(w_pr[:, :, :], ap["w_proj"].rearrange("e (c p) n -> p (e c) n", p=P))\
                .then_inc(s("experts_in"), 16)
            act.wait_ge(s("setup_T"), 1)
            act.copy(routerT[:, :], ps[:, 0, 0:E])
            act.copy(bfcT[:, :], ps[:, 0, 128:128 + E * HC]).then_inc(s("setup_sb"), 1)

            with act.Fori(0, B) as b:
                for half in range(GPB):
                    act.wait_ge(s("d_T"), b * GPB + half + 1)
                    act.copy(yT[:, 3 + half * GT:3 + (half + 1) * GT], ps[:, 0 + half, :]).then_inc(s("d_yT"), 1)
                for half in range(GPB):
                    act.wait_ge(s("d_conv"), b * GPB + half + 1)
                    act.activation(hT[:, half * GT:(half + 1) * GT], cv[:, half, :], ACT.Silu).then_inc(s("d_h"), 1)
                for n in range(BPB):
                    act.wait_ge(s("d_proj"), b * BPB + n + 1)
                    bank = 2 + n % 2
                    act.copy(kqv[:, n, :], ps[:, bank, 0:G0])
                    act.activation(th[:, n, :], ps[:, bank, B0:NPROJ], ACT.Tanh, scale=0.5)
                    act.activation(gs[:, n, :], ps[:, bank, G0:B0], ACT.Silu).then_inc(s("d_kqv"), 1)
                for n in range(BPB):
                    act.wait_ge(s("d_kqT"), b * BPB + n + 1)
                    bank = n % 2
                    act.copy(kT[:, n, :], ps[:, bank, 0:P])
                    act.copy(qT[:, n, :], ps[:, bank, P:2 * P]).then_inc(s("d_kqTs"), 1)
                for n in range(BPB):
                    act.wait_ge(s("d_y1"), b * BPB + n + 1)
                    if n >= 2:
                        act.wait_ge(s("d_uw"), b * BPB + n - 1)
                    act.copy(yv[:, n % 2], ps[:, 2, 0:192].rearrange("p (h d) -> p h d", h=HEADS)).then_inc(s("d_yv"), 1)
                for half in range(GPB):
                    act.wait_ge(s("d_wT"), b * GPB + half + 1)
                    act.copy(wT[:, half * GB:(half + 1) * GB, :],
                             ps[:, half, :].rearrange("p (n c) -> p n c", n=GB)).then_inc(s("d_wTs"), 1)
                for n in range(BPB):
                    act.wait_ge(s("d_o"), b * BPB + n + 1)
                    act.copy(o[:, n, :], ps[:, 6 + n % 2, 0:P]).then_inc(s("d_osb"), 1)
                for half in range(GPB):
                    act.wait_ge(s("d_oT"), b * GPB + half + 1)
                    act.copy(oT[:, half * GT:(half + 1) * GT], ps[:, half, :]).then_inc(s("d_oTs"), 1)

            def moe_scalar(m):
                def evac_y(g):
                    act.wait_ge(s(f"moe{m}_T"), g + 1)
                    act.copy(yTg, ps[:, 0, :]).then_inc(s(f"moe{m}_yT"), 1)

                def group(g, ahead):
                    for e in range(E):
                        for c in range(HC):
                            act.wait_ge(s(f"moe{m}_fc"), g * E * HC + e * HC + c + 1)
                            if c == 0:
                                act.wait_ge(s(f"moe{m}_pr"), g * E + e + 1)
                            act.activation(hid[:, e % 2, c, :], ps[:, 2 + c, :], ACT.Gelu_apprx_tanh,
                                           bias=bfcT[:, e * HC + c:e * HC + c + 1]).then_inc(s(f"moe{m}_hid"), 1)
                        if e == 0:
                            act.wait_ge(s(f"moe{m}_dlt"), g + 1)
                            act.activation(tnh[:, :], dlt[:, :], ACT.Tanh, scale=0.5).then_inc(s(f"moe{m}_tanh"), 1)
                        if e == 1:
                            act.wait_ge(s(f"moe{m}_cT"), g + 1)
                            act.copy(combT[0:E, :], ps[0:E, 0, :]).then_inc(s(f"moe{m}_cTs"), 1)
                    if ahead:
                        evac_y(g + 1)

                act.sem_inc(s(f"moe{m}_hid"), HC)
                evac_y(0)
                with act.Fori(0, NG - 1) as g:
                    group(g, True)
                group(NG - 1, False)

            if phases >= 2:
                act.wait_ge(s("phase_done"), 1)
                moe_scalar(0)
            if phases >= 3:
                kk, rr = l_k, l_r
                act.sem_inc(s("l_xT"), 1)
                with act.Fori(0, B) as b:
                    for half in range(GPB):
                        act.wait_ge(s("l_T"), b * GPB + half + 1)
                        act.copy(yT[:, half * GT:(half + 1) * GT], ps[:, half, :]).then_inc(s("l_yT"), 1)
                    act.wait_ge(s("l_xT"), b + 1)
                    for half in range(GPB):
                        hs = slice(half * GT, half * GT + GT)
                        act.wait_ge(s("l_rkv"), b * GPB + half + 1)
                        act.activation(rr[:, hs], ps[:, 2 + 3 * half, :], ACT.Tanh, bias=half_br[:, :], scale=0.5)
                        act.activation(kk[:, hs], ps[:, 3 + 3 * half, :], ACT.Exp, bias=b_rkv[:, 1:2]).then_inc(s("l_k"), 1)
            if phases >= 4:
                moe_scalar(1)

        @block.tensor
        def _(pe):
            pe.wait_ge(s("consts"), 1)
            pe.wait_ge(s("w_in"), 16 * N_W)
            pe.transpose(ps[:, 0, 0:E], router[0:E, :], ident[0:E, 0:E])
            pe.transpose(ps[:, 0, 128:128 + E * HC], bfc_rows[0:E * HC, :], ident[0:E * HC, 0:E * HC])\
                .then_inc(s("setup_T"), 1)
            pe.wait_ge(s("setup_sb"), 1)

            with pe.Fori(0, B) as b:
                for half in range(GPB):
                    for j in range(GB):
                        n = half * GB + j
                        pe.wait_ge(s("d_y"), b * BPB + n + 1)
                        ins = pe.transpose(ps[:, half, j * P:(j + 1) * P], y[:, n, :], ident[:, :])
                    ins.then_inc(s("d_T"), 1)
                for n in range(BPB):
                    pe.wait_ge(s("d_h"), b * GPB + n // GB + 1)
                    if n >= 2:
                        pe.wait_ge(s("d_kqv"), b * BPB + n - 1)
                    pe.matmul(ps[:, 2 + n % 2, 0:NPROJ], hT[:, n * P:(n + 1) * P], w_all[:, :],
                              start=True, stop=True).then_inc(s("d_proj"), 1)
                def kq_T(n):
                    pe.wait_ge(s("d_kn"), 2 * b + 2)
                    if n >= 2:
                        pe.wait_ge(s("d_kqTs"), b * BPB + n - 1)
                    pe.transpose(ps[:, n % 2, 0:P], kn[:, n].rearrange("p h d -> p (h d)"), ident[:, :])
                    pe.transpose(ps[:, n % 2, P:2 * P], qn[:, n].rearrange("p h d -> p (h d)"), ident[:, :])\
                        .then_inc(s("d_kqT"), 1)

                for n in range(BPB):
                    kq_T(n)
                for n in range(BPB):
                    pe.wait_ge(s("d_kqTs"), b * BPB + (BPB if n else 1))
                    if n >= 2:
                        pe.wait_ge(s("d_gsb"), b * BPB + n - 1)
                    bk = GRAM_BANK[n % 2]
                    for h in range(HEADS):
                        r = slice(DKP * h, DKP * h + DKP)
                        pe.matmul(ps[:, bk + h, 0:P], kT[r, n, :], kT[r, n, :], start=True, stop=True)
                        ins = pe.matmul(ps[:, bk + h, P:2 * P], kT[r, n, :], qT[r, n, :], start=True, stop=True)
                    ins.then_inc(s("d_gram"), 1)
                pe.wait_ge(s("d_R"), b + 1)
                for n in range(BPB + 1):
                    if n < BPB:
                        pe.wait_ge(s("d_tbd"), b * BPB + n + 1)
                        if n >= 1:
                            pe.wait_ge(s("d_zv"), b * BPB + n)
                        for h in range(HEADS):
                            ins = pe.matmul(ps[:, 2, RH * h:RH * h + RH], t_bd[:, n, h, :], R[:, n, h, :],
                                            start=True, stop=True)
                        ins.then_inc(s("d_y1"), 1)
                        pe.wait_ge(s("d_yv"), b * BPB + n + 1)
                        for h in range(HEADS):
                            ins = pe.matmul(ps[:, 2, 192 + RH * h:192 + RH * h + RH], g_off[:, n, h, :], yv[:, n % 2, h, :],
                                            start=True, stop=True)
                        ins.then_inc(s("d_z"), 1)
                        pe.wait_ge(s("d_zv"), b * BPB + n + 1)
                        if n >= 1:
                            pe.wait_ge(s("d_uw"), b * BPB + n)
                        for h in range(HEADS):
                            ins = pe.matmul(ps[:, 3, RH * h:RH * h + RH], t_bd[:, n, h, :], zv[:, n % 2, h, :],
                                            start=True, stop=True)
                        ins.then_inc(s("d_w"), 1)
                    if n >= 1:
                        m = n - 1
                        pe.wait_ge(s("d_uw"), b * BPB + m + 1)
                        ins = pe.transpose(ps[:, m // GB, (m % GB) * P:(m % GB + 1) * P],
                                           wp[:, m].rearrange("p h d -> p (h d)"), ident[:, :])
                        if m % GB == GB - 1:
                            ins.then_inc(s("d_wT"), 1)
                for c in range(BPB * Q):
                    n, q = divmod(c, Q)
                    r = slice(C * q, C * q + C)
                    pe.wait_ge(s("d_wTs"), b * GPB + n // GB + 1)
                    pe.wait_ge(s("d_S"), b * BPB * Q + c + 1)
                    if c >= 1:
                        pe.wait_ge(s("d_u"), b * BPB * Q + c)
                    pe.matmul(ps[r, 5, 0:P], wT[:, n, r], S[:, c % NS, :], start=True, stop=True).then_inc(s("d_ws"), 1)
                    if q == 0 and n >= 2:
                        pe.wait_ge(s("d_osb"), b * BPB + n - 1)
                    pe.matmul(ps[r, 6 + n % 2, 0:P], qT[:, n, r], S[:, c % NS, :], start=True, stop=False,
                              skip_group_check=True)
                    pe.wait_ge(s("d_u"), b * BPB * Q + c + 1)
                    if c + 1 < BPB * Q:
                        pe.matmul(ps[:, 4, 0:P], kn[r, n].rearrange("p h d -> p (h d)"), u[r, n, :],
                                  start=(c == 0), stop=True, skip_group_check=True).then_inc(s("d_ku"), 1)
                    if q == Q - 1:
                        for h in range(HEADS):
                            ins = pe.matmul(ps[:, 6 + n % 2, DV * h:DV * h + DV], pT[:, n, h, :], u[:, n, DV * h:DV * h + DV],
                                            start=False, stop=(h == HEADS - 1), skip_group_check=True)
                        ins.then_inc(s("d_o"), 1)
                pe.wait_ge(s("d_og"), b + 1)
                for half in range(GPB):
                    for j in range(GB):
                        ins = pe.transpose(ps[:, half, j * P:(j + 1) * P], o[:, half * GB + j, :], ident[:, :])
                    ins.then_inc(s("d_oT"), 1)
                for half in range(GPB):
                    pe.wait_ge(s("d_oTs"), b * GPB + half + 1)
                    for j in range(GB):
                        n = half * GB + j
                        ins = pe.matmul(ps[:, 6 + half, j * P:(j + 1) * P], oT[:, n * P:(n + 1) * P], wo[:, :],
                                        start=True, stop=True)
                    ins.then_inc(s("d_out"), 1)

            def moe_tensor(m):
                def turn(g):
                    for j in range(GB):
                        pe.wait_ge(s(f"moe{m}_y"), g * GB + j + 1)
                        ins = pe.transpose(ps[:, 0, j * P:(j + 1) * P], y[:, j, :], ident[:, :])
                    ins.then_inc(s(f"moe{m}_T"), 1)

                def up(g, e):
                    for c in range(HC):
                        pe.wait_ge(s(f"moe{m}_hid"), g * E * HC + e * HC + c + 1)
                        pe.matmul(ps[:, 2 + c, :], w_fc[:, e, c * P:(c + 1) * P], yTg, start=True, stop=True)\
                            .then_inc(s(f"moe{m}_fc"), 1)

                def down(g, e):
                    pe.wait_ge(s(f"moe{m}_hid"), g * E * HC + (e + 1) * HC + HC)
                    pe.wait_ge(s(f"moe{m}_acc"), g * (E + 1) + (e + 1 if e < 2 else e + 2))
                    for j in range(GB):
                        for c in range(HC):
                            ins = pe.matmul(ps[:, 6 + e % 2, j * D:(j + 1) * D], hid[:, e % 2, c, j * P:(j + 1) * P],
                                            w_pr[:, e * HC + c, :], start=(c == 0), stop=(c == HC - 1))
                    ins.then_inc(s(f"moe{m}_pr"), 1)

                def group(g, ahead):
                    pe.wait_ge(s(f"moe{m}_yT"), g + 1)
                    for j in range(GB):
                        ins = pe.matmul(ps[:, 1, j * E:(j + 1) * E], yTg[:, j * P:(j + 1) * P], routerT[:, :],
                                        start=True, stop=True)
                    ins.then_inc(s(f"moe{m}_lg"), 1)
                    up(g, 0)
                    for e in range(E):
                        if e + 1 < E:
                            up(g, e + 1)
                        if e == 0:
                            pe.wait_ge(s(f"moe{m}_comb"), g + 1)
                            for j in range(GB):
                                ins = pe.transpose(ps[0:E, 0, j * P:(j + 1) * P], comb[:, j, :], ident[:, :])
                            ins.then_inc(s(f"moe{m}_cT"), 1)
                        if e == 1:
                            pe.wait_ge(s(f"moe{m}_cTs"), g + 1)
                            for j in range(GB):
                                ins = pe.matmul(ps[:, 0, j * D:(j + 1) * D], combT[0:E, j * P:(j + 1) * P], b_pr[0:E, :],
                                                start=True, stop=True)
                            ins.then_inc(s(f"moe{m}_bias"), 1)
                        if e == 5 and ahead:
                            turn(g + 1)
                        down(g, e)

                pe.sem_inc(s(f"moe{m}_pr"), 2)
                turn(0)
                with pe.Fori(0, NG - 1) as g:
                    group(g, True)
                group(NG - 1, False)

            if phases >= 2:
                pe.wait_ge(s("experts_in"), 32)
                moe_tensor(0)
            if phases >= 3:
                u1 = l_u1
                with pe.Fori(0, B) as b:
                    for half in range(GPB):
                        for j in range(GB):
                            pe.wait_ge(s("l_y"), b * BPB + half * GB + j + 1)
                            ins = pe.transpose(ps[:, half, j * P:(j + 1) * P], y[:, half * GB + j, :], ident[:, :])
                        ins.then_inc(s("l_T"), 1)
                    for half in range(GPB):
                        pe.wait_ge(s("l_yT"), b * GPB + half + 1)
                        for t in range(3):
                            ins = pe.matmul(ps[:, 2 + 3 * half + t, :], w_rkv[:, t * D:(t + 1) * D],
                                            yT[:, half * GT:(half + 1) * GT], start=True, stop=True)
                        ins.then_inc(s("l_rkv"), 1)
                    pe.wait_ge(s("l_xT"), b + 2)
                    for half in range(GPB):
                        for j in range(GB):
                            n = half * GB + j
                            cols = slice(j * D, (j + 1) * D)
                            pe.matmul(ps[:, half, cols], ones_row[0:1, :], bo_row[0:1, :], start=True, stop=False)
                            ins = pe.matmul(ps[:, half, cols], u1[:, n * P:(n + 1) * P], w_o[:, :], start=False, stop=True)
                        ins.then_inc(s("l_out"), 1)
            if phases >= 4:
                moe_tensor(1)


_NAMES = {
    "hidden": "L0_attn_a_hidden_states", "conv_w": "L0_attn_a_conv_w", "Wq": "L0_attn_a_Wq",
    "Wk": "L0_attn_a_Wk", "Wv": "L0_attn_a_Wv", "Wb": "L0_attn_a_Wb", "Wg": "L0_attn_a_Wg",
    "norm_w": "L0_attn_a_norm_w", "Wo": "L0_attn_a_Wo", "W_rkv": "L0_attn_b_W_rkv",
    "b_rkv": "L0_attn_b_b_rkv", "W_o": "L0_attn_b_W_o", "b_o": "L0_attn_b_b_o",
    "nu_log": "L0_attn_b_nu_log", "gamma_log": "L0_attn_b_gamma_log", "router_w": "L0_ffn_router_w",
    "w_fc": "L0_ffn_w_fc", "b_fc": "L0_ffn_b_fc", "w_proj": "L0_ffn_w_proj", "b_proj": "L0_ffn_b_proj",
}
PHASES = 4


def kernel(**inputs):
    import numpy as np
    import concourse.bacc as bacc
    from concourse.bass_utils import run_bass_kernel_spmd

    nc = bacc.Bacc("TRN2", target_bir_lowering=False, num_devices=1)
    arrays, aps = {}, {}
    for short, name in _NAMES.items():
        a = np.ascontiguousarray(inputs[name])
        arrays[f"in_{short}"] = a
        aps[short] = nc.dram_tensor(f"in_{short}", a.shape, F32, kind="ExternalInput").ap()
    out = nc.dram_tensor("out_x", inputs[_NAMES["hidden"]].shape, F32, kind="ExternalOutput").ap()
    hybrid_kernel(nc, aps, out, PHASES)
    r = run_bass_kernel_spmd(nc, [arrays], core_ids=[0])
    return r.results[0]["out_x"]
```

```python
from contextlib import ExitStack

import concourse.bass as bass
from concourse import mybir

F32 = mybir.dt.float32
F32R = mybir.dt.float32r
U32 = mybir.dt.uint32
ALU = mybir.AluOpType
ACT = mybir.ActivationFunctionType
AXX = mybir.AxisListType.X

P = 128
D = 128
HEADS = 4
DK = 16
DKP = 32
DV = 32
RH = DV + DK
C = 32
Q = P // C
SUB = 16
LN_EPS = 1e-5
RMS_EPS = 1e-5
NORM_MIN_SQ = 1e-24
E_CONST = 2.718281828459045


def bc(ap, axis, n):
    v = ap.unsqueeze(axis)
    shape = list(v.shape)
    shape[axis] = n
    return v.to_broadcast(shape)


class Chain:

    def __init__(self, eng, sem):
        self.eng, self.sem, self.base, self.k = eng, sem, 0, 0

    def mark(self, ins):
        ins.then_inc(self.sem, 1)
        self.k += 1
        return self.k

    def link(self, ins):
        self.mark(ins)
        self.wait()

    def wait(self, k=None):
        self.eng.wait_ge(self.sem, self.base + (self.k if k is None else k))

    def enter(self, i, per):
        self.done, self.per, self.k = self.base + self.k, per, 0
        self.base = i * per + self.done

    def leave(self, n):
        assert self.k == self.per, f"{self.k} links in the body, {self.per} stated"
        self.base, self.k = self.done + n * self.per, 0


def hybrid_kernel(nc, ap, out, phases=4):
    B, L, _ = ap["hidden"].shape
    NB = B * L // P
    BPB = L // P
    E, _, HID = ap["w_fc"].shape
    HC = HID // P
    GB = 4
    GT = GB * P
    NG = NB // GB
    GPB = BPB // GB
    assert GPB == 2
    NPROJ = 2 * HEADS * DK + 2 * HEADS * DV + HEADS
    KW = HEADS * DK
    KQ, V0, G0, B0 = 2 * HEADS * DK, 2 * HEADS * DK, 2 * HEADS * DK + HEADS * DV, NPROJ - HEADS

    ctx = ExitStack()
    with ctx:
        delta_ctx = ExitStack()

        def sb(name, shape, dt=F32):
            return ctx.enter_context(nc.sbuf_tensor(name, [P] + shape, dt))

        def sb1(name, shape, dt=F32):
            return delta_ctx.enter_context(nc.sbuf_tensor(name, [P] + shape, dt))

        def sem(name):
            return ctx.enter_context(nc.semaphore(name))

        ps = ctx.enter_context(nc.psum_tensor("ps", [P, 8, 512], F32))

        x = sb("x", [NB, D])
        ident = sb("ident", [P])
        bd = sb("bd", [HEADS * DV])
        m_p = sb("m_p", [C])
        neg_half = sb("neg_half", [NB])
        e_col = sb("e_col", [1])
        iota8 = sb("iota8", [E])
        ones_row = sb("ones_row", [P])
        conv_w = sb("conv_w", [4])
        w_all = sb("w_all", [NPROJ])
        wo = sb("wo", [D])
        normw = sb("normw", [DV])
        w_rkv = sb("w_rkv", [3 * D])
        b_rkv = sb("b_rkv", [3])
        w_o = sb("w_o", [D])
        bo_row = sb("bo_row", [D])
        nu_col = sb("nu_col", [1])
        ga_col = sb("ga_col", [1])
        lam = sb("lam", [4])
        router = sb("router", [P])
        routerT = sb("routerT", [E])
        bfc_rows = sb("bfc_rows", [P])
        bfcT = sb("bfcT", [E * HC])
        b_pr2 = sb("b_pr2", [D])
        half_br = sb("half_br", [1])
        stats = sb("stats", [BPB, 6])
        mv = sb("mv", [BPB, 2])
        unused = sb("unused", [1])
        pool_unused = sb("pool_unused", [4])
        rstd = sb("rstd", [BPB])
        y = sb("y", [BPB, D])
        yT = sb1("yT", [3 + L])
        hT = sb1("hT", [L])
        kqv = sb1("kqv", [BPB, G0])
        gs = sb1("gs", [BPB, HEADS * DV])
        th = sb1("th", [BPB, HEADS])
        beta = sb1("beta", [BPB, HEADS])
        nbeta = sb1("nbeta", [BPB, HEADS])
        ss = sb1("ss", [BPB, 2 * HEADS])
        rn = sb1("rn", [BPB, 2 * HEADS])
        kn = sb1("kn", [BPB, HEADS, DKP])
        qn = sb1("qn", [BPB, HEADS, DKP])
        R = sb1("R", [BPB, HEADS, RH])
        kqT = sb1("kqT", [BPB, 2, P])
        gp = sb1("gp", [BPB, HEADS, C])
        n_c = sb1("n_c", [BPB, HEADS, C])
        sq = n_c[:, :, :, :].rearrange("p n h j -> p n (h j)")
        n_p = sb1("n_p", [C, C])
        t_p = sb1("t_p", [C, C])
        prod = sb1("prod", [2, SUB, SUB])
        prod2 = sb1("prod2", [SUB, C])
        t_c = n_p[:, :, :].rearrange("p (n h) i -> p n h i", h=HEADS)
        t_bd = sb1("t_bd", [BPB, HEADS, P])
        p_bd = sb1("p_bd", [BPB, HEADS, P])
        b_kn = sb1("b_kn", [BPB, KW])
        b_qn = sb1("b_qn", [BPB, KW])
        b_R = sb1("b_R", [BPB, HEADS, RH])
        qp = sb1("qp", [2, KW])
        m_gs = sb1("m_gs", [BPB, HEADS * DV])
        uw = sb1("uw", [BPB, HEADS, RH])
        wk = sb1("wk", [BPB, KW])
        puw = sb1("puw", [BPB, HEADS, RH])
        qpT = sb1("qpT", [BPB, P])
        c_kn = sb1("c_kn", [BPB, KW])
        c_gs = sb1("c_gs", [BPB, HEADS * DV])
        NS = 8
        A = sb1("A", [NS, KW])
        S = sb1("S", [NS, HEADS * DV])
        o = sb1("o", [BPB, HEADS * DV])
        osq = sb1("osq", [GB, P])
        ro = sb1("ro", [2, GB * HEADS])
        oT = sb1("oT", [GT])

        def diagonal_blocks(t, i, what):
            start, dims = {
                "lm -> ml": (0, [[1, i], [C, i]]),
                "row": (i, [[C, i]]),
                "row out": (C * i, [[1, i]]),
            }[what]
            return bass.AP(tensor=t[:, :, :].tensor, offset=t[:, :, :].offset + start,
                           ap=[list(t[:, :, :].ap[0]), [SUB * C + SUB, 2]] + dims)

        delta_ctx.close()
        w_fc = sb("w_fc", [E, HID])
        w_pr = sb("w_pr", [E * HC, D])
        wfh = sb("wfh", [E, HID], F32R)
        wfl = sb("wfl", [E, HID], F32R)
        wph = sb("wph", [E * HC, D], F32R)
        wpl = sb("wpl", [E * HC, D], F32R)
        yTf = sb("yTf", [GT])
        yTh = sb("yTh", [2, GT], F32R)
        yTl = sb("yTl", [2, GT], F32R)
        hidf = sb("hidf", [HC, GT])
        hidh = sb("hidh", [2, HC, GT], F32R)
        hidl = sb("hidl", [2, HC, GT], F32R)
        wb = sb("wb", [2, GT])
        scaled = sb("scaled", [GT])
        acc = sb("acc", [GT])
        lg = sb("lg", [GB, E])
        top = sb("top", [GB, 8])
        idx = sb("idx", [GB, 8], U32)
        idxf = sb("idxf", [GB, 8])
        dlt = sb("dlt", [GB])
        tnh = sb("tnh", [GB])
        w12 = sb("w12", [2, GB])
        oh = sb("oh", [2, GB, E])
        comb = sb("comb", [GB, E])
        comb2 = sb("comb2", [GB, 2 * E], F32R)
        combT = sb("combT", [GT], F32R)
        sel_col = sb("sel_col", [E])
        sel = sb("sel", [E, P], F32R)
        raw = [w[:, :, :].rearrange("p a c -> p (a c)")[:, k * L:(k + 1) * L] for w, n in
               ((w_fc, E * HID), (w_pr, E * HC * D), (hidf, HC * GT)) for k in range(n // L)]
        l_yT, l_kv, l_u1, l_u2, l_k0, l_k1, l_r0, l_r1, l_x = raw[:9]
        l_k, l_r = (l_k0, l_k1), (l_r0, l_r1)
        l_const = sb("l_const", [2])

        SEMS = {}

        def s(name):
            if name not in SEMS:
                SEMS[name] = sem(name)
            return SEMS[name]

        block = ctx.enter_context(nc.Block())

        out_v = out.rearrange("b (n p) c -> p (b n) c", p=P)
        x_v = ap["hidden"].rearrange("b (n p) c -> b p n c", p=P)

        NCH = BPB * Q
        NPAIR = BPB // 2
        A_RSTD, A_Y, A_T, A_CONV, A_PROJ, A_NORM, A_KN, A_R, A_KQT, A_GRAM = 1, 3, 4, 6, 11, 19, 27, 28, 29, 33
        B_COPY, B_PBD, B_INV, B_TC, B_TBD, B_APPLY, B_CKN = 1, 4, 1, 32, 33, (34, 37, 40, 43), 31
        C_POST = (17, 33)
        SLOTS = B_APPLY[-1] + 3
        BK_O, BK_P, BK_B, BK_A = 4, 5, 6, 7

        def spread(act, ring, src, count):
            for q in range(Q):
                r = slice(C * q, C * q + C)
                ins = act.copy(ring[r, :, :, r], src[r])
            ins.then_inc(count, 1)

        N_W = 18

        @block.sync
        def _(sp):
            sp.dma_start(x[:, 0:BPB, :], x_v[0]).then_inc(s("x_in"), 16)
            kw = HEADS * DK
            vw = HEADS * DV
            loads = [
                (conv_w[:, :], ap["conv_w"]),
                (w_all[:, 0:kw], ap["Wk"]), (w_all[:, kw:2 * kw], ap["Wq"]),
                (w_all[:, V0:V0 + vw], ap["Wv"]), (w_all[:, G0:G0 + vw], ap["Wg"]),
                (w_all[:, B0:NPROJ], ap["Wb"]), (wo[:, :], ap["Wo"]),
                (normw[:, :], ap["norm_w"].partition_broadcast(P)),
                (w_rkv[:, :], ap["W_rkv"]), (b_rkv[:, :], ap["b_rkv"].rearrange("(t p) -> p t", p=P)),
                (w_o[:, :], ap["W_o"]), (bo_row[0:1, :], ap["b_o"].rearrange("(a n) -> a n", a=1)),
                (nu_col[:, :], ap["nu_log"].rearrange("(p a) -> p a", a=1)),
                (ga_col[:, :], ap["gamma_log"].rearrange("(p a) -> p a", a=1)),
                (router[0:E, :], ap["router_w"]),
                (bfc_rows[0:E * HC, :], ap["b_fc"].rearrange("e (c p) -> (e c) p", p=P)),
                (b_pr2[0:E, :], ap["b_proj"]), (b_pr2[E:2 * E, :], ap["b_proj"]),
            ]
            assert len(loads) == N_W
            with nc.allow_non_contiguous_dma(reason="a few hundred 4-byte elements, once"):
                for dst, src in loads:
                    sp.dma_start(dst, src).then_inc(s("w_in"), 16)
            sp.wait_ge(s("x_in"), 16)
            for b in range(1, B):
                sp.dma_start(x[:, b * BPB:(b + 1) * BPB, :], x_v[b]).then_inc(s("x_in"), 16)
                sp.wait_ge(s("x_in"), 16 * (b + 1))
            if phases >= 2:
                sp.wait_ge(s("phase_done"), 1)
                for e in range(E):
                    sp.dma_start(w_fc[:, e, :], ap["w_fc"][e]).then_inc(s("fc_in"), 16)
                    sp.dma_start(w_pr[:, e * HC:(e + 1) * HC, :], ap["w_proj"][e].rearrange("(c p) n -> p c n", p=P))\
                        .then_inc(s("pr_in"), 16)
                    sp.wait_ge(s("fc_in"), 16 * e + 16)
                    sp.wait_ge(s("pr_in"), 16 * e + 16)
            if phases >= 4:
                with sp.Fori(0, NG) as g:
                    sp.wait_ge(s("moe1_x"), g + 1)
                    sp.dma_start(out_v[:, bass.ds(g * GB, GB), :], x[:, bass.ds(g * GB, GB), :]).then_inc(s("stored"), 16)
            else:
                sp.wait_ge(s("phase_done"), phases)
                with sp.Fori(0, NG) as g:
                    sp.dma_start(out_v[:, bass.ds(g * GB, GB), :], x[:, bass.ds(g * GB, GB), :]).then_inc(s("stored"), 16)
            sp.wait_ge(s("stored"), 16 * NG)

        @block.gpsimd
        def _(pool):
            ch = Chain(pool, s("pool_chain"))
            pool.memset(ident[:, :], 0.0)
            pool.memset(neg_half[:, :], -0.5)
            pool.memset(e_col[:, :], E_CONST)
            pool.memset(ones_row[:, :], 1.0)
            pool.memset(yT[:, 0:3], 0.0)
            pool.memset(kn[:, :, :, :], 0.0)
            pool.memset(qn[:, :, :, :], 0.0)
            for v in (A, S, qpT):
                pool.memset(v[:, :, :], 0.0)
            pool.memset(t_p[:, :, :], 0.0)
            pool.memset(m_p[:, :], 1.0)
            for v in (t_bd, p_bd):
                pool.memset(v[:, :, :, :], 0.0)
            ch.link(pool.memset(bd[:, :], 1.0))
            pool.affine_select(out=ident[:, :], in_=ident[:, :], compare_op=ALU.not_equal, fill=1.0,
                               base=0, pattern=[[-1, P]], channel_multiplier=1)
            t_diag = t_p[:, :, :]
            pool.affine_select(out=t_diag, in_=t_diag, compare_op=ALU.not_equal, fill=1.0,
                               base=0, pattern=[[1, C], [-1, C]], channel_multiplier=0)
            pool.iota(iota8[:, :], pattern=[[1, E]], base=0, channel_multiplier=0,
                      allow_small_or_imprecise_dtypes=True)
            by_head = bd[:, :].rearrange("p (h d) -> p h d", h=HEADS)
            ch.link(pool.affine_select(out=by_head, in_=by_head, compare_op=ALU.is_ge, fill=0.0,
                                       base=0, pattern=[[-DK, HEADS], [0, DV]], channel_multiplier=1))
            ch.link(pool.affine_select(out=by_head, in_=by_head, compare_op=ALU.is_ge, fill=0.0,
                                       base=DK - 1, pattern=[[DK, HEADS], [0, DV]], channel_multiplier=-1))
            for q in range(Q):
                r = slice(C * q, C * q + C)
                ins = pool.affine_select(out=m_p[r, :], in_=m_p[r, :], compare_op=ALU.is_ge, fill=0.0,
                                         base=0, pattern=[[1, C]], channel_multiplier=-1)
            ch.link(ins)
            ch.eng.sem_inc(s("consts"), 1)

            pool.wait_ge(s("w_in"), 16 * N_W)
            pool.tensor_tensor(lam[:, 2:3], e_col[:, :], nu_col[:, :], ALU.pow)
            ch.link(pool.tensor_tensor(lam[:, 1:2], nu_col[:, :], ga_col[:, :], ALU.add))
            ch.link(pool.tensor_scalar(lam[:, 2:3], lam[:, 2:3], -1.0, None, ALU.mult))
            ch.link(pool.tensor_tensor(lam[:, 1:2], e_col[:, :], lam[:, 1:2], ALU.pow))
            pool.tensor_scalar(lam[:, 1:2], lam[:, 1:2], -1.0, None, ALU.add)
            pool.tensor_tensor(lam[:, 0:1], e_col[:, :], lam[:, 2:3], ALU.pow)
            pool.tensor_scalar(half_br[:, :], b_rkv[:, 0:1], 0.5, None, ALU.mult).then_inc(s("lam_ready"), 1)

            def carry_wait(k, done, count):
                pool.wait_ge(done, count)
                pool.tensor_tensor(pool_unused[:, k:k + 1], e_col[:, :], e_col[:, :], ALU.mult)

            def stage_a(b, t):
                if t == A_RSTD:
                    pool.wait_ge(s("d_var"), b + 1)
                    pool.tensor_tensor(rstd[:, :], rstd[:, :], neg_half[:, 0:BPB], ALU.pow).then_inc(s("d_rstd"), 1)
                if t == A_NORM + 3:
                    pool.wait_ge(s("d_ss"), b + 1)
                    pool.tensor_tensor(rn[:, :, :], ss[:, :, :],
                                       neg_half[:, 0:2 * HEADS * BPB].rearrange("p (n h) -> p n h", n=BPB),
                                       ALU.pow).then_inc(s("d_rn"), 1)

            def stage_b(b, t):
                if t == 0:
                    pool.wait_ge(s("d_kqv"), (b + 1) * BPB)
                    pool.wait_ge(s("d_cgs"), b)
                    carry_wait(0, s("d_mgs"), b)
                    pool.tensor_copy(m_gs[:, :, :], gs[:, :, :]).then_inc(s("d_mgs"), 1)
                if t == B_COPY:
                    pool.wait_ge(s("d_kn"), 2 * (b + 1))
                    pool.wait_ge(s("d_ckn"), b)
                    pool.wait_ge(s("d_qp"), b * NPAIR)
                    carry_wait(3, s("d_bkq"), b)
                    pool.tensor_copy(b_kn[:, :, :].rearrange("p n (h d) -> p n h d", h=HEADS), kn[:, :, :, 0:DK])
                    pool.tensor_copy(b_qn[:, :, :].rearrange("p n (h d) -> p n h d", h=HEADS), qn[:, :, :, 0:DK])\
                        .then_inc(s("d_bkq"), 1)
                if t == B_CKN:
                    pool.wait_ge(s("d_bkq"), b + 1)
                    pool.wait_ge(s("d_prep"), b * NCH)
                    carry_wait(1, s("d_ckn"), b)
                    pool.tensor_copy(c_kn[:, :, :], b_kn[:, :, :])\
                        .then_inc(s("d_ckn"), 1)

            def stage_c(b, t):
                if t == 0:
                    pool.wait_ge(s("d_mgs"), b + 1)
                    pool.wait_ge(s("d_og"), b * GPB)
                    carry_wait(2, s("d_cgs"), b)
                    pool.tensor_copy(c_gs[:, :, :], m_gs[:, :, :]).then_inc(s("d_cgs"), 1)
                for half, t0 in enumerate(C_POST):
                    if t == t0 + 2:
                        pool.wait_ge(s("d_oss"), b * GPB + half + 1)
                        pool.tensor_tensor(ro[:, half], ro[:, half], neg_half[:, 0:GB * HEADS], ALU.pow)\
                            .then_inc(s("d_ro"), 1)

            for t in range(SLOTS):
                stage_a(0, t)
            for t in range(SLOTS):
                stage_b(0, t)
                stage_a(1, t)
            with pool.Fori(0, B - 2) as i:
                for t in range(SLOTS):
                    stage_c(i, t)
                    stage_b(i + 1, t)
                    stage_a(i + 2, t)
            for t in range(SLOTS):
                stage_c(B - 2, t)
                stage_b(B - 1, t)
            for t in range(SLOTS):
                stage_c(B - 1, t)

            def moe_pool(m):
                with pool.Fori(0, NG) as g:
                    pool.wait_ge(s(f"moe{m}_var"), g + 1)
                    pool.tensor_tensor(rstd[:, 0:GB], rstd[:, 0:GB], neg_half[:, 0:GB], ALU.pow)\
                        .then_inc(s(f"moe{m}_rstd"), 1)

            if phases >= 2:
                moe_pool(0)
            if phases >= 3:
                pool.wait_ge(s("phase_done"), 2)
                pool.memset(l_const[:, 1:2], 0.5)
                pool.memset(l_const[:, 0:1], 1e-6).then_inc(s("l_consts"), 1)
                with pool.Fori(0, B) as b:
                    pool.wait_ge(s("l_var"), b + 1)
                    pool.tensor_tensor(rstd[:, :], rstd[:, :], neg_half[:, 0:BPB], ALU.pow).then_inc(s("l_rstd"), 1)
            if phases >= 4:
                moe_pool(1)

        @block.vector
        def _(ve):
            ch = Chain(ve, s("ve_chain"))

            def carry_wait():
                ve.memset(unused[:, :], 0.0)

            def variances(n0, nb, var_sem):
                for j in range(nb):
                    ins = ve.bn_stats(stats[:, j, :], x[:, bass.ds(n0 + j, 1), :].rearrange("p a c -> p (a c)"))
                ch.link(ins)
                carry_wait()
                for j in range(nb):
                    ins = ve.bn_aggr(mv[:, j, :], stats[:, j, :])
                ch.link(ins)
                ve.tensor_scalar(rstd[:, 0:nb], mv[:, 0:nb, 1], LN_EPS, None, ALU.add).then_inc(s(var_sem), 1)

            def normalise(n0, nb, rstd_sem, rstd_at, y_sem):
                ve.wait_ge(s(rstd_sem), rstd_at)
                for j in range(nb):
                    ve.tensor_scalar(y[:, j, :], x[:, bass.ds(n0 + j, 1), :].rearrange("p a c -> p (a c)"),
                                     mv[:, j, 0:1], rstd[:, j:j + 1], ALU.subtract, ALU.mult).then_inc(s(y_sem), 1)

            ve.wait_ge(s("consts"), 1)
            ve.wait_ge(s("w_in"), 16 * N_W)

            LINKS_A, LINKS_B, LINKS_C = 2 + 2 * 3 + 2 + 1, 1 + 2 * (C - 1), 2 * 4
            marks = {}

            def stage_a(b, t):
                if t == 0:
                    ve.wait_ge(s("x_in"), 16 * b + 16)
                    variances(b * BPB, BPB, "d_var")
                if t == A_Y:
                    normalise(b * BPB, BPB, "d_rstd", b + 1, "d_y")
                half, k = divmod(t - A_CONV, 4)
                if 0 <= half < GPB:
                    cv = hT[:, half * GT:(half + 1) * GT]
                    src = yT[:, half * GT + k:half * GT + k + GT]
                    if k == 0:
                        ve.wait_ge(s("d_yT"), b * GPB + GPB)
                        marks["conv"] = ch.mark(ve.tensor_scalar(cv, src, conv_w[:, 0:1], None, ALU.mult))
                    else:
                        ch.wait(marks["conv"])
                        ins = ve.scalar_tensor_tensor(cv, src, conv_w[:, k:k + 1], cv, ALU.mult, ALU.add)
                        if k < 3:
                            marks["conv"] = ch.mark(ins)
                        else:
                            ins.then_inc(s("d_conv"), 1)
                if t == A_NORM:
                    ve.wait_ge(s("d_kqv"), (b + 1) * BPB)
                    marks["sq"] = ch.mark(ve.tensor_tensor(sq, kqv[:, :, 0:KQ], kqv[:, :, 0:KQ], ALU.mult))
                if t == A_NORM + 1:
                    ch.wait(marks["sq"])
                    marks["ss"] = ch.mark(ve.tensor_reduce(ss[:, :, :], sq.rearrange("p n (h d) -> p n h d", d=DK),
                                                           AXX, ALU.add))
                if t == A_NORM + 2:
                    ch.wait(marks["ss"])
                    ve.tensor_scalar(ss[:, :, :], ss[:, :, :], NORM_MIN_SQ, None, ALU.max).then_inc(s("d_ss"), 1)
                if t == A_KN:
                    ve.wait_ge(s("d_rn"), b + 1)
                    ve.wait_ge(s("d_bkq"), b)
                    for dst, c0, h0 in ((kn, 0, 0), (qn, HEADS * DK, HEADS)):
                        ve.tensor_tensor(dst[:, :, :, 0:DK],
                                         kqv[:, :, c0:c0 + HEADS * DK].rearrange("p n (h d) -> p n h d", d=DK),
                                         bc(rn[:, :, h0:h0 + HEADS], 3, DK), ALU.mult).then_inc(s("d_kn"), 1)
                if t == A_R:
                    ve.tensor_scalar(beta[:, :, :], th[:, :, :], 0.5, 0.5, ALU.mult, ALU.add)
                    ch.link(ve.tensor_scalar(nbeta[:, :, :], th[:, :, :], -0.5, -0.5, ALU.mult, ALU.add))
                    ve.wait_ge(s("d_bR"), b)
                    ve.tensor_tensor(R[:, :, :, 0:DV],
                                     kqv[:, :, V0:V0 + HEADS * DV].rearrange("p n (h d) -> p n h d", d=DV),
                                     bc(beta[:, :, :], 3, DV), ALU.mult)
                    ve.wait_ge(s("d_kn"), 2 * b + 2)
                    ve.tensor_tensor(R[:, :, :, DV:RH], kn[:, :, :, 0:DK], bc(beta[:, :, :], 3, DK),
                                     ALU.mult).then_inc(s("d_R"), 1)
                n = t - A_GRAM
                if 0 <= n < BPB:
                    ve.wait_ge(s("d_gram"), b * BPB + n + 1)
                    ve.tensor_tensor(n_c[:, n], ps[:, 0:HEADS, 0:C], bc(nbeta[:, n, :], 2, C), ALU.mult)
                    if n == 0:
                        ve.wait_ge(s("d_pbd"), 2 * b)
                    ve.tensor_tensor(gp[:, n], ps[:, 0:HEADS, C:2 * C], bc(m_p[:, :], 1, HEADS),
                                     ALU.mult).then_inc(s("d_gp"), 1)

            def row_of_inverse(b, t, step):
                i = t - B_INV + 1
                if t == 0 and step == 0:
                    ve.wait_ge(s("d_gp"), (b + 1) * BPB)
                    ve.wait_ge(s("d_tbd"), 2 * b)
                    marks["row"] = ch.mark(ve.transpose(n_p[:, :, :], n_c[:, :, :, :].rearrange("p n h j -> p j (n h)")))
                if 1 <= i < C and step == 0:
                    ch.wait(marks["row"])
                    if i < SUB:
                        ins = ve.tensor_tensor(prod[:, :, 0:i, 0:i], diagonal_blocks(t_p, i, "lm -> ml"),
                                               bc(diagonal_blocks(n_p, i, "row"), 2, i), ALU.mult)
                    else:
                        t_ml = t_p[:, 0:i, 0:SUB].rearrange("p l m -> p m l")
                        n_row = n_p[:, 0:i, i:i + 1].rearrange("p l a -> p a l").to_broadcast([P, SUB, i])
                        ins = ve.tensor_tensor(prod2[:, :, 0:i], t_ml, n_row, ALU.mult)
                    marks["prod"] = ch.mark(ins)
                if 1 <= i < C and step == 1:
                    ch.wait(marks["prod"])
                    if i < SUB:
                        ins = ve.tensor_reduce(diagonal_blocks(t_p, i, "row out"), prod[:, :, 0:i, 0:i], AXX, ALU.add)
                    else:
                        ins = ve.tensor_reduce(t_p[:, i, 0:SUB], prod2[:, :, 0:i], AXX, ALU.add)
                    marks["row"] = ch.mark(ins)

            def stage_b(b, t):
                if t == B_TC:
                    ch.wait(marks["row"])
                    ve.transpose(t_c.rearrange("p n h i -> p i (n h)"), t_p[:, :, :]).then_inc(s("d_inv"), 1)
                for p, t0 in enumerate(B_APPLY):
                    if t == t0 + 1:
                        pair = slice(2 * p, 2 * p + 2)
                        ve.wait_ge(s("d_puw"), b * NPAIR + p + 1)
                        ve.wait_ge(s("d_qT"), b * NPAIR + p)
                        ve.wait_ge(s("d_bkq"), b + 1)
                        ve.tensor_tensor(qp[:, :, :].rearrange("p n (h d) -> p n h d", h=HEADS), b_qn[:, pair, :].rearrange("p n (h d) -> p n h d", h=HEADS),
                                         puw[:, pair, :, DV:RH], ALU.subtract).then_inc(s("d_qp"), 1)

            def states(b, t):
                if t == 0:
                    ve.memset(S[0:KW, 0, :], 0.0).then_inc(s("d_S"), 1)
                c = t - 1
                if 0 <= c < NCH - 1:
                    if c == 0:
                        ve.wait_ge(s("d_prep"), b * NCH + 1)
                    else:
                        ve.wait_ge(s("d_step"), b * (NCH - 2) + c)
                    if c + 1 >= NS:
                        ve.wait_ge(s("d_qs"), b * BPB + (c + 1 - NS) // Q + 1)
                    ve.tensor_tensor(S[0:KW, (c + 1) % NS, :], ps[0:KW, c % Q, P:2 * P], bd[0:KW, :], ALU.mult)\
                        .then_inc(s("d_S"), 1)

            def stage_c(b, t):
                for c in range(Q) if t == 0 else [t + 2] if 2 <= t and t + 2 < NCH else []:
                    ve.wait_ge(s("d_prep"), b * NCH + c + 1)
                    ve.tensor_tensor(A[0:KW, c % NS, :], ident[0:KW, 0:KW], ps[0:KW, c % Q, 0:KW], ALU.subtract)\
                        .then_inc(s("d_A"), 1)
                n, k = divmod(t - Q, Q)
                if 0 <= n < BPB and k == 0:
                    ve.wait_ge(s("d_qs"), b * BPB + n + 1)
                    ve.wait_ge(s("d_oT"), b * GPB)
                    ve.tensor_tensor(o[:, n, :].rearrange("p (h d) -> p h d", h=HEADS), puw[:, n, :, 0:DV],
                                     ps[:, BK_O, 0:P].rearrange("p (h d) -> p h d", h=HEADS), ALU.add)\
                        .then_inc(s("d_o"), 1)
                for half, t0 in enumerate(C_POST):
                    blocks = slice(half * GB, (half + 1) * GB)
                    if t == t0:
                        ve.wait_ge(s("d_o"), b * BPB + (half + 1) * GB)
                        marks["osq"] = ch.mark(ve.tensor_tensor(osq[:, :, :], o[:, blocks, :], o[:, blocks, :], ALU.mult))
                    if t == t0 + 1:
                        ch.wait(marks["osq"])
                        ch.link(ve.tensor_reduce(ro[:, half], osq[:, :, :].rearrange("p n (h d) -> p (n h) d", d=DV),
                                                 AXX, ALU.add))
                        ve.tensor_scalar(ro[:, half], ro[:, half], 1.0 / DV, RMS_EPS, ALU.mult, ALU.add)\
                            .then_inc(s("d_oss"), 1)
                    gs4 = c_gs[:, blocks, :].rearrange("p n (h d) -> p (n h) d", d=DV)
                    if t == t0 + 2:
                        ve.wait_ge(s("d_cgs"), b + 1)
                        marks["gs"] = ch.mark(ve.tensor_tensor(gs4, gs4, bc(normw[:, :], 1, GB * HEADS), ALU.mult))
                    if t == t0 + 3:
                        ch.wait(marks["gs"])
                        marks["gs"] = ch.mark(ve.tensor_tensor(c_gs[:, blocks, :], c_gs[:, blocks, :], o[:, blocks, :],
                                                               ALU.mult))
                    if t == t0 + 5:
                        ch.wait(marks["gs"])
                        ve.wait_ge(s("d_ro"), b * GPB + half + 1)
                        ve.tensor_tensor(o[:, blocks, :].rearrange("p n (h d) -> p (n h) d", d=DV), gs4,
                                         bc(ro[:, half], 2, DV), ALU.mult).then_inc(s("d_og"), 1)
                    if t == t0 + 8:
                        ve.wait_ge(s("d_out"), b * GPB + half + 1)
                        xg = x[:, bass.ds(b * BPB + half * GB, GB), :]
                        ve.tensor_tensor(xg, xg, ps[:, BK_P, :].rearrange("p (n c) -> p n c", n=GB), ALU.add)\
                            .then_inc(s("d_x"), 1)

            for t in range(SLOTS):
                stage_a(0, t)
            for t in range(SLOTS):
                row_of_inverse(0, t, 0)
                row_of_inverse(0, t, 1)
                stage_b(0, t)
                stage_a(1, t)
            with ve.Fori(0, B - 2) as i:
                ch.enter(i, LINKS_C + LINKS_B + LINKS_A)
                for t in range(SLOTS):
                    row_of_inverse(i + 1, t, 0)
                    states(i, t)
                    row_of_inverse(i + 1, t, 1)
                    stage_c(i, t)
                    stage_b(i + 1, t)
                    stage_a(i + 2, t)
                ch.leave(B - 2)
            for t in range(SLOTS):
                row_of_inverse(B - 1, t, 0)
                states(B - 2, t)
                row_of_inverse(B - 1, t, 1)
                stage_c(B - 2, t)
                stage_b(B - 1, t)
            for t in range(SLOTS):
                states(B - 1, t)
                stage_c(B - 1, t)

            ve.wait_ge(s("d_x"), GPB * B)
            ve.sem_inc(s("phase_done"), 1)

            def split_weights():
                ch.link(ve.tensor_tensor(sel_col[0:2 * E, :], ident[0:2 * E, 0:E], ident[0:2 * E, E:2 * E], ALU.add))
                ve.tensor_copy(sel[0:2 * E, :, :], bc(sel_col[0:2 * E, :], 2, P))
                for e in range(E):
                    ve.wait_ge(s("w_hi"), 2 * e + 1)
                    ve.tensor_tensor(wfl[:, e, :], w_fc[:, e, :], wfh[:, e, :].bitcast(F32), ALU.subtract)\
                        .then_inc(s("split"), 1)
                    k = slice(e * HC, (e + 1) * HC)
                    ve.wait_ge(s("w_hi"), 2 * e + 2)
                    ve.tensor_tensor(wpl[:, k, :], w_pr[:, k, :], wph[:, k, :].bitcast(F32), ALU.subtract)\
                        .then_inc(s("split"), 1)

            def moe_vector(m):
                def sm(name):
                    return s(f"moe{m}_{name}")

                def route(g):
                    ve.wait_ge(sm("lg"), g + 1)
                    ch.link(ve.tensor_copy(lg[:, :, :], ps[:, 1, 0:GB * E].rearrange("p (n e) -> p n e", n=GB)))
                    carry_wait()
                    for j in range(GB):
                        ins = ve.max(top[:, j, :], lg[:, j, :])
                    ch.link(ins)
                    carry_wait()
                    for j in range(GB):
                        ins = ve.max_index(idx[:, j, :], top[:, j, :], lg[:, j, :])
                    ch.link(ve.tensor_tensor(dlt[:, :], top[:, :, 1], top[:, :, 0], ALU.subtract))
                    ve.sem_inc(sm("dlt"), 1)
                    ch.link(ve.tensor_copy(idxf[:, :, 0:2], idx[:, :, 0:2]))
                    for k in range(2):
                        ins = ve.tensor_tensor(oh[:, k], bc(iota8[:, :], 1, GB), bc(idxf[:, :, k], 2, E), ALU.is_equal)
                    ch.link(ins)

                def combine(g):
                    ve.wait_ge(sm("tanh"), g + 1)
                    ve.tensor_scalar(w12[:, 0, :], tnh[:, :], -0.5, 0.5, ALU.mult, ALU.add)
                    ch.link(ve.tensor_scalar(w12[:, 1, :], tnh[:, :], 0.5, 0.5, ALU.mult, ALU.add))
                    for k in range(2):
                        ins = ve.tensor_tensor(oh[:, k], oh[:, k], bc(w12[:, k, :], 2, E), ALU.mult)
                    ch.link(ins)
                    ch.link(ve.tensor_tensor(comb[:, :, :], oh[:, 0], oh[:, 1], ALU.add))
                    ch.link(ve.tensor_copy(comb2[:, :, 0:E], comb[:, :, :]))
                    ve.tensor_tensor(comb2[:, :, E:2 * E], comb[:, :, :], comb2[:, :, 0:E].bitcast(F32), ALU.subtract)\
                        .then_inc(sm("comb"), 1)

                LINKS_ROUTE, LINKS_LN, LINKS_HID = 9, 2, E

                def tokens_low(g, p):
                    ve.wait_ge(sm("yh"), g + 1)
                    ve.tensor_tensor(yTl[:, p, :], yTf[:, :], yTh[:, p, :].bitcast(F32), ALU.subtract).then_inc(sm("yl"), 1)

                def hidden_low(g, e, c):
                    ve.wait_ge(sm("hid"), g * E * HC + e * HC + c + 1 + HC)
                    ve.wait_ge(sm("pr"), g * E + e + 1)
                    if c == HC - 1:
                        ch.link(ve.tensor_copy(hidh[:, e % 2, c, :], hidf[:, c, :]))
                    ve.tensor_tensor(hidl[:, e % 2, c, :], hidf[:, c, :], hidh[:, e % 2, c, :].bitcast(F32),
                                     ALU.subtract).then_inc(sm("lo"), 1)

                def weigh(g, e):
                    ve.wait_ge(sm("pr"), g * E + e + 3)
                    ve.wait_ge(sm("wb"), g * E + e + 1)
                    if e == 0:
                        ve.wait_ge(sm("flush"), g)
                    else:
                        ve.wait_ge(sm("acc"), g * (E - 1) + max(e - 1, 0))
                    ve.tensor_tensor(acc[:, :] if e == 0 else scaled[:, :], ps[:, 6, :], wb[:, e % 2, :], ALU.mult)\
                        .then_inc(sm("mul"), 1)

                def gather(g, e):
                    ve.wait_ge(sm("mul"), g * E + e + 1)
                    ve.wait_ge(sm("acc"), g * (E - 1) + e - 1)
                    ve.tensor_tensor(acc[:, :], acc[:, :], scaled[:, :], ALU.add).then_inc(sm("acc"), 1)

                def residual(g):
                    ve.wait_ge(sm("flush"), g + 1)
                    xg = x[:, bass.ds(g * GB, GB), :]
                    ve.tensor_tensor(xg, xg, ps[:, 0, :].rearrange("p (n c) -> p n c", n=GB), ALU.add)\
                        .then_inc(sm("x"), 1)

                def group(g, p, first=False, last=False):
                    if first:
                        for c in range(HC):
                            hidden_low(g, 0, c)
                    for e in range(E):
                        step = (g, e + 1) if e + 1 < E else (g + 1, 0)
                        ahead = e + 1 < E or not last
                        if ahead:
                            hidden_low(*step, 0)
                        if e == 0 and not first:
                            gather(g - 1, E - 1)
                        if e >= 2:
                            gather(g, e - 1)
                        if ahead:
                            for c in range(1, HC):
                                hidden_low(*step, c)
                        weigh(g, e)
                        if e == 0 and not first:
                            residual(g - 1)
                        if last:
                            continue
                        if e == 0:
                            variances((g + 1) * GB, GB, f"moe{m}_var")
                        if e == 1:
                            normalise((g + 1) * GB, GB, f"moe{m}_rstd", g + 2, f"moe{m}_y")
                        if e == 3:
                            route(g + 1)
                        if e == 4:
                            tokens_low(g + 1, 1 - p)
                        if e == 5:
                            combine(g + 1)
                    if last:
                        gather(g, E - 1)

                variances(0, GB, f"moe{m}_var")
                normalise(0, GB, f"moe{m}_rstd", 1, f"moe{m}_y")
                if m == 0:
                    split_weights()
                tokens_low(0, 0)
                route(0)
                combine(0)
                group(0, 0, first=True)
                with ve.Fori(0, (NG - 2) // 2) as i:
                    ch.enter(i, 2 * (LINKS_ROUTE + LINKS_LN + LINKS_HID))
                    group(2 * i + 1, 1)
                    group(2 * i + 2, 0)
                    ch.leave((NG - 2) // 2)
                group(NG - 1, 1, last=True)
                residual(NG - 1)
                ve.wait_ge(sm("x"), NG)
                ve.sem_inc(s("phase_done"), 1)

            if phases >= 2:
                moe_vector(0)

            def linrec_vector():
                decay = lam[:, 0:1].to_broadcast([P, L])

                def residual(b):
                    for half in range(GPB):
                        ve.wait_ge(s("l_out"), b * GPB + half + 1)
                        xg = x[:, bass.ds(b * BPB + half * GB, GB), :]
                        ve.tensor_tensor(xg, xg, ps[:, half, :].rearrange("p (n c) -> p n c", n=GB), ALU.add)\
                            .then_inc(s("l_x"), 1)

                def batch(b, p, first=False, last=False):
                    for half in range(GPB):
                        ve.wait_ge(s("l_k"), b * GPB + half + 1)
                        hs = slice(half * GT, half * GT + GT)
                        ins = ve.scalar_tensor_tensor(l_kv[:, hs], ps[:, 4 + 3 * half, :], b_rkv[:, 2:3],
                                                      l_k[p][:, hs], ALU.add, ALU.mult)
                        ins.then_inc(s("l_kv"), 1)
                    ve.wait_ge(s("l_kv"), (b + 1) * GPB)
                    ch.mark(ve.tensor_tensor_scan(l_u1, decay, l_kv, 0.0, ALU.mult, ALU.add))
                    ch.mark(ve.tensor_tensor_scan(l_u2, decay, l_k[p], 0.0, ALU.mult, ALU.add))
                    if not first:
                        residual(b - 1)
                    if not last:
                        variances((b + 1) * BPB, BPB, "l_var")
                    ch.wait()
                    ve.scalar_tensor_tensor(l_u2, l_k[p], lam[:, 1:2], l_u2, ALU.mult, ALU.add)\
                        .then_inc(s("l_den"), 1)
                    ch.link(ve.scalar_tensor_tensor(l_u1, l_kv, lam[:, 1:2], l_u1, ALU.mult, ALU.add))
                    if not last:
                        normalise((b + 1) * BPB, BPB, "l_rstd", b + 2, "l_y")
                    ve.wait_ge(s("l_eps"), b + 1)
                    ch.link(ve.reciprocal(l_u2, l_u2))
                    ch.link(ve.tensor_tensor(l_u1, l_u1, l_u2, ALU.mult))
                    ve.wait_ge(s("l_r"), b + 1)
                    if not first:
                        ve.wait_ge(s("l_out"), b * GPB)
                    ve.tensor_tensor(l_x, l_u1, l_r[p], ALU.mult).then_inc(s("l_xT"), 1)

                LINKS = 2 + 2 + 1 + 2
                variances(0, BPB, "l_var")
                normalise(0, BPB, "l_rstd", 1, "l_y")
                batch(0, 0, first=True)
                with ve.Fori(0, (B - 2) // 2) as i:
                    ch.enter(i, 2 * LINKS)
                    batch(2 * i + 1, 1)
                    batch(2 * i + 2, 0)
                    ch.leave((B - 2) // 2)
                batch(B - 1, 1, last=True)
                residual(B - 1)
                ve.wait_ge(s("l_x"), GPB * (B + 1))
                ve.sem_inc(s("phase_done"), 1)

            if phases >= 3:
                linrec_vector()
            if phases >= 4:
                moe_vector(1)

        @block.scalar
        def _(act):
            act.wait_ge(s("setup_T"), 1)
            act.copy(routerT[:, :], ps[:, 0, 0:E])
            act.copy(bfcT[:, :], ps[:, 0, 128:128 + E * HC]).then_inc(s("setup_sb"), 1)

            def stage_a(b, t):
                for half in range(GPB):
                    if t == A_T + half:
                        act.wait_ge(s("d_T"), b * GPB + half + 1)
                        act.copy(yT[:, 3 + half * GT:3 + (half + 1) * GT], ps[:, BK_A, :]).then_inc(s("d_yT"), 1)
                    if t == A_CONV + 4 * half + 4:
                        act.wait_ge(s("d_conv"), b * GPB + half + 1)
                        h = hT[:, half * GT:(half + 1) * GT]
                        act.activation(h, h, ACT.Silu).then_inc(s("d_h"), 1)
                n = t - A_PROJ
                if 0 <= n < BPB:
                    act.wait_ge(s("d_proj"), b * BPB + n + 1)
                    if n == 0:
                        act.wait_ge(s("d_R"), b)
                        act.wait_ge(s("d_mgs"), b)
                    act.copy(kqv[:, n, :], ps[:, BK_A, 0:G0])
                    act.activation(th[:, n, :], ps[:, BK_A, B0:NPROJ], ACT.Tanh, scale=0.5)
                    act.activation(gs[:, n, :], ps[:, BK_A, G0:B0], ACT.Silu).then_inc(s("d_kqv"), 1)
                p = t - A_KQT
                if 0 <= p < NPAIR:
                    act.wait_ge(s("d_kqT"), b * NPAIR + p + 1)
                    act.copy(kqT[:, 2 * p:2 * p + 2], ps[:, BK_A, :].rearrange("p (n z t) -> p n z t", n=2, z=2))\
                        .then_inc(s("d_kqTs"), 1)

            def stage_b(b, t):
                if t == B_COPY:
                    act.wait_ge(s("d_R"), b + 1)
                    act.wait_ge(s("d_y1"), b * NPAIR)
                    act.copy(b_R[:, :, :, :], R[:, :, :, :]).then_inc(s("d_bR"), 1)
                for half in range(GPB):
                    blocks = slice(half * GB, (half + 1) * GB)
                    if t == B_PBD + half:
                        act.wait_ge(s("d_gp"), (b + 1) * BPB)
                        act.wait_ge(s("d_pp"), b * NPAIR)
                        spread(act, p_bd[:, blocks], gp[:, blocks], s("d_pbd"))
                    if t == B_TBD:
                        act.wait_ge(s("d_inv"), b + 1)
                        act.wait_ge(s("d_y1"), b * NPAIR)
                        spread(act, t_bd[:, blocks], t_c[:, blocks], s("d_tbd"))
                for p, t0 in enumerate(B_APPLY):
                    pair = slice(2 * p, 2 * p + 2)
                    b_ps = ps[:, BK_B, 0:2 * HEADS * RH].rearrange("p (n h d) -> p n h d", n=2, h=HEADS)
                    later = not (type(b) is int and b == 0)
                    if t == t0:
                        act.wait_ge(s("d_y1"), b * NPAIR + p + 1)
                        if later:
                            act.wait_ge(s("d_prep"), (b - 1) * NCH + 2 * Q * (p + 1))
                        act.copy(wk[:, pair, :].rearrange("p n (h d) -> p n h d", h=HEADS), b_ps[:, :, :, DV:RH])
                        act.copy(uw[:, pair], b_ps).then_inc(s("d_uw"), 1)
                    if t == t0 + 1:
                        act.wait_ge(s("d_pp"), b * NPAIR + p + 1)
                        if later:
                            act.wait_ge(s("d_o"), (b - 1) * BPB + 2 * (p + 1))
                        act.copy(puw[:, pair], b_ps).then_inc(s("d_puw"), 1)
                    if t == t0 + 2:
                        act.wait_ge(s("d_qT"), b * NPAIR + p + 1)
                        if later:
                            act.wait_ge(s("d_qs"), (b - 1) * BPB + 2 * (p + 1))
                        act.copy(qpT[0:KW, 2 * p, :], ps[0:KW, BK_B, 0:P])
                        act.copy(qpT[0:KW, 2 * p + 1, :], ps[KW:2 * KW, BK_B, 0:P]).then_inc(s("d_qTs"), 1)

            def stage_c(b, t):
                for half, t0 in enumerate(C_POST):
                    if t == t0 + 6:
                        act.wait_ge(s("d_oT"), b * GPB + half + 1)
                        act.copy(oT[:, :], ps[:, BK_P, :]).then_inc(s("d_oTs"), 1)

            for t in range(SLOTS):
                stage_a(0, t)
            for t in range(SLOTS):
                stage_b(0, t)
                stage_a(1, t)
            with act.Fori(0, B - 2) as i:
                for t in range(SLOTS):
                    stage_c(i, t)
                    stage_b(i + 1, t)
                    stage_a(i + 2, t)
            for t in range(SLOTS):
                stage_c(B - 2, t)
                stage_b(B - 1, t)
            for t in range(SLOTS):
                stage_c(B - 1, t)

            def moe_scalar(m):
                def sm(name):
                    return s(f"moe{m}_{name}")

                def tokens(g):
                    act.wait_ge(sm("T"), g + 1)
                    act.copy(yTf[:, :], ps[:, 0, :]).then_inc(sm("yf"), 1)

                def tokens_high(g, p):
                    act.wait_ge(sm("yf"), g + 1)
                    act.copy(yTh[:, p, :], yTf[:, :]).then_inc(sm("yh"), 1)

                def weights(g):
                    act.wait_ge(sm("cT"), g + 1)
                    act.copy(combT[0:2 * E, :], ps[0:2 * E, 1, :]).then_inc(sm("cTs"), 1)

                def order(g):
                    act.wait_ge(sm("dlt"), g + 1)
                    act.activation(tnh[:, :], dlt[:, :], ACT.Tanh, scale=0.5).then_inc(sm("tanh"), 1)

                def group(g, p, first=False, last=False):
                    for e in range(E):
                        for c in range(HC):
                            act.wait_ge(sm("fc"), g * E * HC + e * HC + c + 1)
                            act.wait_ge(sm("lo"), g * E * HC + e * HC + c + 1)
                            b_col = bfcT[:, e * HC + c:e * HC + c + 1]
                            ins = act.activation(hidf[:, c, :], ps[:, 2 + c, :], ACT.Gelu_apprx_tanh, bias=b_col)
                            if c < HC - 1:
                                act.wait_ge(sm("pr"), g * E + e + 1)
                                ins = act.activation(hidh[:, e % 2, c, :], ps[:, 2 + c, :], ACT.Gelu_apprx_tanh, bias=b_col)
                            ins.then_inc(sm("hid"), 1)
                            if e == 5 and c == 0 and not last:
                                order(g + 1)
                        act.wait_ge(sm("w"), g * E + e + 1)
                        if not (first and e == 0):
                            act.wait_ge(sm("mul"), g * E + e - 1)
                        act.copy(wb[:, e % 2, :], ps[:, 7, :]).then_inc(sm("wb"), 1)
                        if e == 2 and not last:
                            tokens(g + 1)
                        if e == 3 and not last:
                            tokens_high(g + 1, 1 - p)
                    if not last:
                        weights(g + 1)

                act.sem_inc(sm("hid"), HC)
                act.sem_inc(sm("lo"), HC)
                act.sem_inc(sm("pr"), 2)
                if m == 0:
                    for e in range(E):
                        act.wait_ge(s("fc_in"), 16 * e + 16)
                        act.copy(wfh[:, e, :], w_fc[:, e, :]).then_inc(s("w_hi"), 1)
                        k = slice(e * HC, (e + 1) * HC)
                        act.wait_ge(s("pr_in"), 16 * e + 16)
                        act.copy(wph[:, k, :], w_pr[:, k, :]).then_inc(s("w_hi"), 1)
                tokens(0)
                tokens_high(0, 0)
                order(0)
                weights(0)
                group(0, 0, first=True)
                with act.Fori(0, (NG - 2) // 2) as i:
                    group(2 * i + 1, 1)
                    group(2 * i + 2, 0)
                group(NG - 1, 1, last=True)

            if phases >= 2:
                act.wait_ge(s("phase_done"), 1)
                moe_scalar(0)
            def linrec_scalar():
                def batch(b, p):
                    for half in range(GPB):
                        act.wait_ge(s("l_T"), b * GPB + half + 1)
                        act.copy(l_yT[:, half * GT:(half + 1) * GT], ps[:, half, :]).then_inc(s("l_yT"), 1)
                    for half in range(GPB):
                        hs = slice(half * GT, half * GT + GT)
                        act.wait_ge(s("l_rkv"), b * GPB + half + 1)
                        if half == 0 and not (type(b) is int and b < 2):
                            act.wait_ge(s("l_xT"), b - 1)
                        act.activation(l_k[p][:, hs], ps[:, 3 + 3 * half, :], ACT.Exp, bias=b_rkv[:, 1:2]).then_inc(s("l_k"), 1)
                        act.activation(l_r[p][:, hs], ps[:, 2 + 3 * half, :], ACT.Tanh, bias=half_br[:, :], scale=0.5)\
                            .then_inc(s("l_t"), 1)
                    act.wait_ge(s("l_t"), (b + 1) * GPB)
                    act.activation(l_r[p], l_r[p], ACT.Identity, bias=l_const[:, 1:2], scale=0.5).then_inc(s("l_r"), 1)
                    act.wait_ge(s("l_den"), b + 1)
                    act.activation(l_u2, l_u2, ACT.Identity, bias=l_const[:, 0:1]).then_inc(s("l_eps"), 1)

                act.wait_ge(s("l_consts"), 1)
                batch(0, 0)
                with act.Fori(0, (B - 2) // 2) as i:
                    batch(2 * i + 1, 1)
                    batch(2 * i + 2, 0)
                batch(B - 1, 1)

            if phases >= 3:
                act.wait_ge(s("phase_done"), 2)
                linrec_scalar()
            if phases >= 4:
                moe_scalar(1)

        @block.tensor
        def _(pe):
            pe.wait_ge(s("consts"), 1)
            pe.wait_ge(s("w_in"), 16 * N_W)
            pe.transpose(ps[:, 0, 0:E], router[0:E, :], ident[0:E, 0:E])
            pe.transpose(ps[:, 0, 128:128 + E * HC], bfc_rows[0:E * HC, :], ident[0:E * HC, 0:E * HC])\
                .then_inc(s("setup_T"), 1)
            pe.wait_ge(s("setup_sb"), 1)

            def stage_a(b, t):
                half = t - A_T
                if 0 <= half < GPB:
                    for j in range(GB):
                        pe.wait_ge(s("d_y"), b * BPB + half * GB + j + 1)
                        if half == 1:
                            pe.wait_ge(s("d_yT"), b * GPB + 1)
                        ins = pe.transpose(ps[:, BK_A, j * P:(j + 1) * P], y[:, half * GB + j, :], ident[:, :])
                    ins.then_inc(s("d_T"), 1)
                n = t - A_PROJ
                if 0 <= n < BPB:
                    pe.wait_ge(s("d_h"), b * GPB + n // GB + 1)
                    pe.wait_ge(s("d_kqv"), b * BPB + n)
                    pe.matmul(ps[:, BK_A, 0:NPROJ], hT[:, n * P:(n + 1) * P], w_all[:, :],
                              start=True, stop=True).then_inc(s("d_proj"), 1)
                p = t - A_KQT
                if 0 <= p < NPAIR:
                    pe.wait_ge(s("d_kn"), 2 * b + 2)
                    pe.wait_ge(s("d_kqTs"), b * NPAIR + p)
                    for j in range(2):
                        for z, v in enumerate((kn, qn)):
                            ins = pe.transpose(ps[:, BK_A, (2 * j + z) * P:(2 * j + z + 1) * P],
                                               v[:, 2 * p + j].rearrange("p h d -> p (h d)"), ident[:, :])
                    ins.then_inc(s("d_kqT"), 1)
                n = t - A_GRAM
                if 0 <= n < BPB:
                    pe.wait_ge(s("d_kqTs"), (b + 1) * NPAIR)
                    pe.wait_ge(s("d_gp"), b * BPB + n)
                    for h in range(HEADS):
                        rows = slice(DKP * h, DKP * h + DKP)
                        for q in range(Q):
                            r = slice(C * q, C * q + C)
                            m = slice(0, 2 * C) if q == 0 and h == 0 else r
                            ins = pe.matmul(ps[m, h, 0:2 * C], kqT[rows, n, 0, m], kqT[rows, n, :, r],
                                            start=True, stop=True)
                    ins.then_inc(s("d_gram"), 1)

            def stage_b(b, t):
                for p, t0 in enumerate(B_APPLY):
                    def heads(mat, rhs, done):
                        for j in range(2):
                            for h in range(HEADS):
                                k = (j * HEADS + h) * RH
                                ins = pe.matmul(ps[:, BK_B, k:k + RH], mat[:, 2 * p + j, h, :], rhs[:, 2 * p + j, h, :],
                                                start=True, stop=True)
                        ins.then_inc(done, 1)

                    if t == t0:
                        pe.wait_ge(s("d_bR"), b + 1)
                        pe.wait_ge(s("d_tbd"), 2 * b + p // 2 + 1)
                        pe.wait_ge(s("d_qTs"), b * NPAIR + p)
                        heads(t_bd, b_R, s("d_y1"))
                    if t == t0 + 1:
                        pe.wait_ge(s("d_pbd"), 2 * b + p // 2 + 1)
                        pe.wait_ge(s("d_uw"), b * NPAIR + p + 1)
                        heads(p_bd, uw, s("d_pp"))
                    if t == t0 + 2:
                        pe.wait_ge(s("d_qp"), b * NPAIR + p + 1)
                        pe.transpose(ps[:, BK_B, 0:P], qp[:, :, :].rearrange("p n c -> p (n c)"), ident[:, :])\
                            .then_inc(s("d_qT"), 1)

            def stage_c(b, t):
                def prepare(c):
                    n, q = divmod(c, Q)
                    r = slice(C * q, C * q + C)
                    pe.matmul(ps[0:KW, q, 0:KW], wk[r, n, :], c_kn[r, n, :],
                              start=True, stop=True, skip_group_check=True)
                    pe.matmul(ps[0:KW, q, P:2 * P], c_kn[r, n, :], uw[r, n, :, 0:DV],
                              start=False, stop=True, skip_group_check=True).then_inc(s("d_prep"), 1)

                if t == 0:
                    pe.wait_ge(s("d_gp"), min(b + 2, B) * BPB if type(b) is int else (b + 2) * BPB)
                    pe.wait_ge(s("d_uw"), (b + 1) * NPAIR)
                    pe.wait_ge(s("d_qTs"), (b + 1) * NPAIR)
                    pe.wait_ge(s("d_ckn"), b + 1)
                    for c in range(Q):
                        prepare(c)
                c = t - 1
                if 1 <= c < NCH - 1:
                    pe.wait_ge(s("d_A"), b * NCH + c + 1)
                    pe.wait_ge(s("d_S"), b * NCH + c + 1)
                    pe.matmul(ps[0:KW, c % Q, P:2 * P], A[:, c % NS, :], S[:, c % NS, :],
                              start=False, stop=True, skip_group_check=True).then_inc(s("d_step"), 1)
                    if c + 3 < NCH:
                        prepare(c + 3)
                n, k = divmod(t - Q, Q)
                if 0 <= n < BPB and k == 0:
                    pe.wait_ge(s("d_S"), b * NCH + Q * n + Q)
                    pe.wait_ge(s("d_o"), b * BPB + n)
                    for q in range(Q):
                        r = slice(C * q, C * q + C)
                        ins = pe.matmul(ps[r, BK_O, 0:P], qpT[:, n, r], S[:, (Q * n + q) % NS, :],
                                        start=True, stop=True, skip_group_check=True)
                    ins.then_inc(s("d_qs"), 1)
                for half, t0 in enumerate(C_POST):
                    if t == t0 + 6:
                        pe.wait_ge(s("d_og"), b * GPB + half + 1)
                        pe.wait_ge(s("d_x"), b * GPB + half)
                        for j in range(GB):
                            ins = pe.transpose(ps[:, BK_P, j * P:(j + 1) * P], o[:, half * GB + j, :], ident[:, :])
                        ins.then_inc(s("d_oT"), 1)
                    if t == t0 + 7:
                        pe.wait_ge(s("d_oTs"), b * GPB + half + 1)
                        for j in range(GB):
                            ins = pe.matmul(ps[:, BK_P, j * P:(j + 1) * P], oT[:, j * P:(j + 1) * P], wo[:, :],
                                            start=True, stop=True)
                        ins.then_inc(s("d_out"), 1)

            for t in range(SLOTS):
                stage_a(0, t)
            for t in range(SLOTS):
                stage_b(0, t)
                stage_a(1, t)
            with pe.Fori(0, B - 2) as i:
                for t in range(SLOTS):
                    stage_c(i, t)
                    stage_b(i + 1, t)
                    stage_a(i + 2, t)
            for t in range(SLOTS):
                stage_c(B - 2, t)
                stage_b(B - 1, t)
            for t in range(SLOTS):
                stage_c(B - 1, t)

            def moe_tensor(m):
                def sm(name):
                    return s(f"moe{m}_{name}")

                def turn(g):
                    for j in range(GB):
                        pe.wait_ge(sm("y"), g * GB + j + 1)
                        ins = pe.transpose(ps[:, 0, j * P:(j + 1) * P], y[:, j, :], ident[:, :])
                    ins.then_inc(sm("T"), 1)

                def logits(g):
                    pe.wait_ge(sm("yf"), g + 1)
                    for j in range(GB):
                        ins = pe.matmul(ps[:, 1, j * E:(j + 1) * E], yTf[:, j * P:(j + 1) * P], routerT[:, :],
                                        start=True, stop=True)
                    ins.then_inc(sm("lg"), 1)

                def turn_weights(g):
                    pe.wait_ge(sm("comb"), g + 1)
                    for j in range(GB):
                        ins = pe.transpose(ps[0:2 * E, 1, j * P:(j + 1) * P], comb2[:, j, :].bitcast(F32), ident[:, :])
                    ins.then_inc(sm("cT"), 1)

                def up(g, e, p):
                    if e == 0:
                        pe.wait_ge(sm("yl"), g + 1)
                    if m == 0:
                        pe.wait_ge(s("split"), 2 * e + 1)
                    for c in range(HC):
                        pe.wait_ge(sm("hid"), g * E * HC + e * HC + c + 1)
                        cols = slice(c * P, (c + 1) * P)
                        pe.matmul(ps[:, 2 + c, :], wfh[:, e, cols], yTh[:, p, :], start=True, stop=False)
                        pe.matmul(ps[:, 2 + c, :], wfh[:, e, cols], yTl[:, p, :], start=False, stop=False)
                        pe.matmul(ps[:, 2 + c, :], wfl[:, e, cols], yTh[:, p, :], start=False, stop=True)\
                            .then_inc(sm("fc"), 1)

                def weight(g, e):
                    if e == 0:
                        pe.wait_ge(sm("cTs"), g + 1)
                    pe.wait_ge(sm("wb"), g * E + e)
                    pe.matmul(ps[:, 7, :], sel[0:2 * E, e, :], combT[0:2 * E, :], start=True, stop=True)\
                        .then_inc(sm("w"), 1)

                def down(g, e):
                    if m == 0:
                        pe.wait_ge(s("split"), 2 * e + 2)
                    pe.wait_ge(sm("mul"), g * E + e)
                    for c in range(HC):
                        pe.wait_ge(sm("lo"), g * E * HC + e * HC + c + 1 + HC)
                        k = e * HC + c
                        pe.matmul(ps[:, 6, :], wph[:, k, :], hidh[:, e % 2, c, :], start=(c == 0), stop=False)
                        pe.matmul(ps[:, 6, :], wph[:, k, :], hidl[:, e % 2, c, :], start=False, stop=False)
                        ins = pe.matmul(ps[:, 6, :], wpl[:, k, :], hidh[:, e % 2, c, :], start=False, stop=(c == HC - 1))
                    ins.then_inc(sm("pr"), 1)

                def bias(g, last):
                    if last:
                        pe.wait_ge(sm("x"), g)
                    else:
                        pe.wait_ge(sm("yf"), g + 2)
                    for j in range(GB):
                        pe.matmul(ps[:, 0, j * D:(j + 1) * D], combT[0:2 * E, j * P:(j + 1) * P].bitcast(F32),
                                  b_pr2[0:2 * E, :], start=(j == 0), stop=False, skip_group_check=True)

                def flush(g):
                    pe.wait_ge(sm("acc"), (g + 1) * (E - 1))
                    for j in range(GB):
                        ins = pe.matmul(ps[:, 0, j * D:(j + 1) * D], acc[:, j * P:(j + 1) * P], ident[:, :],
                                        start=False, stop=True, skip_group_check=True)
                    ins.then_inc(sm("flush"), 1)

                def group(g, p, first=False, last=False):
                    if first:
                        up(g, 0, p)
                    for e in range(E):
                        weight(g, e)
                        if e == E - 1:
                            bias(g, last)
                            if not last:
                                turn_weights(g + 1)
                                up(g + 1, 0, 1 - p)
                        else:
                            up(g, e + 1, p)
                        if e == 2 and not last:
                            if not first:
                                pe.wait_ge(sm("x"), g)
                            turn(g + 1)
                        if e == 3 and not last:
                            logits(g + 1)
                        down(g, e)
                        if e == 0 and not first:
                            flush(g - 1)
                    if last:
                        flush(g)

                turn(0)
                logits(0)
                turn_weights(0)
                group(0, 0, first=True)
                with pe.Fori(0, (NG - 2) // 2) as i:
                    group(2 * i + 1, 1)
                    group(2 * i + 2, 0)
                group(NG - 1, 1, last=True)

            if phases >= 2:
                moe_tensor(0)
            def linrec_tensor():
                def front(b):
                    for half in range(GPB):
                        if not (type(b) is int and b < 2):
                            pe.wait_ge(s("l_x"), (b - 1) * GPB + half + 1)
                        for j in range(GB):
                            pe.wait_ge(s("l_y"), b * BPB + half * GB + j + 1)
                            ins = pe.transpose(ps[:, half, j * P:(j + 1) * P], y[:, half * GB + j, :], ident[:, :])
                        ins.then_inc(s("l_T"), 1)
                    for half in range(GPB):
                        pe.wait_ge(s("l_yT"), b * GPB + half + 1)
                        if not (type(b) is int and b == 0):
                            pe.wait_ge(s("l_kv"), (b - 1) * GPB + half + 1)
                        for t in (1, 0, 2):
                            ins = pe.matmul(ps[:, 2 + 3 * half + t, :], w_rkv[:, t * D:(t + 1) * D],
                                            l_yT[:, half * GT:(half + 1) * GT], start=True, stop=True)
                        ins.then_inc(s("l_rkv"), 1)

                def project(b, ahead):
                    pe.wait_ge(s("l_xT"), b + 1)
                    for half in range(GPB):
                        if ahead:
                            pe.wait_ge(s("l_yT"), (b + 1) * GPB + half + 1)
                        for j in range(GB):
                            n = half * GB + j
                            cols = slice(j * D, (j + 1) * D)
                            pe.matmul(ps[:, half, cols], ones_row[0:1, :], bo_row[0:1, :], start=True, stop=False)
                            ins = pe.matmul(ps[:, half, cols], l_x[:, n * P:(n + 1) * P], w_o[:, :], start=False, stop=True)
                        ins.then_inc(s("l_out"), 1)

                pe.sem_inc(s("l_x"), GPB)
                front(0)
                with pe.Fori(0, B - 1) as b:
                    front(b + 1)
                    project(b, True)
                project(B - 1, False)

            if phases >= 3:
                linrec_tensor()
            if phases >= 4:
                moe_tensor(1)


_NAMES = {
    "hidden": "L0_attn_a_hidden_states", "conv_w": "L0_attn_a_conv_w", "Wq": "L0_attn_a_Wq",
    "Wk": "L0_attn_a_Wk", "Wv": "L0_attn_a_Wv", "Wb": "L0_attn_a_Wb", "Wg": "L0_attn_a_Wg",
    "norm_w": "L0_attn_a_norm_w", "Wo": "L0_attn_a_Wo", "W_rkv": "L0_attn_b_W_rkv",
    "b_rkv": "L0_attn_b_b_rkv", "W_o": "L0_attn_b_W_o", "b_o": "L0_attn_b_b_o",
    "nu_log": "L0_attn_b_nu_log", "gamma_log": "L0_attn_b_gamma_log", "router_w": "L0_ffn_router_w",
    "w_fc": "L0_ffn_w_fc", "b_fc": "L0_ffn_b_fc", "w_proj": "L0_ffn_w_proj", "b_proj": "L0_ffn_b_proj",
}
PHASES = 4


def kernel(**inputs):
    import numpy as np
    import concourse.bacc as bacc
    from concourse.bass_utils import run_bass_kernel_spmd

    nc = bacc.Bacc("TRN2", target_bir_lowering=False, num_devices=1)
    arrays, aps = {}, {}
    for short, name in _NAMES.items():
        a = np.ascontiguousarray(inputs[name])
        arrays[f"in_{short}"] = a
        aps[short] = nc.dram_tensor(f"in_{short}", a.shape, F32, kind="ExternalInput").ap()
    out = nc.dram_tensor("out_x", inputs[_NAMES["hidden"]].shape, F32, kind="ExternalOutput").ap()
    hybrid_kernel(nc, aps, out, PHASES)
    r = run_bass_kernel_spmd(nc, [arrays], core_ids=[0])
    return r.results[0]["out_x"]
```

```python
from contextlib import ExitStack

import concourse.bass as bass
from concourse import mybir

F32 = mybir.dt.float32
F32R = mybir.dt.float32r
U32 = mybir.dt.uint32
ALU = mybir.AluOpType
ACT = mybir.ActivationFunctionType
AXX = mybir.AxisListType.X

P = 128
D = 128
HEADS = 4
DK = 16
DKP = 32
DV = 32
RH = DV + DK
C = 32
Q = P // C
SUB = 16
LN_EPS = 1e-5
RMS_EPS = 1e-5
NORM_MIN_SQ = 1e-24
E_CONST = 2.718281828459045


def bc(ap, axis, n):
    v = ap.unsqueeze(axis)
    shape = list(v.shape)
    shape[axis] = n
    return v.to_broadcast(shape)


class Chain:

    def __init__(self, eng, sem):
        self.eng, self.sem, self.base, self.k = eng, sem, 0, 0

    def mark(self, ins):
        ins.then_inc(self.sem, 1)
        self.k += 1
        return self.k

    def link(self, ins):
        self.mark(ins)
        self.wait()

    def wait(self, k=None):
        self.eng.wait_ge(self.sem, self.base + (self.k if k is None else k))

    def enter(self, i, per):
        self.done, self.per, self.k = self.base + self.k, per, 0
        self.base = i * per + self.done

    def leave(self, n):
        assert self.k == self.per, f"{self.k} links in the body, {self.per} stated"
        self.base, self.k = self.done + n * self.per, 0


def hybrid_kernel(nc, ap, out, phases=4):
    B, L, _ = ap["hidden"].shape
    NB = B * L // P
    BPB = L // P
    E, _, HID = ap["w_fc"].shape
    HC = HID // P
    GB = 4
    GT = GB * P
    NG = NB // GB
    GPB = BPB // GB
    assert GPB == 2
    NPROJ = 2 * HEADS * DK + 2 * HEADS * DV + HEADS
    KW = HEADS * DK
    KQ, V0, G0, B0 = 2 * HEADS * DK, 2 * HEADS * DK, 2 * HEADS * DK + HEADS * DV, NPROJ - HEADS

    ctx = ExitStack()
    with ctx:
        delta_ctx = ExitStack()

        def sb(name, shape, dt=F32):
            return ctx.enter_context(nc.sbuf_tensor(name, [P] + shape, dt))

        def sb1(name, shape, dt=F32):
            return delta_ctx.enter_context(nc.sbuf_tensor(name, [P] + shape, dt))

        def sem(name):
            return ctx.enter_context(nc.semaphore(name))

        ps = ctx.enter_context(nc.psum_tensor("ps", [P, 8, 512], F32))

        x = sb("x", [NB, D])
        ident = sb("ident", [P])
        bd = sb("bd", [HEADS * DV])
        m_p = sb("m_p", [C])
        neg_half = sb("neg_half", [NB])
        e_col = sb("e_col", [1])
        iota8 = sb("iota8", [E])
        ones_row = sb("ones_row", [P])
        conv_w = sb("conv_w", [4])
        w_all = sb("w_all", [NPROJ])
        wo = sb("wo", [D])
        normw = sb("normw", [DV])
        w_rkv = sb("w_rkv", [3 * D])
        b_rkv = sb("b_rkv", [3])
        w_o = sb("w_o", [D])
        bo_row = sb("bo_row", [D])
        nu_col = sb("nu_col", [1])
        ga_col = sb("ga_col", [1])
        lam = sb("lam", [4])
        router = sb("router", [P])
        routerT = sb("routerT", [E])
        bfc_rows = sb("bfc_rows", [P])
        bfcT = sb("bfcT", [E * HC])
        b_pr2 = sb("b_pr2", [D])
        half_br = sb("half_br", [1])
        stats = sb("stats", [BPB, 6])
        mv = sb("mv", [BPB, 2])
        unused = sb("unused", [1])
        pool_unused = sb("pool_unused", [4])
        rstd = sb("rstd", [BPB])
        y = sb("y", [BPB, D])
        yT = sb1("yT", [3 + L])
        hT = sb1("hT", [L])
        kqv = sb1("kqv", [BPB, G0])
        gs = sb1("gs", [BPB, HEADS * DV])
        th = sb1("th", [BPB, HEADS])
        beta = sb1("beta", [BPB, HEADS])
        nbeta = sb1("nbeta", [BPB, HEADS])
        ss = sb1("ss", [BPB, 2 * HEADS])
        rn = sb1("rn", [BPB, 2 * HEADS])
        kn = sb1("kn", [BPB, HEADS, DKP])
        qn = sb1("qn", [BPB, HEADS, DKP])
        R = sb1("R", [BPB, HEADS, RH])
        kqT = sb1("kqT", [BPB, 2, P])
        gp = sb1("gp", [BPB, HEADS, C])
        n_c = sb1("n_c", [BPB, HEADS, C])
        sq = n_c[:, :, :, :].rearrange("p n h j -> p n (h j)")
        n_p = sb1("n_p", [C, C])
        t_p = sb1("t_p", [C, C])
        prod = sb1("prod", [2, SUB, SUB])
        prod2 = sb1("prod2", [SUB, C])
        t_c = n_p[:, :, :].rearrange("p (n h) i -> p n h i", h=HEADS)
        t_bd = sb1("t_bd", [BPB, HEADS, P])
        p_bd = sb1("p_bd", [BPB, HEADS, P])
        b_kn = sb1("b_kn", [BPB, KW])
        b_qn = sb1("b_qn", [BPB, KW])
        b_R = sb1("b_R", [BPB, HEADS, RH])
        qp = sb1("qp", [2, KW])
        m_gs = sb1("m_gs", [BPB, HEADS * DV])
        uw = sb1("uw", [BPB, HEADS, RH])
        wk = sb1("wk", [BPB, KW])
        puw = sb1("puw", [BPB, HEADS, RH])
        qpT = sb1("qpT", [BPB, P])
        c_kn = sb1("c_kn", [BPB, KW])
        c_gs = sb1("c_gs", [BPB, HEADS * DV])
        NS = 8
        A = sb1("A", [NS, KW])
        S = sb1("S", [NS, HEADS * DV])
        o = sb1("o", [BPB, HEADS * DV])
        osq = sb1("osq", [GB, P])
        ro = sb1("ro", [2, GB * HEADS])
        oT = sb1("oT", [GT])

        def diagonal_blocks(t, i, what):
            start, dims = {
                "lm -> ml": (0, [[1, i], [C, i]]),
                "row": (i, [[C, i]]),
                "row out": (C * i, [[1, i]]),
            }[what]
            return bass.AP(tensor=t[:, :, :].tensor, offset=t[:, :, :].offset + start,
                           ap=[list(t[:, :, :].ap[0]), [SUB * C + SUB, 2]] + dims)

        delta_ctx.close()
        w_fc = sb("w_fc", [E, HID])
        w_pr = sb("w_pr", [E * HC, D])
        wfh = sb("wfh", [E, HID], F32R)
        wfl = sb("wfl", [E, HID], F32R)
        wph = sb("wph", [E * HC, D], F32R)
        wpl = sb("wpl", [E * HC, D], F32R)
        yTf = sb("yTf", [GT])
        yTh = sb("yTh", [2, GT], F32R)
        yTl = sb("yTl", [2, GT], F32R)
        hidf = sb("hidf", [HC, GT])
        hidh = sb("hidh", [2, HC, GT], F32R)
        hidl = sb("hidl", [2, HC, GT], F32R)
        wb = sb("wb", [2, GT])
        scaled = sb("scaled", [GT])
        acc = sb("acc", [GT])
        lg = sb("lg", [GB, E])
        top = sb("top", [GB, 8])
        idx = sb("idx", [GB, 8], U32)
        idxf = sb("idxf", [GB, 8])
        dlt = sb("dlt", [GB])
        tnh = sb("tnh", [GB])
        w12 = sb("w12", [2, GB])
        oh = sb("oh", [2, GB, E])
        comb = sb("comb", [GB, E])
        comb2 = sb("comb2", [GB, 2 * E], F32R)
        combT = sb("combT", [GT], F32R)
        sel_col = sb("sel_col", [E])
        sel = sb("sel", [E, P], F32R)
        raw = [w[:, :, :].rearrange("p a c -> p (a c)")[:, k * L:(k + 1) * L] for w, n in
               ((w_fc, E * HID), (w_pr, E * HC * D), (hidf, HC * GT)) for k in range(n // L)]
        l_yT, l_kv, l_u1, l_u2, l_k0, l_k1, l_r0, l_r1, l_x = raw[:9]
        l_k, l_r = (l_k0, l_k1), (l_r0, l_r1)
        l_const = sb("l_const", [2])

        SEMS = {}

        def s(name):
            if name not in SEMS:
                SEMS[name] = sem(name)
            return SEMS[name]

        block = ctx.enter_context(nc.Block())

        out_v = out.rearrange("b (n p) c -> p (b n) c", p=P)
        x_v = ap["hidden"].rearrange("b (n p) c -> b p n c", p=P)

        NCH = BPB * Q
        NPAIR = BPB // 2
        L_VAR, L_RSTD, L_Y, L_T, L_CONV = 1, 2, 4, 9, 32
        A_PROJ, A_NORM, A_KN, A_R, A_KQT, A_GRAM = 0, 8, 20, 22, 26, 33
        B_COPY, B_PBD, B_INV, B_TC, B_TBD, B_CKN = 16, 20, 1, 32, 33, 31
        B_APPLY, C_APPLY = ((0, 35), (1, 38)), ((2, 9), (3, 12))
        C_NORMW, C_POST = (5, 24), (17, 33)
        SLOTS = C_POST[-1] + 9
        BK_O, BK_P, BK_B, BK_A = 4, 5, 6, 7

        def spread(act, ring, src, count):
            for q in range(Q):
                r = slice(C * q, C * q + C)
                ins = act.copy(ring[r, :, :, r], src[r])
            ins.then_inc(count, 1)

        N_W = 18

        @block.sync
        def _(sp):
            sp.dma_start(x[:, 0:BPB, :], x_v[0]).then_inc(s("x_in"), 16)
            kw = HEADS * DK
            vw = HEADS * DV
            loads = [
                (conv_w[:, :], ap["conv_w"]),
                (w_all[:, 0:kw], ap["Wk"]), (w_all[:, kw:2 * kw], ap["Wq"]),
                (w_all[:, V0:V0 + vw], ap["Wv"]), (w_all[:, G0:G0 + vw], ap["Wg"]),
                (w_all[:, B0:NPROJ], ap["Wb"]), (wo[:, :], ap["Wo"]),
                (normw[:, :], ap["norm_w"].partition_broadcast(P)),
            ]
            with nc.allow_non_contiguous_dma(reason="a few hundred 4-byte elements, once"):
                for dst, src in loads:
                    sp.dma_start(dst, src).then_inc(s("w_in"), 16)
            sp.wait_ge(s("x_in"), 16)
            for b in range(1, B):
                sp.dma_start(x[:, b * BPB:(b + 1) * BPB, :], x_v[b]).then_inc(s("x_in"), 16)
                sp.wait_ge(s("x_in"), 16 * (b + 1))
            if phases >= 2:
                sp.wait_ge(s("phase_done"), 1)
                for e in range(E):
                    sp.dma_start(w_fc[:, e, :], ap["w_fc"][e]).then_inc(s("fc_in"), 16)
                    sp.dma_start(w_pr[:, e * HC:(e + 1) * HC, :], ap["w_proj"][e].rearrange("(c p) n -> p c n", p=P))\
                        .then_inc(s("pr_in"), 16)
                    sp.wait_ge(s("fc_in"), 16 * e + 16)
                    sp.wait_ge(s("pr_in"), 16 * e + 16)
            if phases >= 4:
                with sp.Fori(0, NG) as g:
                    sp.wait_ge(s("moe1_x"), g + 1)
                    sp.dma_start(out_v[:, bass.ds(g * GB, GB), :], x[:, bass.ds(g * GB, GB), :]).then_inc(s("stored"), 16)
            else:
                sp.wait_ge(s("phase_done"), phases)
                with sp.Fori(0, NG) as g:
                    sp.dma_start(out_v[:, bass.ds(g * GB, GB), :], x[:, bass.ds(g * GB, GB), :]).then_inc(s("stored"), 16)
            sp.wait_ge(s("stored"), 16 * NG)

        @block.gpsimd
        def _(pool):
            ch = Chain(pool, s("pool_chain"))
            pool.memset(ident[:, :], 0.0)
            pool.memset(neg_half[:, :], -0.5)
            pool.memset(e_col[:, :], E_CONST)
            pool.memset(ones_row[:, :], 1.0)
            pool.memset(yT[:, 0:3], 0.0)
            pool.memset(t_p[:, :, :], 0.0)
            pool.memset(m_p[:, :], 1.0)
            ch.link(pool.memset(bd[:, :], 1.0))
            pool.affine_select(out=ident[:, :], in_=ident[:, :], compare_op=ALU.not_equal, fill=1.0,
                               base=0, pattern=[[-1, P]], channel_multiplier=1)
            t_diag = t_p[:, :, :]
            pool.affine_select(out=t_diag, in_=t_diag, compare_op=ALU.not_equal, fill=1.0,
                               base=0, pattern=[[1, C], [-1, C]], channel_multiplier=0)
            pool.iota(iota8[:, :], pattern=[[1, E]], base=0, channel_multiplier=0,
                      allow_small_or_imprecise_dtypes=True)
            by_head = bd[:, :].rearrange("p (h d) -> p h d", h=HEADS)
            ch.link(pool.affine_select(out=by_head, in_=by_head, compare_op=ALU.is_ge, fill=0.0,
                                       base=0, pattern=[[-DK, HEADS], [0, DV]], channel_multiplier=1))
            ch.link(pool.affine_select(out=by_head, in_=by_head, compare_op=ALU.is_ge, fill=0.0,
                                       base=DK - 1, pattern=[[DK, HEADS], [0, DV]], channel_multiplier=-1))
            for q in range(Q):
                r = slice(C * q, C * q + C)
                ins = pool.affine_select(out=m_p[r, :], in_=m_p[r, :], compare_op=ALU.is_ge, fill=0.0,
                                         base=0, pattern=[[1, C]], channel_multiplier=-1)
            ch.link(ins)
            ch.eng.sem_inc(s("consts"), 1)

            def carry_wait(k, done, count):
                pool.wait_ge(done, count)
                pool.tensor_tensor(pool_unused[:, k:k + 1], e_col[:, :], e_col[:, :], ALU.mult)

            def stage_l(b, t):
                if t == L_RSTD:
                    pool.wait_ge(s("d_var"), b + 1)
                    pool.tensor_tensor(rstd[:, :], rstd[:, :], neg_half[:, 0:BPB], ALU.pow).then_inc(s("d_rstd"), 1)

            def stage_a(b, t):
                if t == A_NORM + 5:
                    pool.wait_ge(s("d_ss"), b + 1)
                    pool.tensor_tensor(rn[:, :, :], ss[:, :, :],
                                       neg_half[:, 0:2 * HEADS * BPB].rearrange("p (n h) -> p n h", n=BPB),
                                       ALU.pow).then_inc(s("d_rn"), 1)

            def stage_b(b, t):
                if t == 0:
                    pool.wait_ge(s("d_kqv"), (b + 1) * BPB)
                    pool.wait_ge(s("d_cgs"), b)
                    carry_wait(0, s("d_mgs"), b)
                    pool.tensor_copy(m_gs[:, :, :], gs[:, :, :]).then_inc(s("d_mgs"), 1)
                if t == B_COPY:
                    pool.wait_ge(s("d_kn"), 2 * (b + 1))
                    pool.wait_ge(s("d_ckn"), b)
                    pool.wait_ge(s("d_qp"), b * NPAIR)
                    carry_wait(3, s("d_bkq"), b)
                    pool.tensor_copy(b_kn[:, :, :].rearrange("p n (h d) -> p n h d", h=HEADS), kn[:, :, :, 0:DK])
                    pool.tensor_copy(b_qn[:, :, :].rearrange("p n (h d) -> p n h d", h=HEADS), qn[:, :, :, 0:DK])\
                        .then_inc(s("d_bkq"), 1)
                if t == B_CKN:
                    pool.wait_ge(s("d_bkq"), b + 1)
                    pool.wait_ge(s("d_prep"), b * NCH)
                    carry_wait(1, s("d_ckn"), b)
                    pool.tensor_copy(c_kn[:, :, :], b_kn[:, :, :])\
                        .then_inc(s("d_ckn"), 1)

            def stage_c(b, t):
                if t == 0:
                    pool.wait_ge(s("d_mgs"), b + 1)
                    pool.wait_ge(s("d_og"), b * GPB)
                    carry_wait(2, s("d_cgs"), b)
                    pool.tensor_copy(c_gs[:, :, :], m_gs[:, :, :]).then_inc(s("d_cgs"), 1)
                for half, t0 in enumerate(C_POST):
                    if t == C_NORMW[half]:
                        gs4 = c_gs[:, half * GB:(half + 1) * GB, :].rearrange("p n (h d) -> p (n h) d", d=DV)
                        pool.wait_ge(s("d_cgs"), b + 1)
                        pool.tensor_tensor(gs4, gs4, bc(normw[:, :], 1, GB * HEADS), ALU.mult).then_inc(s("d_gw"), 1)
                    if t == t0 + 2:
                        pool.wait_ge(s("d_oss"), b * GPB + half + 1)
                        pool.tensor_tensor(ro[:, half], ro[:, half], neg_half[:, 0:GB * HEADS], ALU.pow)\
                            .then_inc(s("d_ro"), 1)

            for t in range(SLOTS):
                stage_l(0, t)

            for v in (t_bd, p_bd):
                ins = pool.memset(v[:, :, :, :], 0.0)
            ins.then_inc(s("zeros"), 1)

            pool.wait_ge(s("w_in"), 16 * N_W)
            pool.tensor_tensor(lam[:, 2:3], e_col[:, :], nu_col[:, :], ALU.pow)
            ch.link(pool.tensor_tensor(lam[:, 1:2], nu_col[:, :], ga_col[:, :], ALU.add))
            ch.link(pool.tensor_scalar(lam[:, 2:3], lam[:, 2:3], -1.0, None, ALU.mult))
            ch.link(pool.tensor_tensor(lam[:, 1:2], e_col[:, :], lam[:, 1:2], ALU.pow))
            pool.tensor_scalar(lam[:, 1:2], lam[:, 1:2], -1.0, None, ALU.add)
            pool.tensor_tensor(lam[:, 0:1], e_col[:, :], lam[:, 2:3], ALU.pow)
            pool.tensor_scalar(half_br[:, :], b_rkv[:, 0:1], 0.5, None, ALU.mult).then_inc(s("lam_ready"), 1)
            for t in range(SLOTS):
                stage_a(0, t)
                stage_l(1, t)
            for t in range(SLOTS):
                stage_b(0, t)
                stage_a(1, t)
                stage_l(2, t)
            for t in range(SLOTS):
                stage_c(0, t)
                stage_b(1, t)
                stage_a(2, t)
                stage_l(3, t)
            with pool.Fori(1, B - 3) as i:
                for t in range(SLOTS):
                    stage_c(i, t)
                    stage_b(i + 1, t)
                    stage_a(i + 2, t)
                    stage_l(i + 3, t)
            for t in range(SLOTS):
                stage_c(B - 3, t)
                stage_b(B - 2, t)
                stage_a(B - 1, t)
            for t in range(SLOTS):
                stage_c(B - 2, t)
                stage_b(B - 1, t)
            for t in range(SLOTS):
                stage_c(B - 1, t)

            def moe_pool(m):
                with pool.Fori(0, NG) as g:
                    pool.wait_ge(s(f"moe{m}_var"), g + 1)
                    pool.tensor_tensor(rstd[:, 0:GB], rstd[:, 0:GB], neg_half[:, 0:GB], ALU.pow)\
                        .then_inc(s(f"moe{m}_rstd"), 1)

            if phases >= 2:
                moe_pool(0)
            if phases >= 3:
                pool.wait_ge(s("phase_done"), 2)
                pool.memset(l_const[:, 1:2], 0.5)
                pool.memset(l_const[:, 0:1], 1e-6).then_inc(s("l_consts"), 1)
                with pool.Fori(0, B) as b:
                    pool.wait_ge(s("l_var"), b + 1)
                    pool.tensor_tensor(rstd[:, :], rstd[:, :], neg_half[:, 0:BPB], ALU.pow).then_inc(s("l_rstd"), 1)
            if phases >= 4:
                moe_pool(1)

        @block.vector
        def _(ve):
            ch = Chain(ve, s("ve_chain"))

            def carry_wait():
                ve.memset(unused[:, :], 0.0)

            def variances(n0, nb, var_sem):
                for j in range(nb):
                    ins = ve.bn_stats(stats[:, j, :], x[:, bass.ds(n0 + j, 1), :].rearrange("p a c -> p (a c)"))
                ch.link(ins)
                carry_wait()
                for j in range(nb):
                    ins = ve.bn_aggr(mv[:, j, :], stats[:, j, :])
                ch.link(ins)
                ve.tensor_scalar(rstd[:, 0:nb], mv[:, 0:nb, 1], LN_EPS, None, ALU.add).then_inc(s(var_sem), 1)

            def normalise(n0, nb, rstd_sem, rstd_at, y_sem):
                ve.wait_ge(s(rstd_sem), rstd_at)
                for j in range(nb):
                    ve.tensor_scalar(y[:, j, :], x[:, bass.ds(n0 + j, 1), :].rearrange("p a c -> p (a c)"),
                                     mv[:, j, 0:1], rstd[:, j:j + 1], ALU.subtract, ALU.mult).then_inc(s(y_sem), 1)

            LINKS_A, LINKS_B, LINKS_C = 2 + 2 * 3 + 2 + 1, 2 * (C - 1), 2 * 2
            marks = {}

            def stage_l(b, t):
                if t == L_VAR:
                    ve.wait_ge(s("x_in"), 16 * b + 16)
                    variances(b * BPB, BPB, "d_var")
                if t == L_Y:
                    normalise(b * BPB, BPB, "d_rstd", b + 1, "d_y")
                half, k = divmod(t - L_CONV, 4)
                if 0 <= half < GPB:
                    cv = hT[:, half * GT:(half + 1) * GT]
                    src = yT[:, half * GT + k:half * GT + k + GT]
                    if k == 0:
                        ve.wait_ge(s("d_yT"), b * GPB + GPB)
                        marks["conv"] = ch.mark(ve.tensor_scalar(cv, src, conv_w[:, 0:1], None, ALU.mult))
                    else:
                        ch.wait(marks["conv"])
                        ins = ve.scalar_tensor_tensor(cv, src, conv_w[:, k:k + 1], cv, ALU.mult, ALU.add)
                        if k < 3:
                            marks["conv"] = ch.mark(ins)
                        else:
                            ins.then_inc(s("d_conv"), 1)

            def stage_a(b, t):
                for half in range(GPB):
                    hb = slice(half * GB, (half + 1) * GB)
                    if t == A_NORM + 2 + half:
                        ve.wait_ge(s("d_sq"), b * GPB + half + 1)
                        marks["ss"] = ch.mark(ve.tensor_reduce(ss[:, hb], sq[:, hb].rearrange("p n (h d) -> p n h d", d=DK),
                                                               AXX, ALU.add))
                if t == A_NORM + 4:
                    ch.wait(marks["ss"])
                    ve.tensor_scalar(ss[:, :, :], ss[:, :, :], NORM_MIN_SQ, None, ALU.max).then_inc(s("d_ss"), 1)
                for k, (dst, c0, h0) in enumerate(((kn, 0, 0), (qn, HEADS * DK, HEADS))):
                    if t == A_KN + k:
                        ve.wait_ge(s("d_rn"), b + 1)
                        ve.wait_ge(s("d_bkq"), b)
                        ve.tensor_tensor(dst[:, :, :, 0:DK],
                                         kqv[:, :, c0:c0 + HEADS * DK].rearrange("p n (h d) -> p n h d", d=DK),
                                         bc(rn[:, :, h0:h0 + HEADS], 3, DK), ALU.mult).then_inc(s("d_kn"), 1)
                if t == A_R:
                    ve.tensor_scalar(beta[:, :, :], th[:, :, :], 0.5, 0.5, ALU.mult, ALU.add)
                    marks["beta"] = ch.mark(ve.tensor_scalar(nbeta[:, :, :], th[:, :, :], -0.5, -0.5, ALU.mult, ALU.add))
                for half in range(GPB):
                    hb = slice(half * GB, (half + 1) * GB)
                    if t == A_R + 1 + half:
                        ch.wait(marks["beta"])
                        ve.wait_ge(s("d_bR"), b)
                        ve.tensor_tensor(R[:, hb, :, 0:DV],
                                         kqv[:, hb, V0:V0 + HEADS * DV].rearrange("p n (h d) -> p n h d", d=DV),
                                         bc(beta[:, hb, :], 3, DV), ALU.mult)
                if t == A_R + 3:
                    ve.wait_ge(s("d_kn"), 2 * b + 2)
                    ve.tensor_tensor(R[:, :, :, DV:RH], kn[:, :, :, 0:DK], bc(beta[:, :, :], 3, DK),
                                     ALU.mult).then_inc(s("d_R"), 1)
                n = t - A_GRAM
                if 0 <= n < BPB:
                    ve.wait_ge(s("d_gram"), b * BPB + n + 1)
                    ve.tensor_tensor(n_c[:, n], ps[:, 0:HEADS, 0:C], bc(nbeta[:, n, :], 2, C), ALU.mult)
                    if n == 0:
                        ve.wait_ge(s("d_pbd"), 2 * b)
                    ve.tensor_tensor(gp[:, n], ps[:, 0:HEADS, C:2 * C], bc(m_p[:, :], 1, HEADS),
                                     ALU.mult).then_inc(s("d_gp"), 1)

            def row_of_inverse(b, t, step):
                i = t - B_INV + 1
                if t == 0 and step == 0:
                    ve.wait_ge(s("d_gp"), (b + 1) * BPB)
                    ve.wait_ge(s("d_tbd"), 2 * b)
                    ve.transpose(n_p[:, :, :], n_c[:, :, :, :].rearrange("p n h j -> p j (n h)")).then_inc(s("d_np"), 1)
                if 1 <= i < C and step == 0:
                    if i == 1:
                        ve.wait_ge(s("d_np"), b + 1)
                    else:
                        ch.wait(marks["row"])
                    if i < SUB:
                        ins = ve.tensor_tensor(prod[:, :, 0:i, 0:i], diagonal_blocks(t_p, i, "lm -> ml"),
                                               bc(diagonal_blocks(n_p, i, "row"), 2, i), ALU.mult)
                    else:
                        t_ml = t_p[:, 0:i, 0:SUB].rearrange("p l m -> p m l")
                        n_row = n_p[:, 0:i, i:i + 1].rearrange("p l a -> p a l").to_broadcast([P, SUB, i])
                        ins = ve.tensor_tensor(prod2[:, :, 0:i], t_ml, n_row, ALU.mult)
                    marks["prod"] = ch.mark(ins)
                if 1 <= i < C and step == 1:
                    ch.wait(marks["prod"])
                    if i < SUB:
                        ins = ve.tensor_reduce(diagonal_blocks(t_p, i, "row out"), prod[:, :, 0:i, 0:i], AXX, ALU.add)
                    else:
                        ins = ve.tensor_reduce(t_p[:, i, 0:SUB], prod2[:, :, 0:i], AXX, ALU.add)
                    marks["row"] = ch.mark(ins)

            def stage_b(b, t):
                if t == B_TC:
                    ch.wait(marks["row"])
                    ve.transpose(t_c.rearrange("p n h i -> p i (n h)"), t_p[:, :, :]).then_inc(s("d_inv"), 1)
                apply(b, t, B_APPLY)

            def apply(b, t, pairs):
                for p, t0 in pairs:
                    if t == t0 + 1:
                        pair = slice(2 * p, 2 * p + 2)
                        ve.wait_ge(s("d_puw"), b * NPAIR + p + 1)
                        ve.wait_ge(s("d_qT"), b * NPAIR + p)
                        ve.wait_ge(s("d_bkq"), b + 1)
                        ve.tensor_tensor(qp[:, :, :].rearrange("p n (h d) -> p n h d", h=HEADS), b_qn[:, pair, :].rearrange("p n (h d) -> p n h d", h=HEADS),
                                         puw[:, pair, :, DV:RH], ALU.subtract).then_inc(s("d_qp"), 1)

            def states(b, t):
                if t == 0:
                    ve.memset(S[0:KW, 0, :], 0.0).then_inc(s("d_S"), 1)
                c = t - 1
                if 0 <= c < NCH - 1:
                    if c == 0:
                        ve.wait_ge(s("d_prep"), b * NCH + 1)
                    else:
                        ve.wait_ge(s("d_step"), b * (NCH - 2) + c)
                    if c + 1 >= NS:
                        ve.wait_ge(s("d_qs"), b * BPB + (c + 1 - NS) // Q + 1)
                    ve.tensor_tensor(S[0:KW, (c + 1) % NS, :], ps[0:KW, c % Q, P:2 * P], bd[0:KW, :], ALU.mult)\
                        .then_inc(s("d_S"), 1)

            def stage_c(b, t):
                apply(b, t, C_APPLY)
                for c in range(Q) if t == 0 else [t + 2] if 2 <= t and t + 2 < NCH else []:
                    ve.wait_ge(s("d_prep"), b * NCH + c + 1)
                    ve.tensor_tensor(A[0:KW, c % NS, :], ident[0:KW, 0:KW], ps[0:KW, c % Q, 0:KW], ALU.subtract)\
                        .then_inc(s("d_A"), 1)
                n, k = divmod(t - Q, Q)
                if 0 <= n < BPB and k == 0:
                    ve.wait_ge(s("d_qs"), b * BPB + n + 1)
                    ve.wait_ge(s("d_oT"), b * GPB)
                    ve.tensor_tensor(o[:, n, :].rearrange("p (h d) -> p h d", h=HEADS), puw[:, n, :, 0:DV],
                                     ps[:, BK_O, 0:P].rearrange("p (h d) -> p h d", h=HEADS), ALU.add)\
                        .then_inc(s("d_o"), 1)
                for half, t0 in enumerate(C_POST):
                    blocks = slice(half * GB, (half + 1) * GB)
                    if t == t0 + 1:
                        ve.wait_ge(s("d_osq"), b * GPB + half + 1)
                        ch.link(ve.tensor_reduce(ro[:, half], osq[:, :, :].rearrange("p n (h d) -> p (n h) d", d=DV),
                                                 AXX, ALU.add))
                        ve.tensor_scalar(ro[:, half], ro[:, half], 1.0 / DV, RMS_EPS, ALU.mult, ALU.add)\
                            .then_inc(s("d_oss"), 1)
                    gs4 = c_gs[:, blocks, :].rearrange("p n (h d) -> p (n h) d", d=DV)
                    if t == t0 + 3:
                        ve.wait_ge(s("d_gw"), b * GPB + half + 1)
                        marks["gs"] = ch.mark(ve.tensor_tensor(c_gs[:, blocks, :], c_gs[:, blocks, :], o[:, blocks, :],
                                                               ALU.mult))
                    if t == t0 + 5:
                        ch.wait(marks["gs"])
                        ve.wait_ge(s("d_ro"), b * GPB + half + 1)
                        ve.tensor_tensor(o[:, blocks, :].rearrange("p n (h d) -> p (n h) d", d=DV), gs4,
                                         bc(ro[:, half], 2, DV), ALU.mult).then_inc(s("d_og"), 1)
                    if t == t0 + 8:
                        ve.wait_ge(s("d_out"), b * GPB + half + 1)
                        xg = x[:, bass.ds(b * BPB + half * GB, GB), :]
                        ve.tensor_tensor(xg, xg, ps[:, BK_P, :].rearrange("p (n c) -> p n c", n=GB), ALU.add)\
                            .then_inc(s("d_x"), 1)

            for t in range(SLOTS):
                if t == L_T:
                    for v in (A, S, qpT):
                        ve.memset(v[:, :, :], 0.0)
                    for v in (kn, qn):
                        ins = ve.memset(v[:, :, :, :], 0.0)
                    ins.then_inc(s("zeros"), 1)
                if t == L_CONV:
                    ve.wait_ge(s("zeros"), 2)
                    ve.wait_ge(s("consts"), 1)
                    ve.wait_ge(s("w_in"), 16 * N_W)
                stage_l(0, t)
            for t in range(SLOTS):
                stage_a(0, t)
                stage_l(1, t)
            for t in range(SLOTS):
                row_of_inverse(0, t, 0)
                row_of_inverse(0, t, 1)
                stage_b(0, t)
                stage_a(1, t)
                stage_l(2, t)
            for t in range(SLOTS):
                row_of_inverse(1, t, 0)
                states(0, t)
                row_of_inverse(1, t, 1)
                stage_c(0, t)
                stage_b(1, t)
                stage_a(2, t)
                stage_l(3, t)
            with ve.Fori(1, B - 3) as i:
                ch.enter(i - 1, LINKS_C + LINKS_B + LINKS_A)
                for t in range(SLOTS):
                    row_of_inverse(i + 1, t, 0)
                    states(i, t)
                    row_of_inverse(i + 1, t, 1)
                    stage_c(i, t)
                    stage_b(i + 1, t)
                    stage_a(i + 2, t)
                    stage_l(i + 3, t)
                ch.leave(B - 4)
            for t in range(SLOTS):
                row_of_inverse(B - 2, t, 0)
                states(B - 3, t)
                row_of_inverse(B - 2, t, 1)
                stage_c(B - 3, t)
                stage_b(B - 2, t)
                stage_a(B - 1, t)
            for t in range(SLOTS):
                row_of_inverse(B - 1, t, 0)
                states(B - 2, t)
                row_of_inverse(B - 1, t, 1)
                stage_c(B - 2, t)
                stage_b(B - 1, t)
            for t in range(SLOTS):
                states(B - 1, t)
                stage_c(B - 1, t)

            ve.wait_ge(s("d_x"), GPB * B)
            ve.sem_inc(s("phase_done"), 1)

            def selectors():
                ch.link(ve.tensor_tensor(sel_col[0:2 * E, :], ident[0:2 * E, 0:E], ident[0:2 * E, E:2 * E], ALU.add))
                ve.tensor_copy(sel[0:2 * E, :, :], bc(sel_col[0:2 * E, :], 2, P))

            def weights_low(e):
                ve.wait_ge(s("w_hi"), 2 * e + 1)
                ve.tensor_tensor(wfl[:, e, :], w_fc[:, e, :], wfh[:, e, :].bitcast(F32), ALU.subtract)\
                    .then_inc(s("split"), 1)
                k = slice(e * HC, (e + 1) * HC)
                ve.wait_ge(s("w_hi"), 2 * e + 2)
                ve.tensor_tensor(wpl[:, k, :], w_pr[:, k, :], wph[:, k, :].bitcast(F32), ALU.subtract)\
                    .then_inc(s("split"), 1)

            def moe_vector(m):
                def sm(name):
                    return s(f"moe{m}_{name}")

                def route(g):
                    ve.wait_ge(sm("lg"), g + 1)
                    ch.link(ve.tensor_copy(lg[:, :, :], ps[:, 1, 0:GB * E].rearrange("p (n e) -> p n e", n=GB)))
                    carry_wait()
                    for j in range(GB):
                        ins = ve.max(top[:, j, :], lg[:, j, :])
                    ch.link(ins)
                    carry_wait()
                    for j in range(GB):
                        ins = ve.max_index(idx[:, j, :], top[:, j, :], lg[:, j, :])
                    ch.link(ve.tensor_tensor(dlt[:, :], top[:, :, 1], top[:, :, 0], ALU.subtract))
                    ve.sem_inc(sm("dlt"), 1)
                    ch.link(ve.tensor_copy(idxf[:, :, 0:2], idx[:, :, 0:2]))
                    for k in range(2):
                        ins = ve.tensor_tensor(oh[:, k], bc(iota8[:, :], 1, GB), bc(idxf[:, :, k], 2, E), ALU.is_equal)
                    ch.link(ins)

                def combine(g):
                    ve.wait_ge(sm("tanh"), g + 1)
                    ve.tensor_scalar(w12[:, 0, :], tnh[:, :], -0.5, 0.5, ALU.mult, ALU.add)
                    ch.link(ve.tensor_scalar(w12[:, 1, :], tnh[:, :], 0.5, 0.5, ALU.mult, ALU.add))
                    for k in range(2):
                        ins = ve.tensor_tensor(oh[:, k], oh[:, k], bc(w12[:, k, :], 2, E), ALU.mult)
                    ch.link(ins)
                    ch.link(ve.tensor_tensor(comb[:, :, :], oh[:, 0], oh[:, 1], ALU.add))
                    ch.link(ve.tensor_copy(comb2[:, :, 0:E], comb[:, :, :]))
                    ve.tensor_tensor(comb2[:, :, E:2 * E], comb[:, :, :], comb2[:, :, 0:E].bitcast(F32), ALU.subtract)\
                        .then_inc(sm("comb"), 1)

                LINKS_ROUTE, LINKS_LN, LINKS_HID = 9, 2, E

                def tokens_low(g, p):
                    ve.wait_ge(sm("yh"), g + 1)
                    ve.tensor_tensor(yTl[:, p, :], yTf[:, :], yTh[:, p, :].bitcast(F32), ALU.subtract).then_inc(sm("yl"), 1)

                def hidden_low(g, e, c):
                    ve.wait_ge(sm("hid"), g * E * HC + e * HC + c + 1 + HC)
                    ve.wait_ge(sm("pr"), g * E + e + 1)
                    if c == HC - 1:
                        ch.link(ve.tensor_copy(hidh[:, e % 2, c, :], hidf[:, c, :]))
                    ve.tensor_tensor(hidl[:, e % 2, c, :], hidf[:, c, :], hidh[:, e % 2, c, :].bitcast(F32),
                                     ALU.subtract).then_inc(sm("lo"), 1)

                def weigh(g, e):
                    ve.wait_ge(sm("pr"), g * E + e + 3)
                    ve.wait_ge(sm("wb"), g * E + e + 1)
                    if e == 0:
                        ve.wait_ge(sm("flush"), g)
                    else:
                        ve.wait_ge(sm("acc"), g * (E - 1) + max(e - 1, 0))
                    ve.tensor_tensor(acc[:, :] if e == 0 else scaled[:, :], ps[:, 6, :], wb[:, e % 2, :], ALU.mult)\
                        .then_inc(sm("mul"), 1)

                def gather(g, e):
                    ve.wait_ge(sm("mul"), g * E + e + 1)
                    ve.wait_ge(sm("acc"), g * (E - 1) + e - 1)
                    ve.tensor_tensor(acc[:, :], acc[:, :], scaled[:, :], ALU.add).then_inc(sm("acc"), 1)

                def residual(g):
                    ve.wait_ge(sm("flush"), g + 1)
                    xg = x[:, bass.ds(g * GB, GB), :]
                    ve.tensor_tensor(xg, xg, ps[:, 0, :].rearrange("p (n c) -> p n c", n=GB), ALU.add)\
                        .then_inc(sm("x"), 1)

                def group(g, p, first=False, last=False):
                    if first:
                        for c in range(HC):
                            hidden_low(g, 0, c)
                    for e in range(E):
                        step = (g, e + 1) if e + 1 < E else (g + 1, 0)
                        ahead = e + 1 < E or not last
                        if m == 0 and first and e + 3 < E:
                            weights_low(e + 3)
                        if ahead:
                            hidden_low(*step, 0)
                        if e == 0 and not first:
                            gather(g - 1, E - 1)
                        if e >= 2:
                            gather(g, e - 1)
                        if ahead:
                            for c in range(1, HC):
                                hidden_low(*step, c)
                        weigh(g, e)
                        if e == 0 and not first:
                            residual(g - 1)
                        if last:
                            continue
                        if e == 0:
                            variances((g + 1) * GB, GB, f"moe{m}_var")
                        if e == 1:
                            normalise((g + 1) * GB, GB, f"moe{m}_rstd", g + 2, f"moe{m}_y")
                        if e == 3:
                            route(g + 1)
                        if e == 4:
                            tokens_low(g + 1, 1 - p)
                        if e == 5:
                            combine(g + 1)
                    if last:
                        gather(g, E - 1)

                variances(0, GB, f"moe{m}_var")
                normalise(0, GB, f"moe{m}_rstd", 1, f"moe{m}_y")
                if m == 0:
                    selectors()
                    weights_low(0)
                tokens_low(0, 0)
                if m == 0:
                    weights_low(1)
                route(0)
                combine(0)
                if m == 0:
                    weights_low(2)
                group(0, 0, first=True)
                with ve.Fori(0, (NG - 2) // 2) as i:
                    ch.enter(i, 2 * (LINKS_ROUTE + LINKS_LN + LINKS_HID))
                    group(2 * i + 1, 1)
                    group(2 * i + 2, 0)
                    ch.leave((NG - 2) // 2)
                group(NG - 1, 1, last=True)
                residual(NG - 1)
                ve.wait_ge(sm("x"), NG)
                ve.sem_inc(s("phase_done"), 1)

            if phases >= 2:
                moe_vector(0)

            def linrec_vector():
                decay = lam[:, 0:1].to_broadcast([P, L])

                def residual(b):
                    for half in range(GPB):
                        ve.wait_ge(s("l_out"), b * GPB + half + 1)
                        xg = x[:, bass.ds(b * BPB + half * GB, GB), :]
                        ve.tensor_tensor(xg, xg, ps[:, half, :].rearrange("p (n c) -> p n c", n=GB), ALU.add)\
                            .then_inc(s("l_x"), 1)

                def batch(b, p, first=False, last=False):
                    for half in range(GPB):
                        ve.wait_ge(s("l_k"), b * GPB + half + 1)
                        hs = slice(half * GT, half * GT + GT)
                        ins = ve.scalar_tensor_tensor(l_kv[:, hs], ps[:, 4 + 3 * half, :], b_rkv[:, 2:3],
                                                      l_k[p][:, hs], ALU.add, ALU.mult)
                        ins.then_inc(s("l_kv"), 1)
                    ve.wait_ge(s("l_kv"), (b + 1) * GPB)
                    ch.mark(ve.tensor_tensor_scan(l_u1, decay, l_kv, 0.0, ALU.mult, ALU.add))
                    ch.mark(ve.tensor_tensor_scan(l_u2, decay, l_k[p], 0.0, ALU.mult, ALU.add))
                    if not first:
                        residual(b - 1)
                    if not last:
                        variances((b + 1) * BPB, BPB, "l_var")
                    ch.wait()
                    ve.scalar_tensor_tensor(l_u2, l_k[p], lam[:, 1:2], l_u2, ALU.mult, ALU.add)\
                        .then_inc(s("l_den"), 1)
                    ch.link(ve.scalar_tensor_tensor(l_u1, l_kv, lam[:, 1:2], l_u1, ALU.mult, ALU.add))
                    if not last:
                        normalise((b + 1) * BPB, BPB, "l_rstd", b + 2, "l_y")
                    ve.wait_ge(s("l_eps"), b + 1)
                    ch.link(ve.reciprocal(l_u2, l_u2))
                    ch.link(ve.tensor_tensor(l_u1, l_u1, l_u2, ALU.mult))
                    ve.wait_ge(s("l_r"), b + 1)
                    if not first:
                        ve.wait_ge(s("l_out"), b * GPB)
                    ve.tensor_tensor(l_x, l_u1, l_r[p], ALU.mult).then_inc(s("l_xT"), 1)

                LINKS = 2 + 2 + 1 + 2
                variances(0, BPB, "l_var")
                normalise(0, BPB, "l_rstd", 1, "l_y")
                batch(0, 0, first=True)
                with ve.Fori(0, (B - 2) // 2) as i:
                    ch.enter(i, 2 * LINKS)
                    batch(2 * i + 1, 1)
                    batch(2 * i + 2, 0)
                    ch.leave((B - 2) // 2)
                batch(B - 1, 1, last=True)
                residual(B - 1)
                ve.wait_ge(s("l_x"), GPB * (B + 1))
                ve.sem_inc(s("phase_done"), 1)

            if phases >= 3:
                linrec_vector()
            if phases >= 4:
                moe_vector(1)

        @block.scalar
        def _(act):
            loads = [
                (w_rkv[:, :], ap["W_rkv"]), (b_rkv[:, :], ap["b_rkv"].rearrange("(t p) -> p t", p=P)),
                (w_o[:, :], ap["W_o"]), (bo_row[0:1, :], ap["b_o"].rearrange("(a n) -> a n", a=1)),
                (nu_col[:, :], ap["nu_log"].rearrange("(p a) -> p a", a=1)),
                (ga_col[:, :], ap["gamma_log"].rearrange("(p a) -> p a", a=1)),
                (router[0:E, :], ap["router_w"]),
                (bfc_rows[0:E * HC, :], ap["b_fc"].rearrange("e (c p) -> (e c) p", p=P)),
                (b_pr2[0:E, :], ap["b_proj"]), (b_pr2[E:2 * E, :], ap["b_proj"]),
            ]
            with nc.allow_non_contiguous_dma(reason="a few hundred 4-byte elements, once"):
                for dst, src in loads:
                    act.dma_start(dst, src).then_inc(s("w_in"), 16)

            def stage_l(b, t):
                for half in range(GPB):
                    if t == L_T + half:
                        act.wait_ge(s("d_T"), b * GPB + half + 1)
                        act.copy(yT[:, 3 + half * GT:3 + (half + 1) * GT], ps[:, BK_A, :]).then_inc(s("d_yT"), 1)
                    if t == L_CONV + 4 * half + 4:
                        act.wait_ge(s("d_conv"), b * GPB + half + 1)
                        h = hT[:, half * GT:(half + 1) * GT]
                        act.activation(h, h, ACT.Silu).then_inc(s("d_h"), 1)

            def stage_a(b, t):
                n = t - A_PROJ
                if 0 <= n < BPB:
                    act.wait_ge(s("d_proj"), b * BPB + n + 1)
                    if n == 0:
                        act.wait_ge(s("d_R"), b)
                        act.wait_ge(s("d_mgs"), b)
                    bank = (BK_A, BK_B)[n % 2]
                    act.copy(kqv[:, n, :], ps[:, bank, 0:G0])
                    act.activation(th[:, n, :], ps[:, bank, B0:NPROJ], ACT.Tanh, scale=0.5)
                    act.activation(gs[:, n, :], ps[:, bank, G0:B0], ACT.Silu).then_inc(s("d_kqv"), 1)
                half = t - (A_NORM + 1)
                if 0 <= half < GPB:
                    hb = slice(half * GB, (half + 1) * GB)
                    act.wait_ge(s("d_kqv"), b * BPB + (half + 1) * GB)
                    if half == 0:
                        act.wait_ge(s("d_np"), b)
                    act.activation(sq[:, hb], kqv[:, hb, 0:KQ], ACT.Square).then_inc(s("d_sq"), 1)
                p = t - A_KQT
                if 0 <= p < NPAIR:
                    act.wait_ge(s("d_kqT"), b * NPAIR + p + 1)
                    act.copy(kqT[:, 2 * p:2 * p + 2], ps[:, BK_A, :].rearrange("p (n z t) -> p n z t", n=2, z=2))\
                        .then_inc(s("d_kqTs"), 1)

            def stage_b(b, t):
                if t == B_COPY:
                    act.wait_ge(s("d_R"), b + 1)
                    act.wait_ge(s("d_y1"), b * NPAIR)
                    act.copy(b_R[:, :, :, :], R[:, :, :, :]).then_inc(s("d_bR"), 1)
                for half in range(GPB):
                    blocks = slice(half * GB, (half + 1) * GB)
                    if t == B_PBD + half:
                        act.wait_ge(s("d_gp"), (b + 1) * BPB)
                        act.wait_ge(s("d_pp"), b * NPAIR)
                        spread(act, p_bd[:, blocks], gp[:, blocks], s("d_pbd"))
                    if t == B_TBD:
                        act.wait_ge(s("d_inv"), b + 1)
                        act.wait_ge(s("d_y1"), b * NPAIR)
                        spread(act, t_bd[:, blocks], t_c[:, blocks], s("d_tbd"))
                apply(b, t, B_APPLY)

            def apply(b, t, pairs):
                for p, t0 in pairs:
                    pair = slice(2 * p, 2 * p + 2)
                    b_ps = ps[:, BK_B, 0:2 * HEADS * RH].rearrange("p (n h d) -> p n h d", n=2, h=HEADS)
                    taken = b if p >= 2 else b - 1
                    some = 0 if p >= 2 else 2 * (p + 1)
                    later = not (type(b) is int and taken < 0)
                    if t == t0:
                        act.wait_ge(s("d_y1"), b * NPAIR + p + 1)
                        if later:
                            act.wait_ge(s("d_prep"), taken * NCH + some * Q)
                        act.copy(wk[:, pair, :].rearrange("p n (h d) -> p n h d", h=HEADS), b_ps[:, :, :, DV:RH])
                        act.copy(uw[:, pair], b_ps).then_inc(s("d_uw"), 1)
                    if t == t0 + 1:
                        act.wait_ge(s("d_pp"), b * NPAIR + p + 1)
                        if later:
                            act.wait_ge(s("d_o"), taken * BPB + some)
                        act.copy(puw[:, pair], b_ps).then_inc(s("d_puw"), 1)
                    if t == t0 + 2:
                        act.wait_ge(s("d_qT"), b * NPAIR + p + 1)
                        if later:
                            act.wait_ge(s("d_qs"), taken * BPB + some)
                        act.copy(qpT[0:KW, 2 * p, :], ps[0:KW, BK_B, 0:P])
                        act.copy(qpT[0:KW, 2 * p + 1, :], ps[KW:2 * KW, BK_B, 0:P]).then_inc(s("d_qTs"), 1)

            def stage_c(b, t):
                apply(b, t, C_APPLY)
                for half, t0 in enumerate(C_POST):
                    if t == t0:
                        act.wait_ge(s("d_o"), b * BPB + (half + 1) * GB)
                        act.wait_ge(s("d_oss"), b * GPB + half)
                        act.activation(osq[:, :, :], o[:, half * GB:(half + 1) * GB, :], ACT.Square).then_inc(s("d_osq"), 1)
                    if t == t0 + 6:
                        act.wait_ge(s("d_oT"), b * GPB + half + 1)
                        act.copy(oT[:, :], ps[:, BK_P, :]).then_inc(s("d_oTs"), 1)

            for t in range(SLOTS):
                stage_l(0, t)
                if t == L_T + GPB:
                    act.wait_ge(s("setup_T"), 1)
                    act.copy(routerT[:, :], ps[:, 0, 0:E])
                    act.copy(bfcT[:, :], ps[:, 0, 128:128 + E * HC]).then_inc(s("setup_sb"), 1)
            for t in range(SLOTS):
                stage_a(0, t)
                stage_l(1, t)
            for t in range(SLOTS):
                stage_b(0, t)
                stage_a(1, t)
                stage_l(2, t)
            for t in range(SLOTS):
                stage_c(0, t)
                stage_b(1, t)
                stage_a(2, t)
                stage_l(3, t)
            with act.Fori(1, B - 3) as i:
                for t in range(SLOTS):
                    stage_c(i, t)
                    stage_b(i + 1, t)
                    stage_a(i + 2, t)
                    stage_l(i + 3, t)
            for t in range(SLOTS):
                stage_c(B - 3, t)
                stage_b(B - 2, t)
                stage_a(B - 1, t)
            for t in range(SLOTS):
                stage_c(B - 2, t)
                stage_b(B - 1, t)
            for t in range(SLOTS):
                stage_c(B - 1, t)

            def weights_high(e):
                act.wait_ge(s("fc_in"), 16 * e + 16)
                act.copy(wfh[:, e, :], w_fc[:, e, :]).then_inc(s("w_hi"), 1)
                k = slice(e * HC, (e + 1) * HC)
                act.wait_ge(s("pr_in"), 16 * e + 16)
                act.copy(wph[:, k, :], w_pr[:, k, :]).then_inc(s("w_hi"), 1)

            def moe_scalar(m):
                def sm(name):
                    return s(f"moe{m}_{name}")

                def tokens(g):
                    act.wait_ge(sm("T"), g + 1)
                    act.copy(yTf[:, :], ps[:, 0, :]).then_inc(sm("yf"), 1)

                def tokens_high(g, p):
                    act.wait_ge(sm("yf"), g + 1)
                    act.copy(yTh[:, p, :], yTf[:, :]).then_inc(sm("yh"), 1)

                def weights(g):
                    act.wait_ge(sm("cT"), g + 1)
                    act.copy(combT[0:2 * E, :], ps[0:2 * E, 1, :]).then_inc(sm("cTs"), 1)

                def order(g):
                    act.wait_ge(sm("dlt"), g + 1)
                    act.activation(tnh[:, :], dlt[:, :], ACT.Tanh, scale=0.5).then_inc(sm("tanh"), 1)

                def group(g, p, first=False, last=False):
                    for e in range(E):
                        if m == 0 and first and e + 3 < E:
                            weights_high(e + 3)
                        for c in range(HC):
                            act.wait_ge(sm("fc"), g * E * HC + e * HC + c + 1)
                            act.wait_ge(sm("lo"), g * E * HC + e * HC + c + 1)
                            b_col = bfcT[:, e * HC + c:e * HC + c + 1]
                            ins = act.activation(hidf[:, c, :], ps[:, 2 + c, :], ACT.Gelu_apprx_tanh, bias=b_col)
                            if c < HC - 1:
                                act.wait_ge(sm("pr"), g * E + e + 1)
                                ins = act.activation(hidh[:, e % 2, c, :], ps[:, 2 + c, :], ACT.Gelu_apprx_tanh, bias=b_col)
                            ins.then_inc(sm("hid"), 1)
                            if e == 5 and c == 0 and not last:
                                order(g + 1)
                        act.wait_ge(sm("w"), g * E + e + 1)
                        if not (first and e == 0):
                            act.wait_ge(sm("mul"), g * E + e - 1)
                        act.copy(wb[:, e % 2, :], ps[:, 7, :]).then_inc(sm("wb"), 1)
                        if e == 2 and not last:
                            tokens(g + 1)
                        if e == 3 and not last:
                            tokens_high(g + 1, 1 - p)
                    if not last:
                        weights(g + 1)

                act.sem_inc(sm("hid"), HC)
                act.sem_inc(sm("lo"), HC)
                act.sem_inc(sm("pr"), 2)
                if m == 0:
                    weights_high(0)
                tokens(0)
                tokens_high(0, 0)
                if m == 0:
                    weights_high(1)
                order(0)
                if m == 0:
                    weights_high(2)
                weights(0)
                group(0, 0, first=True)
                with act.Fori(0, (NG - 2) // 2) as i:
                    group(2 * i + 1, 1)
                    group(2 * i + 2, 0)
                group(NG - 1, 1, last=True)

            if phases >= 2:
                act.wait_ge(s("phase_done"), 1)
                moe_scalar(0)
            def linrec_scalar():
                def batch(b, p):
                    for half in range(GPB):
                        act.wait_ge(s("l_T"), b * GPB + half + 1)
                        act.copy(l_yT[:, half * GT:(half + 1) * GT], ps[:, half, :]).then_inc(s("l_yT"), 1)
                    for half in range(GPB):
                        hs = slice(half * GT, half * GT + GT)
                        act.wait_ge(s("l_rkv"), b * GPB + half + 1)
                        if half == 0 and not (type(b) is int and b < 2):
                            act.wait_ge(s("l_xT"), b)
                        act.activation(l_k[p][:, hs], ps[:, 3 + 3 * half, :], ACT.Exp, bias=b_rkv[:, 1:2]).then_inc(s("l_k"), 1)
                        act.activation(l_r[p][:, hs], ps[:, 2 + 3 * half, :], ACT.Tanh, bias=half_br[:, :], scale=0.5)\
                            .then_inc(s("l_t"), 1)
                    act.wait_ge(s("l_t"), (b + 1) * GPB)
                    act.activation(l_r[p], l_r[p], ACT.Identity, bias=l_const[:, 1:2], scale=0.5).then_inc(s("l_r"), 1)
                    act.wait_ge(s("l_den"), b + 1)
                    act.activation(l_u2, l_u2, ACT.Identity, bias=l_const[:, 0:1]).then_inc(s("l_eps"), 1)

                act.wait_ge(s("l_consts"), 1)
                act.sem_inc(s("l_xT"), 1)
                batch(0, 0)
                with act.Fori(0, (B - 2) // 2) as i:
                    batch(2 * i + 1, 1)
                    batch(2 * i + 2, 0)
                batch(B - 1, 1)

            if phases >= 3:
                act.wait_ge(s("phase_done"), 2)
                linrec_scalar()
            if phases >= 4:
                moe_scalar(1)

        @block.tensor
        def _(pe):
            pe.wait_ge(s("consts"), 1)

            def stage_l(b, t):
                half = t - L_T
                if 0 <= half < GPB:
                    for j in range(GB):
                        pe.wait_ge(s("d_y"), b * BPB + half * GB + j + 1)
                        pe.wait_ge(s("d_yT"), b * GPB + half)
                        pe.wait_ge(s("d_kqv"), b * BPB)
                        ins = pe.transpose(ps[:, BK_A, j * P:(j + 1) * P], y[:, half * GB + j, :], ident[:, :])
                    ins.then_inc(s("d_T"), 1)

            def stage_a(b, t):
                n = t - A_PROJ
                if 0 <= n < BPB:
                    pe.wait_ge(s("d_h"), b * GPB + n // GB + 1)
                    bank = (BK_A, BK_B)[n % 2]
                    if n >= 2:
                        pe.wait_ge(s("d_kqv"), b * BPB + n - 1)
                    if n == 1 and not (type(b) is int and b < 2):
                        pe.wait_ge(s("d_qTs"), (b - 2) * NPAIR + 2)
                    pe.matmul(ps[:, bank, 0:NPROJ], hT[:, n * P:(n + 1) * P], w_all[:, :],
                              start=True, stop=True).then_inc(s("d_proj"), 1)
                p = t - A_KQT
                if 0 <= p < NPAIR:
                    pe.wait_ge(s("d_kn"), 2 * b + 2)
                    pe.wait_ge(s("d_kqTs"), b * NPAIR + p)
                    pe.wait_ge(s("d_yT"), (min(b + 2, B) if type(b) is int else b + 2) * GPB)
                    for j in range(2):
                        for z, v in enumerate((kn, qn)):
                            ins = pe.transpose(ps[:, BK_A, (2 * j + z) * P:(2 * j + z + 1) * P],
                                               v[:, 2 * p + j].rearrange("p h d -> p (h d)"), ident[:, :])
                    ins.then_inc(s("d_kqT"), 1)
                n = t - A_GRAM
                if 0 <= n < BPB:
                    pe.wait_ge(s("d_kqTs"), (b + 1) * NPAIR)
                    pe.wait_ge(s("d_gp"), b * BPB + n)
                    for h in range(HEADS):
                        rows = slice(DKP * h, DKP * h + DKP)
                        for q in range(Q):
                            r = slice(C * q, C * q + C)
                            m = slice(0, 2 * C) if q == 0 and h == 0 else r
                            ins = pe.matmul(ps[m, h, 0:2 * C], kqT[rows, n, 0, m], kqT[rows, n, :, r],
                                            start=True, stop=True)
                    ins.then_inc(s("d_gram"), 1)

            def stage_b(b, t):
                apply(b, t, B_APPLY)

            def apply(b, t, pairs):
                for p, t0 in pairs:
                    def heads(mat, rhs, done):
                        for j in range(2):
                            for h in range(HEADS):
                                k = (j * HEADS + h) * RH
                                ins = pe.matmul(ps[:, BK_B, k:k + RH], mat[:, 2 * p + j, h, :], rhs[:, 2 * p + j, h, :],
                                                start=True, stop=True)
                        ins.then_inc(done, 1)

                    if t == t0:
                        pe.wait_ge(s("d_bR"), b + 1)
                        pe.wait_ge(s("d_tbd"), 2 * b + p // 2 + 1)
                        pe.wait_ge(s("d_qTs"), b * NPAIR + p)
                        if p == 2:
                            pe.wait_ge(s("d_kqv"), (min(b + 3, B) if type(b) is int else b + 3) * BPB)
                        heads(t_bd, b_R, s("d_y1"))
                    if t == t0 + 1:
                        pe.wait_ge(s("d_pbd"), 2 * b + p // 2 + 1)
                        pe.wait_ge(s("d_uw"), b * NPAIR + p + 1)
                        heads(p_bd, uw, s("d_pp"))
                    if t == t0 + 2:
                        pe.wait_ge(s("d_qp"), b * NPAIR + p + 1)
                        pe.transpose(ps[:, BK_B, 0:P], qp[:, :, :].rearrange("p n c -> p (n c)"), ident[:, :])\
                            .then_inc(s("d_qT"), 1)

            def stage_c(b, t):
                apply(b, t, C_APPLY)

                def prepare(c):
                    n, q = divmod(c, Q)
                    r = slice(C * q, C * q + C)
                    if c % (2 * Q) == 0:
                        pe.wait_ge(s("d_uw"), b * NPAIR + n // 2 + 1)
                    pe.matmul(ps[0:KW, q, 0:KW], wk[r, n, :], c_kn[r, n, :],
                              start=True, stop=True, skip_group_check=True)
                    pe.matmul(ps[0:KW, q, P:2 * P], c_kn[r, n, :], uw[r, n, :, 0:DV],
                              start=False, stop=True, skip_group_check=True).then_inc(s("d_prep"), 1)

                if t == 0:
                    pe.wait_ge(s("d_gp"), min(b + 2, B) * BPB if type(b) is int else (b + 2) * BPB)
                    pe.wait_ge(s("d_ckn"), b + 1)
                    for c in range(Q):
                        prepare(c)
                c = t - 1
                if 1 <= c < NCH - 1:
                    pe.wait_ge(s("d_A"), b * NCH + c + 1)
                    pe.wait_ge(s("d_S"), b * NCH + c + 1)
                    pe.matmul(ps[0:KW, c % Q, P:2 * P], A[:, c % NS, :], S[:, c % NS, :],
                              start=False, stop=True, skip_group_check=True).then_inc(s("d_step"), 1)
                    if c + 3 < NCH:
                        prepare(c + 3)
                n, k = divmod(t - Q, Q)
                if 0 <= n < BPB and k == 0:
                    pe.wait_ge(s("d_S"), b * NCH + Q * n + Q)
                    pe.wait_ge(s("d_qTs"), b * NPAIR + n // 2 + 1)
                    pe.wait_ge(s("d_o"), b * BPB + n)
                    for q in range(Q):
                        r = slice(C * q, C * q + C)
                        ins = pe.matmul(ps[r, BK_O, 0:P], qpT[:, n, r], S[:, (Q * n + q) % NS, :],
                                        start=True, stop=True, skip_group_check=True)
                    ins.then_inc(s("d_qs"), 1)
                for half, t0 in enumerate(C_POST):
                    if t == t0 + 6:
                        pe.wait_ge(s("d_og"), b * GPB + half + 1)
                        pe.wait_ge(s("d_x"), b * GPB + half)
                        for j in range(GB):
                            ins = pe.transpose(ps[:, BK_P, j * P:(j + 1) * P], o[:, half * GB + j, :], ident[:, :])
                        ins.then_inc(s("d_oT"), 1)
                    if t == t0 + 7:
                        pe.wait_ge(s("d_oTs"), b * GPB + half + 1)
                        for j in range(GB):
                            ins = pe.matmul(ps[:, BK_P, j * P:(j + 1) * P], oT[:, j * P:(j + 1) * P], wo[:, :],
                                            start=True, stop=True)
                        ins.then_inc(s("d_out"), 1)

            for t in range(SLOTS):
                stage_l(0, t)
                if t == L_T + GPB:
                    pe.wait_ge(s("w_in"), 16 * N_W)
                    pe.transpose(ps[:, 0, 0:E], router[0:E, :], ident[0:E, 0:E])
                    pe.transpose(ps[:, 0, 128:128 + E * HC], bfc_rows[0:E * HC, :], ident[0:E * HC, 0:E * HC])\
                        .then_inc(s("setup_T"), 1)
                    pe.wait_ge(s("setup_sb"), 1)
            pe.wait_ge(s("zeros"), 2)
            for t in range(SLOTS):
                stage_a(0, t)
                stage_l(1, t)
            for t in range(SLOTS):
                stage_b(0, t)
                stage_a(1, t)
                stage_l(2, t)
            for t in range(SLOTS):
                stage_c(0, t)
                stage_b(1, t)
                stage_a(2, t)
                stage_l(3, t)
            with pe.Fori(1, B - 3) as i:
                for t in range(SLOTS):
                    stage_c(i, t)
                    stage_b(i + 1, t)
                    stage_a(i + 2, t)
                    stage_l(i + 3, t)
            for t in range(SLOTS):
                stage_c(B - 3, t)
                stage_b(B - 2, t)
                stage_a(B - 1, t)
            for t in range(SLOTS):
                stage_c(B - 2, t)
                stage_b(B - 1, t)
            for t in range(SLOTS):
                stage_c(B - 1, t)

            def moe_tensor(m):
                def sm(name):
                    return s(f"moe{m}_{name}")

                def turn(g):
                    for j in range(GB):
                        pe.wait_ge(sm("y"), g * GB + j + 1)
                        ins = pe.transpose(ps[:, 0, j * P:(j + 1) * P], y[:, j, :], ident[:, :])
                    ins.then_inc(sm("T"), 1)

                def logits(g):
                    pe.wait_ge(sm("yf"), g + 1)
                    for j in range(GB):
                        ins = pe.matmul(ps[:, 1, j * E:(j + 1) * E], yTf[:, j * P:(j + 1) * P], routerT[:, :],
                                        start=True, stop=True)
                    ins.then_inc(sm("lg"), 1)

                def turn_weights(g):
                    pe.wait_ge(sm("comb"), g + 1)
                    for j in range(GB):
                        ins = pe.transpose(ps[0:2 * E, 1, j * P:(j + 1) * P], comb2[:, j, :].bitcast(F32), ident[:, :])
                    ins.then_inc(sm("cT"), 1)

                def up(g, e, p):
                    if e == 0:
                        pe.wait_ge(sm("yl"), g + 1)
                    if m == 0:
                        pe.wait_ge(s("split"), 2 * e + 1)
                    for c in range(HC):
                        pe.wait_ge(sm("hid"), g * E * HC + e * HC + c + 1)
                        cols = slice(c * P, (c + 1) * P)
                        pe.matmul(ps[:, 2 + c, :], wfh[:, e, cols], yTh[:, p, :], start=True, stop=False)
                        pe.matmul(ps[:, 2 + c, :], wfh[:, e, cols], yTl[:, p, :], start=False, stop=False)
                        pe.matmul(ps[:, 2 + c, :], wfl[:, e, cols], yTh[:, p, :], start=False, stop=True)\
                            .then_inc(sm("fc"), 1)

                def weight(g, e):
                    if e == 0:
                        pe.wait_ge(sm("cTs"), g + 1)
                    pe.wait_ge(sm("wb"), g * E + e)
                    pe.matmul(ps[:, 7, :], sel[0:2 * E, e, :], combT[0:2 * E, :], start=True, stop=True)\
                        .then_inc(sm("w"), 1)

                def down(g, e):
                    if m == 0:
                        pe.wait_ge(s("split"), 2 * e + 2)
                    pe.wait_ge(sm("mul"), g * E + e)
                    for c in range(HC):
                        pe.wait_ge(sm("lo"), g * E * HC + e * HC + c + 1 + HC)
                        k = e * HC + c
                        pe.matmul(ps[:, 6, :], wph[:, k, :], hidh[:, e % 2, c, :], start=(c == 0), stop=False)
                        pe.matmul(ps[:, 6, :], wph[:, k, :], hidl[:, e % 2, c, :], start=False, stop=False)
                        ins = pe.matmul(ps[:, 6, :], wpl[:, k, :], hidh[:, e % 2, c, :], start=False, stop=(c == HC - 1))
                    ins.then_inc(sm("pr"), 1)

                def bias(g, last):
                    if last:
                        pe.wait_ge(sm("x"), g)
                    else:
                        pe.wait_ge(sm("yf"), g + 2)
                    for j in range(GB):
                        pe.matmul(ps[:, 0, j * D:(j + 1) * D], combT[0:2 * E, j * P:(j + 1) * P].bitcast(F32),
                                  b_pr2[0:2 * E, :], start=(j == 0), stop=False, skip_group_check=True)

                def flush(g):
                    pe.wait_ge(sm("acc"), (g + 1) * (E - 1))
                    for j in range(GB):
                        ins = pe.matmul(ps[:, 0, j * D:(j + 1) * D], acc[:, j * P:(j + 1) * P], ident[:, :],
                                        start=False, stop=True, skip_group_check=True)
                    ins.then_inc(sm("flush"), 1)

                def group(g, p, first=False, last=False):
                    if first:
                        up(g, 0, p)
                    for e in range(E):
                        weight(g, e)
                        if e == E - 1:
                            bias(g, last)
                            if not last:
                                turn_weights(g + 1)
                                up(g + 1, 0, 1 - p)
                        else:
                            up(g, e + 1, p)
                        if e == 2 and not last:
                            if not first:
                                pe.wait_ge(sm("x"), g)
                            turn(g + 1)
                        if e == 3 and not last:
                            logits(g + 1)
                        down(g, e)
                        if e == 0 and not first:
                            flush(g - 1)
                    if last:
                        flush(g)

                turn(0)
                logits(0)
                turn_weights(0)
                group(0, 0, first=True)
                with pe.Fori(0, (NG - 2) // 2) as i:
                    group(2 * i + 1, 1)
                    group(2 * i + 2, 0)
                group(NG - 1, 1, last=True)

            if phases >= 2:
                moe_tensor(0)
            def linrec_tensor():
                def front(b):
                    for half in range(GPB):
                        if not (type(b) is int and b < 2):
                            pe.wait_ge(s("l_x"), (b - 1) * GPB + half + 1)
                        for j in range(GB):
                            pe.wait_ge(s("l_y"), b * BPB + half * GB + j + 1)
                            ins = pe.transpose(ps[:, half, j * P:(j + 1) * P], y[:, half * GB + j, :], ident[:, :])
                        ins.then_inc(s("l_T"), 1)
                    for half in range(GPB):
                        pe.wait_ge(s("l_yT"), b * GPB + half + 1)
                        if not (type(b) is int and b == 0):
                            pe.wait_ge(s("l_kv"), (b - 1) * GPB + half + 1)
                        for t in (1, 0, 2):
                            ins = pe.matmul(ps[:, 2 + 3 * half + t, :], w_rkv[:, t * D:(t + 1) * D],
                                            l_yT[:, half * GT:(half + 1) * GT], start=True, stop=True)
                        ins.then_inc(s("l_rkv"), 1)

                def project(b, ahead):
                    pe.wait_ge(s("l_xT"), b + 2)
                    for half in range(GPB):
                        if ahead:
                            pe.wait_ge(s("l_yT"), (b + 1) * GPB + half + 1)
                        for j in range(GB):
                            n = half * GB + j
                            cols = slice(j * D, (j + 1) * D)
                            pe.matmul(ps[:, half, cols], ones_row[0:1, :], bo_row[0:1, :], start=True, stop=False)
                            ins = pe.matmul(ps[:, half, cols], l_x[:, n * P:(n + 1) * P], w_o[:, :], start=False, stop=True)
                        ins.then_inc(s("l_out"), 1)

                pe.sem_inc(s("l_x"), GPB)
                front(0)
                with pe.Fori(0, B - 1) as b:
                    front(b + 1)
                    project(b, True)
                project(B - 1, False)

            if phases >= 3:
                linrec_tensor()
            if phases >= 4:
                moe_tensor(1)


_NAMES = {
    "hidden": "L0_attn_a_hidden_states", "conv_w": "L0_attn_a_conv_w", "Wq": "L0_attn_a_Wq",
    "Wk": "L0_attn_a_Wk", "Wv": "L0_attn_a_Wv", "Wb": "L0_attn_a_Wb", "Wg": "L0_attn_a_Wg",
    "norm_w": "L0_attn_a_norm_w", "Wo": "L0_attn_a_Wo", "W_rkv": "L0_attn_b_W_rkv",
    "b_rkv": "L0_attn_b_b_rkv", "W_o": "L0_attn_b_W_o", "b_o": "L0_attn_b_b_o",
    "nu_log": "L0_attn_b_nu_log", "gamma_log": "L0_attn_b_gamma_log", "router_w": "L0_ffn_router_w",
    "w_fc": "L0_ffn_w_fc", "b_fc": "L0_ffn_b_fc", "w_proj": "L0_ffn_w_proj", "b_proj": "L0_ffn_b_proj",
}
PHASES = 4


def kernel(**inputs):
    import numpy as np
    import concourse.bacc as bacc
    from concourse.bass_utils import run_bass_kernel_spmd

    nc = bacc.Bacc("TRN2", target_bir_lowering=False, num_devices=1)
    arrays, aps = {}, {}
    for short, name in _NAMES.items():
        a = np.ascontiguousarray(inputs[name])
        arrays[f"in_{short}"] = a
        aps[short] = nc.dram_tensor(f"in_{short}", a.shape, F32, kind="ExternalInput").ap()
    out = nc.dram_tensor("out_x", inputs[_NAMES["hidden"]].shape, F32, kind="ExternalOutput").ap()
    hybrid_kernel(nc, aps, out, PHASES)
    r = run_bass_kernel_spmd(nc, [arrays], core_ids=[0])
    return r.results[0]["out_x"]
```
